# Optimizing a Trainium2 kernel written in Bass

```python
import numpy as np
import jax
import jax.numpy as jnp

def _softmax(x, axis=-1):
    return jax.nn.softmax(x, axis=axis)

def _gelu(x):
    return jax.nn.gelu(x, approximate=True)

def _silu(x):
    return jax.nn.silu(x)

def _sigmoid(x):
    return jax.nn.sigmoid(x)

def _layernorm(x, axis=-1, eps=1e-05):
    m = jnp.mean(x, axis=axis, keepdims=True)
    v = jnp.var(x, axis=axis, keepdims=True)
    return (x - m) / jnp.sqrt(v + eps)

def _scatter_add(tgt, idx, src, axis=0):
    return tgt.at[idx].add(src)

def _segment_sum(src, seg, n):
    return jax.ops.segment_sum(src, seg, n)
kernel_name = 'mk_seq_postln_d1_jaxref_r8_00a292'

def setup_inputs(seed: int=0):
    np.random.seed(seed)
    _w = jnp.asarray

    def _L0_attn_setup():
        import jax, jax.numpy as jnp
        import numpy as np
        D_MODEL = 128
        K_HEADS = 32
        ANCHOR = 4
        M_THETA = 4
        CONV_K = 4
        H_DIM = D_MODEL // K_HEADS
        TOTAL = 2 * D_MODEL + K_HEADS
        key = jax.random.key(seed)
        ks = jax.random.split(key, 12)
        B, L = (4, 256)
        x = jax.random.normal(ks[0], (B, L, D_MODEL), dtype=jnp.float32)
        W_in = jax.random.normal(ks[1], (D_MODEL, TOTAL), dtype=jnp.float32) / np.sqrt(D_MODEL)
        w_conv = jax.random.normal(ks[2], (CONV_K, 1, TOTAL), dtype=jnp.float32) / np.sqrt(CONV_K)
        b_conv = jnp.zeros((TOTAL,), dtype=jnp.float32)
        grid = np.linspace(-np.pi / 3, np.pi / 3, M_THETA, dtype=np.float32)
        theta = jnp.asarray(np.tile(grid.reshape(1, 1, 1, 1, M_THETA), (1, 1, K_HEADS, H_DIM, 1)))
        dec_rates = np.geomspace(0.001, 0.1, K_HEADS - ANCHOR).astype(np.float32)
        decay_slopes = jnp.asarray(np.log(np.exp(dec_rates) - 1))
        anc_rates = np.geomspace(0.01, 0.1, ANCHOR).astype(np.float32)
        anchor_slopes = jnp.asarray(np.log(np.exp(anc_rates) - 1))
        score_scale = jnp.ones((K_HEADS,), dtype=jnp.float32)
        deriv_logits = jnp.asarray([5.0, 0.0, 0.0], dtype=jnp.float32)
        norm_scale = jnp.ones((2 * H_DIM * M_THETA,), dtype=jnp.float32)
        lim = np.sqrt(6.0 / (H_DIM * M_THETA + H_DIM))
        W_re = jax.random.uniform(ks[3], (H_DIM * M_THETA, H_DIM), jnp.float32, -lim, lim)
        W_im = jax.random.uniform(ks[4], (H_DIM * M_THETA, H_DIM), jnp.float32, -lim, lim)
        W_out = jax.random.normal(ks[5], (D_MODEL, D_MODEL), dtype=jnp.float32) / np.sqrt(D_MODEL)
        return {'x': x, 'W_in': W_in, 'w_conv': w_conv, 'b_conv': b_conv, 'theta': theta, 'decay_slopes': decay_slopes, 'anchor_slopes': anchor_slopes, 'score_scale': score_scale, 'deriv_logits': deriv_logits, 'norm_scale': norm_scale, 'W_re': W_re, 'W_im': W_im, 'W_out': W_out}
    _L0_attn_in = _L0_attn_setup()

    def _L0_ffn_setup():
        import jax, jax.numpy as jnp
        import numpy as np
        DIM = 128
        DEPTH = 6
        HEADS = 16
        DIM_HEAD = 64
        WINDOW = 32
        INNER = HEADS * DIM_HEAD
        DIM_INNER = int(DIM * 4 * 2 / 3)
        QK_SCALE = 8.0

        def shift_tokens(t):
            a, s = jnp.split(t, 2, -1)
            s = jnp.pad(s, ((0, 0), (1, 0), (0, 0)))[:, :-1]
            return jnp.concatenate([a, s], -1)

        def l2norm(t):
            return t / jnp.maximum(jnp.linalg.norm(t, axis=-1, keepdims=True), 1e-12)

        def rotate_half(x):
            x1, x2 = jnp.split(x, 2, -1)
            return jnp.concatenate([-x2, x1], -1)

        def rotary_tables(n):
            half = jnp.arange(0, DIM_HEAD, 2, dtype=jnp.float32)
            inv_freq = 1.0 / 10000.0 ** (half / DIM_HEAD)
            t = jnp.arange(n, dtype=jnp.float32)
            freqs = t[:, None] * inv_freq[None, :]
            freqs = jnp.concatenate([freqs, freqs], -1)
            base_scale = (half + 0.4 * DIM_HEAD) / (1.4 * DIM_HEAD)
            power = (t - n // 2) / (WINDOW // 2)
            scale = base_scale[None, :] ** power[:, None]
            scale = jnp.concatenate([scale, scale], -1)
            return (freqs, scale)

        def local_attention(q, k, v):
            b, h, n, d = q.shape
            w = WINDOW
            nw = n // w
            bq = q.reshape(b, h, nw, w, d)
            bk = k.reshape(b, h, nw, w, d)
            bv = v.reshape(b, h, nw, w, d)

            def look(t):
                p = jnp.pad(t, ((0, 0), (0, 0), (1, 0), (0, 0), (0, 0)))
                return jnp.concatenate([p[:, :, :nw], p[:, :, 1:]], axis=3)
            bk2, bv2 = (look(bk), look(bv))
            seq = jnp.arange(n).reshape(nw, w)
            seq_p = jnp.pad(seq, ((1, 0), (0, 0)), constant_values=-1)
            jt = jnp.concatenate([seq_p[:nw], seq_p[1:]], axis=1)
            it = seq[:, :, None]
            jb = jt[:, None, :]
            mask = (it < jb) | (it > jb + w) | (jb == -1)
            sim = jnp.einsum('bhwie,bhwje->bhwij', bq, bk2) * QK_SCALE
            sim = jnp.where(mask, -jnp.finfo(sim.dtype).max, sim)
            attn = jax.nn.softmax(sim, -1)
            out = jnp.einsum('bhwij,bhwje->bhwie', attn, bv2)
            return out.reshape(b, h, n, d)

        def attn_layer(x, Wqkv, qs, ksc, Wo):
            b, n, _ = x.shape
            qkv = x @ Wqkv
            q, k, v = jnp.split(qkv, 3, -1)
            sh = lambda t: t.reshape(b, n, HEADS, DIM_HEAD).transpose(0, 2, 1, 3)
            q, k, v = (sh(q), sh(k), sh(v))
            q = l2norm(q) * qs
            k = l2norm(k) * ksc
            freqs, scale = rotary_tables(n)
            cos, sin = (jnp.cos(freqs), jnp.sin(freqs))
            q = q * cos * scale + rotate_half(q) * sin * scale
            inv = 1.0 / scale
            k = k * cos * inv + rotate_half(k) * sin * inv
            out = local_attention(q, k, v)
            out = out.transpose(0, 2, 1, 3).reshape(b, n, INNER)
            return out @ Wo

        def ffn_layer(x, g, bln, W1, b1, W2, b2):
            mu = x.mean(-1, keepdims=True)
            var = ((x - mu) ** 2).mean(-1, keepdims=True)
            xn = (x - mu) / jnp.sqrt(var + 1e-05) * g + bln
            hg = xn @ W1 + b1
            a, gate = jnp.split(hg, 2, -1)
            return a * jax.nn.gelu(gate, approximate=False) @ W2 + b2
        key = jax.random.key(seed)
        ks = jax.random.split(key, 8)
        B, N = (2, 256)
        init = lambda k, shape: jax.random.normal(k, shape, jnp.float32) * 0.02
        return {'x': jax.random.normal(ks[0], (B, N, DIM), jnp.float32), 'Wqkv': init(ks[1], (DEPTH, DIM, 3 * INNER)), 'q_scale': jnp.ones((DEPTH, DIM_HEAD), jnp.float32), 'k_scale': jnp.ones((DEPTH, DIM_HEAD), jnp.float32), 'Wo': init(ks[2], (DEPTH, INNER, DIM)), 'ln_g': jnp.ones((DEPTH, DIM), jnp.float32), 'ln_b': jnp.zeros((DEPTH, DIM), jnp.float32), 'W1': init(ks[3], (DEPTH, DIM, 2 * DIM_INNER)), 'b1': jnp.zeros((DEPTH, 2 * DIM_INNER), jnp.float32), 'W2': init(ks[4], (DEPTH, DIM_INNER, DIM)), 'b2': jnp.zeros((DEPTH, DIM), jnp.float32)}
    _L0_ffn_in = _L0_ffn_setup()
    _d = {'L0_attn_x': _L0_attn_in['x'], 'L0_attn_W_in': _L0_attn_in['W_in'], 'L0_attn_w_conv': _L0_attn_in['w_conv'], 'L0_attn_b_conv': _L0_attn_in['b_conv'], 'L0_attn_theta': _L0_attn_in['theta'], 'L0_attn_decay_slopes': _L0_attn_in['decay_slopes'], 'L0_attn_anchor_slopes': _L0_attn_in['anchor_slopes'], 'L0_attn_score_scale': _L0_attn_in['score_scale'], 'L0_attn_deriv_logits': _L0_attn_in['deriv_logits'], 'L0_attn_norm_scale': _L0_attn_in['norm_scale'], 'L0_attn_W_re': _L0_attn_in['W_re'], 'L0_attn_W_im': _L0_attn_in['W_im'], 'L0_attn_W_out': _L0_attn_in['W_out'], 'L0_ffn_Wqkv': _L0_ffn_in['Wqkv'], 'L0_ffn_q_scale': _L0_ffn_in['q_scale'], 'L0_ffn_k_scale': _L0_ffn_in['k_scale'], 'L0_ffn_Wo': _L0_ffn_in['Wo'], 'L0_ffn_ln_g': _L0_ffn_in['ln_g'], 'L0_ffn_ln_b': _L0_ffn_in['ln_b'], 'L0_ffn_W1': _L0_ffn_in['W1'], 'L0_ffn_b1': _L0_ffn_in['b1'], 'L0_ffn_W2': _L0_ffn_in['W2'], 'L0_ffn_b2': _L0_ffn_in['b2']}
    _x0 = _d['L0_attn_x']
    _d['L0_attn_x'] = jax.random.normal(jax.random.fold_in(jax.random.key(seed), 1), (8, 512, 128), dtype=_x0.dtype)
    del _x0
    return _d

def reference(L0_attn_x, L0_attn_W_in, L0_attn_w_conv, L0_attn_b_conv, L0_attn_theta, L0_attn_decay_slopes, L0_attn_anchor_slopes, L0_attn_score_scale, L0_attn_deriv_logits, L0_attn_norm_scale, L0_attn_W_re, L0_attn_W_im, L0_attn_W_out, L0_ffn_Wqkv, L0_ffn_q_scale, L0_ffn_k_scale, L0_ffn_Wo, L0_ffn_ln_g, L0_ffn_ln_b, L0_ffn_W1, L0_ffn_b1, L0_ffn_W2, L0_ffn_b2):

    def _L0_attn_ref(x, W_in, w_conv, b_conv, theta, decay_slopes, anchor_slopes, score_scale, deriv_logits, norm_scale, W_re, W_im, W_out):
        import jax, jax.numpy as jnp
        import numpy as np
        D_MODEL = 128
        K_HEADS = 32
        ANCHOR = 4
        M_THETA = 4
        CONV_K = 4
        H_DIM = D_MODEL // K_HEADS
        TOTAL = 2 * D_MODEL + K_HEADS
        B, L, D = x.shape
        K, H, M = (K_HEADS, H_DIM, M_THETA)
        z = x @ W_in
        z = jax.lax.conv_general_dilated(z, w_conv, window_strides=(1,), padding=[(CONV_K - 1, 0)], feature_group_count=z.shape[-1], dimension_numbers=('NWC', 'WIO', 'NWC')) + b_conv
        x_val = z[..., :D].reshape(B, L, K, H)
        x_gate = jax.nn.silu(z[..., D:2 * D])
        s_raw = z[..., 2 * D:].reshape(B, L, K, 1)
        pos = jnp.arange(L, dtype=jnp.float32)
        sd = jax.nn.softplus(decay_slopes)
        dist = jnp.maximum(L - 1 - pos, 0.0)
        w_dec = jnp.exp(-sd[None, :] * dist[:, None])
        sa = jax.nn.softplus(anchor_slopes)
        w_anc = jnp.exp(-sa[None, :] * pos[:, None])
        time_w = jnp.concatenate([w_dec, w_anc], axis=1)[None, :, :, None]
        p = jnp.exp(jnp.clip(score_scale[None, None, :, None] * s_raw, -20.0, 20.0))
        x5 = x_val[..., None]
        phi = x5 * theta
        cos_b, sin_b = (jnp.cos(phi), jnp.sin(phi))
        w = jax.nn.softmax(deriv_logits)
        poly = w[0] + w[1] * x5 - w[2] * jnp.square(x5)
        re_m = poly * cos_b
        im_m = poly * sin_b
        p_w = (p * time_w)[..., None]
        flat = (B, L, K * H * M)
        merged = jnp.concatenate([(p_w * re_m).reshape(flat), (p_w * im_m).reshape(flat), jnp.broadcast_to(p_w, (B, L, K, H, M)).reshape(flat)], axis=-1)
        cs = jnp.cumsum(merged, axis=1)
        num_re, num_im, den = jnp.split(cs, 3, axis=-1)
        inv_den = 1.0 / jnp.maximum(den, 0.0001)
        re = (num_re * inv_den).reshape(B, L, K, H * M)
        im = (num_im * inv_den).reshape(B, L, K, H * M)
        mean_sq = (jnp.sum(jnp.square(re), -1) + jnp.sum(jnp.square(im), -1)) / (2.0 * H * M)
        rsq = jax.lax.rsqrt(mean_sq[..., None] + 1e-05)
        re_n = re * rsq * norm_scale[:H * M]
        im_n = im * rsq * norm_scale[H * M:]
        y = re_n @ W_re + im_n @ W_im
        y = y.reshape(B, L, D)
        return y * x_gate @ W_out

    def _L0_ffn_ref(x, Wqkv, q_scale, k_scale, Wo, ln_g, ln_b, W1, b1, W2, b2):
        import jax, jax.numpy as jnp
        import numpy as np
        DIM = 128
        DEPTH = 6
        HEADS = 16
        DIM_HEAD = 64
        WINDOW = 32
        INNER = HEADS * DIM_HEAD
        DIM_INNER = int(DIM * 4 * 2 / 3)
        QK_SCALE = 8.0

        def shift_tokens(t):
            a, s = jnp.split(t, 2, -1)
            s = jnp.pad(s, ((0, 0), (1, 0), (0, 0)))[:, :-1]
            return jnp.concatenate([a, s], -1)

        def l2norm(t):
            return t / jnp.maximum(jnp.linalg.norm(t, axis=-1, keepdims=True), 1e-12)

        def rotate_half(x):
            x1, x2 = jnp.split(x, 2, -1)
            return jnp.concatenate([-x2, x1], -1)

        def rotary_tables(n):
            half = jnp.arange(0, DIM_HEAD, 2, dtype=jnp.float32)
            inv_freq = 1.0 / 10000.0 ** (half / DIM_HEAD)
            t = jnp.arange(n, dtype=jnp.float32)
            freqs = t[:, None] * inv_freq[None, :]
            freqs = jnp.concatenate([freqs, freqs], -1)
            base_scale = (half + 0.4 * DIM_HEAD) / (1.4 * DIM_HEAD)
            power = (t - n // 2) / (WINDOW // 2)
            scale = base_scale[None, :] ** power[:, None]
            scale = jnp.concatenate([scale, scale], -1)
            return (freqs, scale)

        def local_attention(q, k, v):
            b, h, n, d = q.shape
            w = WINDOW
            nw = n // w
            bq = q.reshape(b, h, nw, w, d)
            bk = k.reshape(b, h, nw, w, d)
            bv = v.reshape(b, h, nw, w, d)

            def look(t):
                p = jnp.pad(t, ((0, 0), (0, 0), (1, 0), (0, 0), (0, 0)))
                return jnp.concatenate([p[:, :, :nw], p[:, :, 1:]], axis=3)
            bk2, bv2 = (look(bk), look(bv))
            seq = jnp.arange(n).reshape(nw, w)
            seq_p = jnp.pad(seq, ((1, 0), (0, 0)), constant_values=-1)
            jt = jnp.concatenate([seq_p[:nw], seq_p[1:]], axis=1)
            it = seq[:, :, None]
            jb = jt[:, None, :]
            mask = (it < jb) | (it > jb + w) | (jb == -1)
            sim = jnp.einsum('bhwie,bhwje->bhwij', bq, bk2) * QK_SCALE
            sim = jnp.where(mask, -jnp.finfo(sim.dtype).max, sim)
            attn = jax.nn.softmax(sim, -1)
            out = jnp.einsum('bhwij,bhwje->bhwie', attn, bv2)
            return out.reshape(b, h, n, d)

        def attn_layer(x, Wqkv, qs, ksc, Wo):
            b, n, _ = x.shape
            qkv = x @ Wqkv
            q, k, v = jnp.split(qkv, 3, -1)
            sh = lambda t: t.reshape(b, n, HEADS, DIM_HEAD).transpose(0, 2, 1, 3)
            q, k, v = (sh(q), sh(k), sh(v))
            q = l2norm(q) * qs
            k = l2norm(k) * ksc
            freqs, scale = rotary_tables(n)
            cos, sin = (jnp.cos(freqs), jnp.sin(freqs))
            q = q * cos * scale + rotate_half(q) * sin * scale
            inv = 1.0 / scale
            k = k * cos * inv + rotate_half(k) * sin * inv
            out = local_attention(q, k, v)
            out = out.transpose(0, 2, 1, 3).reshape(b, n, INNER)
            return out @ Wo

        def ffn_layer(x, g, bln, W1, b1, W2, b2):
            mu = x.mean(-1, keepdims=True)
            var = ((x - mu) ** 2).mean(-1, keepdims=True)
            xn = (x - mu) / jnp.sqrt(var + 1e-05) * g + bln
            hg = xn @ W1 + b1
            a, gate = jnp.split(hg, 2, -1)
            return a * jax.nn.gelu(gate, approximate=False) @ W2 + b2
        for i in range(DEPTH):
            x = attn_layer(shift_tokens(x), Wqkv[i], q_scale[i], k_scale[i], Wo[i]) + x
            x = ffn_layer(shift_tokens(x), ln_g[i], ln_b[i], W1[i], b1[i], W2[i], b2[i]) + x
        return x
    x = L0_attn_x
    x = _layernorm(x + _L0_attn_ref(x, L0_attn_W_in, L0_attn_w_conv, L0_attn_b_conv, L0_attn_theta, L0_attn_decay_slopes, L0_attn_anchor_slopes, L0_attn_score_scale, L0_attn_deriv_logits, L0_attn_norm_scale, L0_attn_W_re, L0_attn_W_im, L0_attn_W_out), axis=-1)
    x = _layernorm(x + _L0_ffn_ref(x, L0_ffn_Wqkv, L0_ffn_q_scale, L0_ffn_k_scale, L0_ffn_Wo, L0_ffn_ln_g, L0_ffn_ln_b, L0_ffn_W1, L0_ffn_b1, L0_ffn_W2, L0_ffn_b2), axis=-1)
    return x

_drawn_inputs = setup_inputs


def setup_inputs(seed=0):
    import zlib

    import numpy as np

    out = dict(_drawn_inputs(seed))
    spreads = {'L0_attn_b_conv': (0.0, 0.1),
     'L0_attn_score_scale': (1.0, 0.6),
     'L0_attn_norm_scale': (1.0, 0.2),
     'L0_ffn_q_scale': (1.0, 0.6),
     'L0_ffn_k_scale': (1.0, 0.6),
     'L0_ffn_ln_g': (1.0, 0.6),
     'L0_ffn_ln_b': (0.0, 0.8),
     'L0_ffn_b1': (0.0, 0.8),
     'L0_ffn_b2': (0.0, 0.1)}
    factors = {'L0_attn_anchor_slopes': 31.208, 'L0_ffn_W1': 3.657, 'L0_ffn_W2': 3.586}
    for name, (base, spread) in spreads.items():
        noise = np.random.default_rng([zlib.crc32(name.encode()), seed]).standard_normal(out[name].shape)
        drawn = base * np.exp(spread * noise) if base else spread * noise
        out[name] = jnp.asarray(drawn.astype(out[name].dtype))
    for name, factor in factors.items():
        out[name] = (out[name] * factor).astype(out[name].dtype)
    return out
```

```python
from contextlib import ExitStack

import numpy as np

import concourse.bass as bass
from concourse import mybir

F32 = mybir.dt.float32
BF16 = mybir.dt.bfloat16
I32 = mybir.dt.int32
ALU = mybir.AluOpType
ACT = mybir.ActivationFunctionType
AX = mybir.AxisListType

P = 128
B, L, D = 8, 512, 128
TILES = L // P
K, H, M = 32, 4, 4
TAPS = 4
TOTAL = 2 * D + K
LN_EPS = 1e-5
MAGIC = 12582912.0
TWO_PI = 6.283185
TURN = 1.0 / 6.283185307179586
DEPTH, HEADS, DH, WIN = 6, 16, 64, 32
DEPTH_RUN = DEPTH
INNER = HEADS * DH
PAIRS = HEADS // 2
HID = int(D * 4 * 2 / 3)
CHUNKS = [(c, min(P, HID - c)) for c in range(0, HID, P)]
PAD = WIN + 1
SPAN = PAD + L
MASKED = -1e30
ONE = 1


def constants():
    f = np.float32
    ident = np.eye(P, dtype=f)
    i = np.arange(P)
    late = (np.arange(L)[None, :] >= i[:, None]).astype(f)
    block = (np.arange(K)[None, None, :] == 8 * np.arange(4)[None, :, None] + (i // 16)[:, None, None]).astype(f)
    spread = (np.arange(P)[None, :] // H == np.arange(K)[:, None]).astype(f)
    rep16 = (np.arange(P)[None, :] % 16 == np.arange(16)[:, None]).astype(f)
    pos = np.arange(L, dtype=f)
    dist = np.concatenate([np.tile(f(L - 1) - pos, (K - 4, 1)), np.tile(pos, (4, 1))], 0).astype(f)
    half = np.arange(0, DH, 2, dtype=f)
    inv = f(1.0) / f(10000.0) ** (half / f(DH))
    fr = (pos[:, None] * inv[None, :]).astype(f)
    fr = np.concatenate([fr, fr], -1)
    base = ((half + f(0.4 * DH)) / f(1.4 * DH)).astype(f)
    power = (pos - L // 2) / f(WIN // 2)
    sc = base[None, :] ** power[:, None]
    sc = np.concatenate([sc, sc], -1).astype(f)
    sign = np.where(np.arange(DH) < DH // 2, -1, 1).astype(f)
    cos, sin = np.cos(fr), np.sin(fr) * sign
    q = np.stack([cos * sc * 8, sin * sc * 8], 1)
    k = np.stack([cos / sc, sin / sc], 1)
    rope = np.stack([q, k], 1).reshape(TILES, P, 2, 2, DH).transpose(1, 0, 2, 3, 4)
    a, b = (i % WIN)[:, None], np.arange(2 * WIN)[None, :]
    off = (b < a) | (b > a + WIN)
    first = off | ((i < WIN)[:, None] & (b < WIN))
    mask = np.stack([np.tile(np.where(m, MASKED, 0.0), (1, 8)) for m in (first, off)], 1)
    out = dict(ident=ident, late=late, block=block.reshape(P, 4 * K), spread=spread, rep16=rep16,
               dist=dist, rope=rope.reshape(P, -1), mask=mask.reshape(P, -1))
    return {n: np.ascontiguousarray(x, f) for n, x in out.items()}


class Steps:

    def __init__(self, sem, names):
        self.sem, self.names, self.at = sem, names, 0

    def did(self, instruction, name):
        assert self.names[self.at] == name, (self.names[self.at], name)
        self.at = (self.at + 1) % len(self.names)
        instruction.then_inc(self.sem, 1)

    def count(self, rounds, name):
        return rounds * len(self.names) + self.names.index(name) + 1 + ONE


class Event:

    def __init__(self, sem, per=1):
        self.sem, self.per = sem, per

    def value(self, rounds, part=None):
        return rounds * self.per + (self.per if part is None else part + 1) + 2 * self.per


def rsqrt(dve, tick, x, y, h):
    yi = y.bitcast(I32)
    tick(dve.tensor_scalar(yi, x.bitcast(I32), 1, None, ALU.logical_shift_right))
    tick(dve.tensor_scalar(yi, yi, -1.0, float(0x5F3759DF), ALU.mult, ALU.add))
    for _ in range(3):
        tick(dve.scalar_tensor_tensor(out=h, in0=y, scalar=-0.5, in1=y, op0=ALU.mult, op1=ALU.mult))
        tick(dve.tensor_tensor(h, h, x, ALU.mult))
        tick(dve.scalar_tensor_tensor(out=y, in0=h, scalar=1.5, in1=y, op0=ALU.add, op1=ALU.mult))


ABS_BITS = 0x7FFFFFFF
RSQRT = 11


def state_space_layer(nc, a, XT, X1T, ident):
    with ExitStack() as ctx:
        def sb(name, shape, dt=F32):
            return ctx.enter_context(nc.sbuf_tensor("a_" + name, shape, dt))

        def sem(name):
            return ctx.enter_context(nc.semaphore("a_" + name))

        bank = [ctx.enter_context(nc.psum_tensor(f"a_bank{i}", [P, 512], F32)) for i in range(8)]
        xin, xtok = sb("xin", [P, B, L]), sb("xtok", [P, B, TILES, D])
        w_in, w_out = sb("w_in", [P, TOTAL]), sb("w_out", [P, D])
        taps, bias = sb("taps", [P, 3, TAPS]), sb("bias", [P, 3])
        theta, logit = sb("theta", [P, P, M]), sb("logit", [P, 3])
        top, weights, total = sb("top", [P, 1]), sb("weights", [P, 3]), sb("total", [P, 1])
        slope, sscale = sb("slope", [K, 1]), sb("sscale", [K, 1])
        soft = sb("soft", [K, 10])
        w16, nscale, wrep = sb("w16", [16, 8]), sb("nscale", [16, 2]), sb("wrep", [P, 8])
        late, block = sb("late", [P, L]), sb("block", [P, 4 * K])
        spread, rep16 = sb("spread", [K, P]), sb("rep16", [16, P])
        time_w = sb("time_w", [K, L])
        w_blk, sum_blk = sb("w_blk", [P, 8, P]), sb("sum_blk", [P, 4, P])
        magic, quarter, eps = sb("magic", [P, 1]), sb("quarter", [P, 1]), sb("eps", [P, 1])
        ones = sb("ones", [P, L])
        z, conv, gate = sb("z", [P, 3, TAPS - 1 + L]), sb("conv", [P, 3, L]), sb("gate", [P, L])
        pw, poly, den = sb("pw", [K, L]), sb("poly", [P, L]), sb("den", [P, L])
        g_tok = sb("g_tok", [P, TILES, P])
        whole, turn, turn_abs = (sb(n, [P, 2, 512]) for n in ("whole", "turn", "turn_abs"))
        sin, cos = sb("sin", [P, 2, 512]), sb("cos", [P, 2, 512])
        moments = sb("moments", [P, TILES, 2 * 512])
        num, sq = sb("num", [P, 2, L]), sb("sq", [P, 2, L])
        ms, yg = sb("ms", [P, L]), sb("yg", [P, L])
        res, res_n = sb("res", [P, TILES, D]), sb("res_n", [P, TILES, D])
        stats, mv, dev = sb("stats", [P, TILES, 6]), sb("mv", [P, TILES, 2]), sb("dev", [P, TILES])
        pause = sb("pause", [P, 1])

        loaded = sem("loaded")
        vector_ready, scalar_ready, spread_ready = sem("vector_ready"), sem("scalar_ready"), sem("spread_ready")
        setup_done, vector_own = sem("setup_done"), sem("vector_own")
        pe_s = Steps(sem("tensor_step"), ["z2", "z0", "z1", "spread", "g turned"]
                     + [f"phase{t}" for t in range(TILES)]
                     + ["cumulated0"] + [f"{n}" for c in range(1, 8) for n in (f"cumulated{c}", f"contracted{c - 1}")]
                     + ["contracted7", "out", "turned"])
        act_s = Steps(sem("scalar_step"), ["z2", "z0", "z1", "p", "silu", "g turned"]
                      + [f"{n}{t}" for t in range(TILES) for n in ("magic", "sin", "cos")]
                      + [f"square{c}" for c in range(8)] + ["rms", "deviation", "stored", "kept"])
        dve_s = Steps(sem("vector_step"), [f"conv2{j}" for j in range(TAPS)] + ["clip low", "clip"]
                      + [f"conv{c}{j}" for c in (0, 1) for j in range(TAPS)]
                      + ["weight", "poly1", "poly2", "g", "den"]
                      + [f"{n}{t}" for t in range(TILES) for n in ("turn", "turn_abs", "re", "im")]
                      + [f"num{c}" for c in range(8)]
                      + ["den floor", "inv den", "ms1", "ms2", "ms3", "inv rms", "factor", "y", "yg",
                         "residual"] + [f"stats{t}" for t in range(TILES)]
                      + [f"mean{t}" for t in range(TILES)] + ["inv dev"] + [f"norm{t}" for t in range(TILES)])
        col = lambda x: x.rearrange("(p o) -> p o", o=1)
        loads = [(xin[:, :, :], a["xT"]), (w_in[:, :], a["W_in"]), (w_out[:, :], a["W_out"]),
                 (taps[:, 0:2, :], a["w_conv"][0:2 * P, :].rearrange("(c p) j -> p c j", p=P)),
                 (taps[0:K, 2, :], a["w_conv"][2 * P:TOTAL, :]),
                 (bias[:, 0:1], col(a["b_conv"][0:P])), (bias[:, 1:2], col(a["b_conv"][P:2 * P])),
                 (bias[0:K, 2:3], col(a["b_conv"][2 * P:TOTAL])),
                 (theta[:, :, :], a["theta"].rearrange("p (c m) -> p c m", m=M)), (logit[:, :], a["logits"]),
                 (slope[:, :], col(a["slopes"])), (sscale[:, :], col(a["score_scale"])),
                 (w16[:, 0:4], a["W_re"]), (w16[:, 4:8], a["W_im"]),
                 (nscale[:, 0:1], col(a["norm_scale"][0:16])), (nscale[:, 1:2], col(a["norm_scale"][16:32])),
                 (late[:, :], a["late"]), (block[:, :], a["block"]), (spread[:, :], a["spread"]),
                 (rep16[:, :], a["rep16"]), (time_w[:, :], a["dist"]), (ident[:, :], a["ident"])]
        loads += [(xtok[:, s, :, :], a["x"][s].rearrange("(t p) d -> p t d", p=P)) for s in range(B)]

        blk = ctx.enter_context(nc.Block())

        @blk.sync
        def _(sp):
            for dst, src in loads:
                sp.dma_start(dst, src).then_inc(loaded, 16)

        @blk.vector
        def _(dve):
            dve.sem_inc(dve_s.sem, ONE)
            own = [0]

            def tick(instruction):
                own[0] += 1
                instruction.then_inc(vector_own, 1)
                dve.wait_ge(vector_own, own[0])

            for buf, v in ((ones, 1.0), (magic, MAGIC), (quarter, 1.5707963267948966), (eps, LN_EPS)):
                dve.memset(buf[:, :], v)
            dve.memset(z[:, :, 0:TAPS - 1], 0.0)
            tick(dve.memset(XT[:, :, 0:PAD], 0.0))
            dve.wait_ge(loaded, 16 * len(loads))
            tick(dve.tensor_reduce(top[:, :], logit[:, :], AX.X, ALU.max))
            dve.tensor_scalar(logit[:, :], logit[:, :], top[:, 0:1], None, ALU.subtract).then_inc(vector_ready, 1)
            dve.tensor_scalar(soft[:, 0:1].bitcast(I32), slope[:, :].bitcast(I32), ABS_BITS, None, ALU.bitwise_and).then_inc(vector_ready, 1)
            dve.wait_ge(scalar_ready, 2)
            tick(dve.tensor_reduce(total[:, :], logit[:, :], AX.X, ALU.add))
            tick(dve.reciprocal(total[:, :], total[:, :]))
            tick(dve.tensor_scalar(weights[:, :], logit[:, :], total[:, 0:1], None, ALU.mult))
            dve.tensor_scalar(soft[:, 2:3], soft[:, 1:2], 1.0, None, ALU.add).then_inc(vector_ready, 1)
            dve.wait_ge(vector_ready, 3)
            tick(dve.tensor_scalar(soft[:, 3:4], soft[:, 2:3], 1.0, None, ALU.subtract))
            tick(dve.tensor_tensor(soft[:, 4:5], soft[:, 1:2], soft[:, 3:4], ALU.subtract))
            tick(dve.reciprocal(soft[:, 5:6], soft[:, 2:3]))
            dve.wait_ge(scalar_ready, 3)
            tick(dve.scalar_tensor_tensor(out=soft[:, 7:8], in0=soft[:, 4:5], scalar=soft[:, 5:6],
                                          in1=soft[:, 6:7], op0=ALU.mult, op1=ALU.add))
            tick(dve.scalar_tensor_tensor(out=soft[:, 8:9], in0=slope[:, :], scalar=0.0,
                                          in1=soft[:, 7:8], op0=ALU.max, op1=ALU.add))
            dve.tensor_scalar(time_w[:, :], time_w[:, :], soft[:, 8:9], None, ALU.mult).then_inc(vector_ready, 1)
            dve.tensor_scalar(w16[:, 0:4], w16[:, 0:4], nscale[:, 0:1], None, ALU.mult)
            dve.tensor_scalar(w16[:, 4:8], w16[:, 4:8], nscale[:, 1:2], None, ALU.mult).then_inc(vector_ready, 1)
            tick(dve.scalar_tensor_tensor(out=theta[:, :, :], in0=theta[:, :, :], scalar=TURN,
                                          in1=ident[:, :].unsqueeze(2).to_broadcast([P, P, M]),
                                          op0=ALU.mult, op1=ALU.mult))
            blocks = block[:, :].unsqueeze(2).to_broadcast([P, 4 * K, H])
            tick(dve.tensor_copy(sum_blk[:, :, :].rearrange("p c (k h) -> p (c k) h", h=H), blocks))
            dve.wait_ge(spread_ready, 1)
            tick(dve.tensor_copy(wrep[:, :], bank[0][:, 0:8]))
            for i in range(2):
                tick(dve.tensor_tensor(w_blk[:, 4 * i:4 * i + 4, :].rearrange("p c (k h) -> p (c k) h", h=H), blocks,
                                       wrep[:, 4 * i:4 * i + 4].unsqueeze(1).to_broadcast([P, 4 * K, H]), ALU.mult))
            tick(dve.tensor_scalar(top[:, :], weights[:, 2:3], -1.0, None, ALU.mult))
            dve.sem_inc(setup_done, 1)

            with dve.Fori(0, B) as s:
                def after(steps, name):
                    dve.wait_ge(steps.sem, steps.count(s, name))

                def step(instruction, name, wait=True):
                    dve_s.did(instruction, name)
                    if wait:
                        after(dve_s, name)

                for c in (2, 0, 1):
                    w = K if c == 2 else P
                    after(act_s, f"z{c}")
                    step(dve.tensor_scalar(conv[0:w, c, :], z[0:w, c, 0:L], taps[0:w, c, 0:1], bias[0:w, c:c + 1],
                                           ALU.mult, ALU.add), f"conv{c}0")
                    for j in range(1, TAPS):
                        step(dve.scalar_tensor_tensor(out=conv[0:w, c, :], in0=z[0:w, c, j:j + L],
                                                      scalar=taps[0:w, c, j:j + 1], in1=conv[0:w, c, :],
                                                      op0=ALU.mult, op1=ALU.add), f"conv{c}{j}")
                    if c == 2:
                        step(dve.tensor_scalar(conv[0:K, 2, :], conv[0:K, 2, :], sscale[:, 0:1], -20.0,
                                               ALU.mult, ALU.max), "clip low")
                        step(dve.tensor_scalar(conv[0:K, 2, :], conv[0:K, 2, :], 20.0, None, ALU.min), "clip", False)
                after(act_s, "p")
                step(dve.tensor_tensor(pw[:, :], conv[0:K, 2, :], time_w[:, :], ALU.mult), "weight", False)
                step(dve.tensor_scalar(poly[:, :], conv[:, 0, :], top[:, 0:1], weights[:, 1:2], ALU.mult, ALU.add), "poly1")
                step(dve.tensor_tensor(poly[:, :], poly[:, :], conv[:, 0, :], ALU.mult), "poly2")
                after(pe_s, "spread")
                step(dve.scalar_tensor_tensor(out=poly[:, :], in0=poly[:, :], scalar=weights[:, 0:1], in1=bank[3][:, :],
                                              op0=ALU.add, op1=ALU.mult), "g", False)
                step(dve.tensor_tensor_scan(den[:, :], ones[:, :], bank[3][:, :], 0.0, ALU.mult, ALU.add), "den", False)
                for t in range(TILES):
                    i = t % 2
                    after(act_s, f"magic{t}")
                    step(dve.scalar_tensor_tensor(out=turn[:, i, :], in0=whole[:, i, :], scalar=MAGIC,
                                                  in1=bank[4 + i][:, :], op0=ALU.subtract, op1=ALU.subtract), f"turn{t}")
                    step(dve.tensor_scalar(turn_abs[:, i, :].bitcast(I32), turn[:, i, :].bitcast(I32), ABS_BITS, None,
                                           ALU.bitwise_and), f"turn_abs{t}", False)
                    amp = g_tok[:, t, :].unsqueeze(2).to_broadcast([P, P, M])
                    after(act_s, f"cos{t}")
                    for n, (part, trig) in enumerate((("re", cos), ("im", sin))):
                        step(dve.tensor_tensor(moments[:, t, 512 * n:512 * n + 512].rearrange("p (c m) -> p c m", m=M),
                                               trig[:, i, :].rearrange("p (c m) -> p c m", m=M), amp, ALU.mult),
                             f"{part}{t}", False)
                for c in range(8):
                    after(pe_s, f"cumulated{c}")
                    if c >= 2:
                        after(pe_s, f"contracted{c - 2}")
                    step(dve.tensor_copy(num[:, c % 2, :], bank[c % 2][:, :]), f"num{c}", False)
                step(dve.tensor_scalar(den[:, :], den[:, :], 1e-4, None, ALU.max), "den floor")
                step(dve.reciprocal(den[:, :], den[:, :]), "inv den")
                after(pe_s, "contracted7")
                step(dve.tensor_tensor(ms[:, :], bank[2][:, :], den[:, :], ALU.mult), "ms1")
                step(dve.tensor_tensor(ms[:, :], ms[:, :], den[:, :], ALU.mult), "ms2")
                step(dve.tensor_scalar(ms[:, :], ms[:, :], 1.0 / (2 * H * M), 1e-5, ALU.mult, ALU.add), "ms3", False)
                after(act_s, "rms")
                step(dve.reciprocal(ms[:, :], ms[:, :]), "inv rms")
                step(dve.tensor_tensor(ms[:, :], ms[:, :], den[:, :], ALU.mult), "factor")
                step(dve.tensor_tensor(yg[:, :], bank[7][:, :], ms[:, :], ALU.mult), "y")
                step(dve.tensor_tensor(yg[:, :], yg[:, :], gate[:, :], ALU.mult), "yg", False)
                after(pe_s, "out")
                step(dve.tensor_tensor(res[:, :, :].rearrange("p t d -> p (t d)"), bank[3][:, :],
                                       xtok[:, bass.ds(s, 1), :, :].rearrange("p o t d -> p (o t d)"), ALU.add), "residual")
                for t in range(TILES):
                    step(dve.bn_stats(stats[:, t, :], res[:, t, :]), f"stats{t}", t == TILES - 1)
                dve.memset(pause[:, :], 0.0)
                for t in range(TILES):
                    step(dve.bn_aggr(mv[:, t, :], stats[:, t, :]), f"mean{t}", False)
                after(act_s, "deviation")
                step(dve.reciprocal(dev[:, :], dev[:, :]), "inv dev")
                for t in range(TILES):
                    step(dve.tensor_scalar(res_n[:, t, :], res[:, t, :], mv[:, t, 0:1], dev[:, t:t + 1],
                                           ALU.subtract, ALU.mult), f"norm{t}", False)

        @blk.scalar
        def _(act):
            act.sem_inc(act_s.sem, ONE)
            act.wait_ge(vector_ready, 1)
            act.activation(logit[:, :], logit[:, :], ACT.Exp).then_inc(scalar_ready, 1)
            act.wait_ge(vector_ready, 2)
            act.activation(soft[:, 1:2], soft[:, 0:1], ACT.Exp, scale=-1.0).then_inc(scalar_ready, 1)
            act.wait_ge(vector_ready, 3)
            act.activation(soft[:, 6:7], soft[:, 2:3], ACT.Ln).then_inc(scalar_ready, 1)
            act.wait_ge(vector_ready, 4)
            act.activation(time_w[:, :], time_w[:, :], ACT.Exp, scale=-1.0).then_inc(scalar_ready, 1)
            act.wait_ge(setup_done, 1)

            with act.Fori(0, B) as s:
                def after(steps, name):
                    act.wait_ge(steps.sem, steps.count(s, name))

                for c in (2, 0, 1):
                    w = K if c == 2 else P
                    after(pe_s, f"z{c}")
                    act_s.did(act.activation(z[0:w, c, TAPS - 1:], bank[c][0:w, :], ACT.Identity), f"z{c}")
                after(dve_s, "clip")
                act_s.did(act.activation(conv[0:K, 2, :], conv[0:K, 2, :], ACT.Exp), "p")
                after(dve_s, f"conv1{TAPS - 1}")
                act_s.did(act.activation(gate[:, :], conv[:, 1, :], ACT.Silu), "silu")
                after(pe_s, "g turned")
                act_s.did(act.activation(g_tok[:, :, :].rearrange("p t c -> p (t c)"), bank[6][:, :], ACT.Identity), "g turned")
                for t in range(TILES):
                    i = t % 2
                    after(pe_s, f"phase{t}")
                    if t >= 2:
                        after(dve_s, f"turn{t - 2}")
                    act_s.did(act.activation(whole[:, i, :], bank[4 + i][:, :], ACT.Identity, bias=magic[:, 0:1]), f"magic{t}")
                    after(dve_s, f"turn_abs{t}")
                    if t >= 2:
                        after(dve_s, f"im{t - 2}")
                    act_s.did(act.activation(sin[:, i, :], turn[:, i, :], ACT.Sin, scale=-TWO_PI), f"sin{t}")
                    act_s.did(act.activation(cos[:, i, :], turn_abs[:, i, :], ACT.Sin, scale=-TWO_PI, bias=quarter[:, 0:1]), f"cos{t}")
                for c in range(8):
                    after(dve_s, f"num{c}")
                    if c >= 2:
                        after(pe_s, f"contracted{c - 2}")
                    act_s.did(act.activation(sq[:, c % 2, :], num[:, c % 2, :], ACT.Square), f"square{c}")
                after(dve_s, "ms3")
                act_s.did(act.activation(ms[:, :], ms[:, :], ACT.Sqrt), "rms")
                after(dve_s, f"mean{TILES - 1}")
                act_s.did(act.activation(dev[:, :], mv[:, :, 1], ACT.Sqrt, bias=eps[:, 0:1]), "deviation")
                after(pe_s, "turned")
                act_s.did(act.activation(XT[:, bass.ds(s, 1), PAD:].rearrange("p o t -> p (o t)"), bank[6][:, :], ACT.Identity), "stored")
                act_s.did(act.activation(X1T[:, bass.ds(s, 1), :].rearrange("p o t -> p (o t)"), bank[6][:, :], ACT.Identity), "kept")
            act.wait_ge(act_s.sem, act_s.count(B - 1, "kept"))

        @blk.tensor
        def _(pe):
            pe.sem_inc(pe_s.sem, ONE)
            pe.wait_ge(loaded, 16 * len(loads))
            pe.wait_ge(vector_ready, 5)
            pe.matmul(bank[0][:, 0:8], rep16[:, :], w16[:, :], start=True, stop=True).then_inc(spread_ready, 1)
            pe.wait_ge(setup_done, 1)
            with pe.Fori(0, B) as s:
                def after(steps, name):
                    pe.wait_ge(steps.sem, steps.count(s, name))

                pe.wait_ge(act_s.sem, act_s.count(s, "kept") - len(act_s.names))
                for c in (2, 0, 1):
                    w = K if c == 2 else P
                    pe_s.did(pe.matmul(bank[c][0:w, :], w_in[:, P * c:P * c + w],
                                       xin[:, bass.ds(s, 1), :].rearrange("p o t -> p (o t)"), start=True, stop=True), f"z{c}")
                after(dve_s, "weight")
                pe_s.did(pe.matmul(bank[3][:, :], spread[:, :], pw[:, :], start=True, stop=True), "spread")
                after(dve_s, "g")
                for t in range(TILES):
                    mm = pe.transpose(bank[6][:, P * t:P * t + P], poly[:, P * t:P * t + P], ident[:, :])
                pe_s.did(mm, "g turned")
                for t in range(TILES):
                    if t >= 2:
                        after(dve_s, f"turn{t - 2}")
                    pe_s.did(pe.matmul(bank[4 + t % 2][:, :], conv[:, 0, P * t:P * t + P],
                                       theta[:, :, :].rearrange("p c m -> p (c m)"), start=True, stop=True), f"phase{t}")
                after(dve_s, f"im{TILES - 1}")

                def contract(c):
                    after(act_s, f"square{c}")
                    pe.matmul(bank[7][:, :], w_blk[:, c, :], num[:, c % 2, :], start=(c == 0), stop=(c == 7))
                    pe_s.did(pe.matmul(bank[2][:, :], sum_blk[:, c % 4, :], sq[:, c % 2, :],
                                       start=(c == 0), stop=(c == 7)), f"contracted{c}")

                for c in range(8):
                    if c >= 2:
                        after(dve_s, f"num{c - 2}")
                    for t in range(TILES):
                        mm = pe.matmul(bank[c % 2][:, P * t:L], moments[:, t, P * c:P * c + P], late[:, 0:L - P * t],
                                       start=(t == 0), stop=(t == TILES - 1))
                    pe_s.did(mm, f"cumulated{c}")
                    if c >= 1:
                        contract(c - 1)
                contract(7)
                after(dve_s, "yg")
                for t in range(TILES):
                    mm = pe.matmul(bank[3][:, P * t:P * t + P], yg[:, P * t:P * t + P], w_out[:, :], start=True, stop=True)
                pe_s.did(mm, "out")
                after(dve_s, f"norm{TILES - 1}")
                for t in range(TILES):
                    mm = pe.transpose(bank[6][:, P * t:P * t + P], res_n[:, t, :], ident[:, :])
                pe_s.did(mm, "turned")


def attention_layers(nc, a, XT, ident):
    with ExitStack() as ctx:
        def sb(name, shape, dt=F32):
            return ctx.enter_context(nc.sbuf_tensor("b_" + name, shape, dt))

        def event(name, per=1):
            return Event(ctx.enter_context(nc.semaphore("b_" + name)), per)

        proj = [ctx.enter_context(nc.psum_tensor(f"b_proj{i}", [P, 512], F32)) for i in range(2)]
        scores = ctx.enter_context(nc.psum_tensor("b_scores", [P, 2, 512], F32))
        turned = [ctx.enter_context(nc.psum_tensor(f"b_turned{i}", [P, 4, P], F32)) for i in range(2)]
        mix = ctx.enter_context(nc.psum_tensor("b_mix", [P, 2, 512], F32))

        wqkv, wo = sb("wqkv", [P, 3 * INNER]), sb("wo", [P, PAIRS, D])
        w1, w2 = sb("w1", [P, 2 * HID]), sb("w2", [P, len(CHUNKS), D])
        vectors, vec = sb("vectors", [P, DEPTH, 9]), sb("vec", [P, 9])
        B1, B1_GATE, LN_G, LN_B, B2 = 0, 3, 6, 7, 8
        rope, qk_scale = sb("rope", [P, TILES, 2, 2, DH]), sb("qk_scale", [P, 2, 2, DH])
        table = sb("table", [P, TILES, 2, 2, DH])
        mask32, mask = sb("mask32", [P, 2, 512]), sb("mask", [P, 2, 512], BF16)
        ident16 = sb("ident16", [P, P], BF16)
        xs = sb("xs", [P, 2, WIN + P])
        raw, sq = sb("raw", [P, 4, 512]), sb("sq", [P, 2, 512])
        qk, other = sb("qk", [P, 2, 4, 512]), sb("other", [P, 2, 512])
        ss, inv, half = sb("ss", [P, 32]), sb("inv", [P, 2, 32]), sb("half", [P, 32])
        qT, kT = sb("qT", [P, PAIRS, P]), sb("kT", [P, 2, PAIRS, 2, WIN + P])
        top, total = sb("top", [P, HEADS]), sb("total", [P, HEADS])
        prob, probT = sb("prob", [P, HEADS, 2 * WIN]), sb("probT", [P, PAIRS, P])
        v = sb("v", [P, 2, TILES, PAIRS, P])
        mixed_n, mixedT = sb("mixed_n", [P, HEADS, DH]), sb("mixedT", [P, PAIRS, P])
        xf, xn, xnT = sb("xf", [P, L]), sb("xn", [P, TILES, D]), sb("xnT", [P, L])
        hid = sb("hid", [P, 3, L])
        stats, mv = sb("stats", [P, TILES, 6]), sb("mv", [P, TILES, 2])
        var, dev, dev_half, pause = sb("var", [P, TILES]), sb("dev", [P, TILES]), sb("dev_half", [P, TILES]), sb("pause", [P, 1])

        fixed_loaded, qkv_loaded, scale_loaded = event("fixed_loaded"), event("qkv_loaded"), event("scale_loaded")
        wo_loaded, ffn_loaded = event("wo_loaded"), event("ffn_loaded")
        fixed_made, tables_made = event("fixed_made", 3), event("tables_made", 3)
        staged = event("staged")
        qk_projected = event("qk_projected", 4)
        copied, squared = event("copied", 4), event("squared", 4)
        rotated = event("rotated", 4)
        squares_summed = event("squares_summed", 4)
        norm_step = event("norm_step", RSQRT + 1)
        rope_summed, normed = event("rope_summed", 4), event("normed", 4)
        qk_turned, qk_placed = event("qk_turned", 4), event("qk_placed", 4)
        carried = event("carried")
        scored = event("scored")
        top_found, subtracted = event("top_found"), event("subtracted")
        exped = event("exped")
        totalled, inverted = event("totalled"), event("inverted")
        p_turned, p_placed = event("p_turned", 2), event("p_placed", 2)
        v_projected, v_placed = event("v_projected", TILES), event("v_placed", TILES)
        mixed, normalised = event("mixed", 2), event("normalised")
        o_turned, o_placed = event("o_turned", 2), event("o_placed", 2)
        attn_projected, attn_added = event("attn_projected"), event("attn_added")
        f_staged, f_turned = event("f_staged"), event("f_turned")
        f_norm_step, f_normed = event("f_norm_step", 3 + RSQRT), event("f_normed")
        f_back, f_scaled = event("f_back"), event("f_scaled")
        f_gate, f_value = event("f_gate", 3), event("f_value", 3)
        gated, hidden = event("gated", 3), event("hidden", 3)
        f_out, f_added = event("f_out"), event("f_added")

        def wait(engine, ev, rounds, part=None):
            engine.wait_ge(ev.sem, ev.value(rounds, part))

        def lags(t, prev, new):
            return new, (new or t < 1) and (prev or t >= 1), (new or t < 2) and (prev or t >= 2)

        def rounds(engine, body):
            with engine.Fori(0, DEPTH_RUN) as layer:
                body(layer, layer * B, 0, False, True)
                with engine.Fori(1, B) as s:
                    body(layer, layer * B + s, s, True, True)
                body(layer, layer * B + B, B, True, False)

        b1 = a["b1"]
        fixed = [(rope[:, :, :, :, :].rearrange("p t q c d -> p (t q c d)"), a["rope"]),
                 (mask32[:, :, :].rearrange("p n c -> p (n c)"), a["mask"]),
                 (vectors[:, :, LN_G], a["ln_g"]), (vectors[:, :, LN_B], a["ln_b"]), (vectors[:, :, B2], a["b2"])]
        for c, (c0, rows) in enumerate(CHUNKS):
            for col, at in ((B1, c0), (B1_GATE, HID + c0)):
                fixed.append((vectors[0:rows, :, col + c], b1[:, at:at + rows].rearrange("l p -> p l")))

        blk = ctx.enter_context(nc.Block())

        @blk.sync
        def _(sp):
            wait(sp, fixed_made, 0, 0)
            with nc.allow_non_contiguous_dma(reason="small per-channel vectors"):
                for dst, src in fixed:
                    sp.dma_start(dst, src).then_inc(fixed_loaded.sem, 16)
            with sp.Fori(0, DEPTH_RUN) as layer:
                one = lambda x: x[bass.ds(layer, 1)]
                wait(sp, v_projected, layer * (B * TILES) - 1)
                sp.dma_start(wqkv[:, :], one(a["Wqkv"]).rearrange("o p n -> p (o n)")).then_inc(qkv_loaded.sem, 16)
                wait(sp, tables_made, layer - 1)
                sp.dma_start(qk_scale[:, :, :, :].rearrange("p q c d -> p (q c d)"),
                             one(a["qk_scale"]).rearrange("o p n -> p (o n)")).then_inc(scale_loaded.sem, 16)
                wait(sp, attn_projected, layer * (B * TILES) - 1)
                sp.dma_start(wo[:, :, :], one(a["Wo"]).rearrange("o (c p) n -> p (o c) n", p=P)).then_inc(wo_loaded.sem, 16)
                wait(sp, f_out, layer * B - 1)
                sp.dma_start(w1[:, :], one(a["W1"]).rearrange("o p n -> p (o n)")).then_inc(ffn_loaded.sem, 16)
                sp.dma_start(w2[:, 0:2, :], a["W2"][bass.ds(layer, 1), 0:2 * P].rearrange("o (c p) n -> p (o c) n", p=P)).then_inc(ffn_loaded.sem, 16)
                sp.dma_start(w2[0:CHUNKS[2][1], 2, :], a["W2"][bass.ds(layer, 1), 2 * P:HID].rearrange("o p n -> p (o n)")).then_inc(ffn_loaded.sem, 16)

        @blk.vector
        def _(dve):
            credit = (staged, rotated, squares_summed, norm_step, top_found, subtracted, totalled, inverted,
                      normalised, attn_added, f_staged, f_norm_step, f_normed, hidden, f_added, tables_made, fixed_made)
            for ev in credit:
                dve.sem_inc(ev.sem, 2 * ev.per)
            dve.memset(vectors[:, :, :], 0.0).then_inc(fixed_made.sem, 1)
            dve.memset(v[:, 0, :, :, :].rearrange("p t c d -> p (t c d)"), 0.0)
            dve.memset(v[:, 1, :, :, :].rearrange("p t c d -> p (t c d)"), 0.0)
            dve.memset(kT[:, 0, :, :, :].rearrange("p c n t -> p (c n t)"), 0.0)
            dve.memset(kT[:, 1, :, :, :].rearrange("p c n t -> p (c n t)"), 0.0).then_inc(fixed_made.sem, 1)
            dve.wait_ge(fixed_loaded.sem, 16 * len(fixed))
            dve.tensor_copy(ident16[:, :], ident[:, :])
            dve.tensor_copy(mask[:, :, :], mask32[:, :, :]).then_inc(fixed_made.sem, 1)

            def body(layer, it, s, prev, new):
                slot = bass.ds(s, 1)
                before = bass.ds(s - 1, 1)

                def stage(t):
                    n = it * TILES + t
                    wait(dve, v_projected, n - 2)
                    for h in range(2):
                        ch = slice(DH * h, DH * h + DH)
                        at = PAD - WIN + P * t - h
                        cp = dve.tensor_copy(xs[ch, t % 2, :], XT[ch, slot, at:at + WIN + P].rearrange("p o t -> p (o t)"))
                    cp.then_inc(staged.sem, 1)

                if not prev:
                    dve.wait_ge(scale_loaded.sem, layer * 16 + 16)
                    wait(dve, rotated, it * TILES - 1)
                    for q in range(2):
                        for c in range(2):
                            tb = dve.tensor_tensor(table[:, :, q, c, :], rope[:, :, q, c, :],
                                                   qk_scale[:, q, c, :].unsqueeze(1).to_broadcast([P, TILES, DH]), ALU.mult)
                    tb.then_inc(tables_made.sem, 1)
                    wait(dve, hidden, it - 1)
                    wait(dve, f_scaled, it - 1)
                    wait(dve, gated, it - 1)
                    wait(dve, f_added, it - 1)
                    dve.tensor_copy(vec[:, :], vectors[:, bass.ds(layer, 1), :].rearrange("p o c -> p (o c)")).then_inc(tables_made.sem, 1)
                    dve.memset(pause[:, :], 0.0).then_inc(tables_made.sem, 1)
                    wait(dve, tables_made, layer)
                for t in range(TILES):
                    cur, l1, l2 = lags(t, prev, new)
                    n = it * TILES + t
                    i = t % 2
                    if cur and t == 0:
                        stage(0)
                    if cur and t < TILES - 1:
                        stage(t + 1)
                    if prev and t == 2:
                        wait(dve, attn_added, it * TILES - 1)
                        for h in range(2):
                            ch = slice(DH * h, DH * h + DH)
                            cp = dve.tensor_copy(xf[ch, :], XT[ch, before, PAD - h:PAD - h + L].rearrange("p o t -> p (o t)"))
                        cp.then_inc(f_staged.sem, 1)
                    if cur:
                        wait(dve, qk_turned, n - 2)
                        for j in range(4):
                            kind = j // 2
                            wait(dve, copied, n, j)
                            heads = raw[:, j, :].rearrange("p (h c d) -> p h c d", c=2, d=DH // 2)
                            cos = table[:, t, kind, 0, :].rearrange("p (c d) -> p c d", c=2).unsqueeze(1).to_broadcast([P, 8, 2, DH // 2])
                            sin = table[:, t, kind, 1, :].rearrange("p (c d) -> p c d", c=2).unsqueeze(1).to_broadcast([P, 8, 2, DH // 2])
                            dve.tensor_tensor(qk[:, i, j, :].rearrange("p (h c d) -> p h c d", c=2, d=DH // 2), heads, cos, ALU.mult)
                            if j >= 2:
                                wait(dve, rope_summed, n, j - 2)
                            else:
                                wait(dve, rope_summed, n - 1, j + 2)
                            dve.tensor_tensor(other[:, j % 2, :].rearrange("p (h c d) -> p h c d", c=2, d=DH // 2),
                                              heads[:, :, ::-1, :], sin, ALU.mult).then_inc(rotated.sem, 1)
                            wait(dve, squared, n, j)
                            dve.tensor_reduce(ss[:, 8 * j:8 * j + 8], sq[:, j % 2, :].rearrange("p (h d) -> p h d", d=DH),
                                              AX.X, ALU.add).then_inc(squares_summed.sem, 1)
                        wait(dve, squares_summed, n)
                        wait(dve, normed, n - 2)
                        own = [0]

                        def tick(ins):
                            ins.then_inc(norm_step.sem, 1)
                            wait(dve, norm_step, n, own[0])
                            own[0] += 1

                        tick(dve.tensor_scalar(ss[:, :], ss[:, :], 1e-24, None, ALU.max))
                        rsqrt(dve, tick, ss[:, :], inv[:, i, :], half[:, :])
                        assert own[0] == norm_step.per
                    if l2:
                        wait(dve, mixed, n - 2)
                        wait(dve, o_turned, n - 3)
                        dve.tensor_tensor(mixed_n[:, :, :], mix[:, :, :].rearrange("p n (h d) -> p (n h) d", d=DH),
                                          total[:, :].unsqueeze(2).to_broadcast([P, HEADS, DH]), ALU.mult).then_inc(normalised.sem, 1)
                    if l1:
                        wait(dve, scored, n - 1)
                        s3 = scores[:, :, :].rearrange("p n (h j) -> p (n h) j", j=2 * WIN)
                        dve.tensor_reduce(top[:, :], s3, AX.X, ALU.max).then_inc(top_found.sem, 1)
                        wait(dve, top_found, n - 1)
                        wait(dve, p_turned, n - 2)
                        dve.tensor_tensor(prob[:, :, :], s3, top[:, :].unsqueeze(2).to_broadcast([P, HEADS, 2 * WIN]),
                                          ALU.subtract).then_inc(subtracted.sem, 1)
                        wait(dve, exped, n - 1)
                        dve.tensor_reduce(total[:, :], prob[:, :, :], AX.X, ALU.add).then_inc(totalled.sem, 1)
                        wait(dve, totalled, n - 1)
                        dve.reciprocal(total[:, :], total[:, :]).then_inc(inverted.sem, 1)
                        wait(dve, inverted, n - 1)
                    if l2:
                        wait(dve, attn_projected, n - 2)
                        at = PAD + P * ((t - 2) % TILES)
                        x = XT[:, slot if t >= 2 else before, at:at + P].rearrange("p o t -> p (o t)")
                        dve.tensor_tensor(x, x, mix[:, 0, 0:P], ALU.add).then_inc(attn_added.sem, 1)
                    if prev and t == 2:
                        wait(dve, f_turned, it - 1)
                        m = mix[:, 1, :].rearrange("p (t d) -> p t d", d=D)
                        fown = [0]

                        def ftick(ins):
                            ins.then_inc(f_norm_step.sem, 1)
                            wait(dve, f_norm_step, it - 1, fown[0])
                            fown[0] += 1

                        for k in range(TILES):
                            st = dve.bn_stats(stats[:, k, :], m[:, k, :])
                        ftick(st)
                        dve.memset(pause[:, :], 0.0)
                        for k in range(TILES):
                            st = dve.bn_aggr(mv[:, k, :], stats[:, k, :])
                        ftick(st)
                        ftick(dve.tensor_scalar(var[:, :], mv[:, :, 1], LN_EPS, None, ALU.add))
                        rsqrt(dve, ftick, var[:, :], dev[:, :], dev_half[:, :])
                        for k in range(TILES):
                            st = dve.tensor_scalar(xn[:, k, :], m[:, k, :], mv[:, k, 0:1], dev[:, k:k + 1], ALU.subtract, ALU.mult)
                        st.then_inc(f_normed.sem, 1)
                    if prev and t == 3:
                        for c, (_, rows) in enumerate(CHUNKS):
                            wait(dve, gated, it - 1, c)
                            wait(dve, f_value, it - 1, c)
                            dve.scalar_tensor_tensor(out=hid[0:rows, c, :], in0=mix[0:rows, 1, :], scalar=vec[0:rows, B1 + c:B1 + c + 1],
                                                     in1=hid[0:rows, c, :], op0=ALU.add, op1=ALU.mult).then_inc(hidden.sem, 1)
                        wait(dve, f_out, it - 1)
                        x = XT[:, before, PAD:].rearrange("p o t -> p (o t)")
                        dve.scalar_tensor_tensor(out=x, in0=mix[:, 0, :], scalar=vec[:, B2:B2 + 1], in1=x,
                                                 op0=ALU.add, op1=ALU.add).then_inc(f_added.sem, 1)

            rounds(dve, body)

        @blk.scalar
        def _(act):
            for ev in (copied, squared, qk_placed, carried, exped, p_placed, v_placed, o_placed, f_scaled, gated):
                act.sem_inc(ev.sem, 2 * ev.per)
            wait(act, fixed_made, 0)

            def body(layer, it, s, prev, new):
                for t in range(TILES):
                    cur, l1, l2 = lags(t, prev, new)
                    n = it * TILES + t
                    i = t % 2
                    if cur:
                        for j in range(4):
                            wait(act, qk_projected, n, j)
                            wait(act, rotated, n - 1, j)
                            act.activation(raw[:, j, :], proj[j % 2][:, :], ACT.Identity).then_inc(copied.sem, 1)
                            wait(act, copied, n, j)
                            if j >= 2:
                                wait(act, squares_summed, n, j - 2)
                            else:
                                wait(act, squares_summed, n - 1, j + 2)
                            act.activation(sq[:, j % 2, :], raw[:, j, :], ACT.Square).then_inc(squared.sem, 1)
                    if l2:
                        for j in range(2):
                            wait(act, p_turned, n - 2, j)
                            act.activation(probT[:, 4 * j:4 * j + 4, :], turned[j][:, :, :], ACT.Identity).then_inc(p_placed.sem, 1)
                    if l1:
                        o = (t - 1) % 2
                        for j in range(4):
                            wait(act, qk_turned, n - 1, j)
                            pairs = slice(4 * (j % 2), 4 * (j % 2) + 4)
                            if j < 2:
                                cp = act.activation(qT[:, pairs, :], turned[j % 2][:, :, :], ACT.Identity)
                            else:
                                for h in range(2):
                                    ch = slice(DH * h, DH * h + DH)
                                    cp = act.activation(kT[ch, o, pairs, h, WIN:], turned[j % 2][ch, :, :], ACT.Identity)
                            cp.then_inc(qk_placed.sem, 1)
                        wait(act, qk_placed, n - 1)
                        act.activation(kT[:, 1 - o, :, :, 0:WIN].rearrange("p c n t -> p (c n) t"),
                                       kT[:, o, :, :, P:].rearrange("p c n t -> p (c n) t"), ACT.Identity).then_inc(carried.sem, 1)
                    if l2:
                        for j in range(2):
                            wait(act, o_turned, n - 2, j)
                            act.activation(mixedT[:, 4 * j:4 * j + 4, :], turned[j][:, :, :], ACT.Identity).then_inc(o_placed.sem, 1)

                    def place_v(w):
                        wait(act, v_projected, n, w)
                        for h in range(2):
                            ch = slice(DH * h, DH * h + DH)
                            cp = act.activation(v[ch, i, w, :, ch], proj[w % 2][ch, :].rearrange("p (c d) -> p c d", d=DH), ACT.Identity)
                        cp.then_inc(v_placed.sem, 1)

                    if cur:
                        place_v(0)
                        place_v(1)
                    if l1:
                        wait(act, subtracted, n - 1)
                        act.activation(prob[:, :, :], prob[:, :, :], ACT.Exp).then_inc(exped.sem, 1)
                    if cur:
                        place_v(2)
                        place_v(3)
                    if prev and t == 3:
                        wait(act, f_back, it - 1)
                        act.activation(xnT[:, :], mix[:, 1, :], ACT.Identity, scale=vec[:, LN_G:LN_G + 1],
                                       bias=vec[:, LN_B:LN_B + 1]).then_inc(f_scaled.sem, 1)
                        for c, (_, rows) in enumerate(CHUNKS):
                            wait(act, f_gate, it - 1, c)
                            act.activation(hid[0:rows, c, :], mix[0:rows, 0, :], ACT.Gelu,
                                           bias=vec[0:rows, B1_GATE + c:B1_GATE + c + 1]).then_inc(gated.sem, 1)

            rounds(act, body)

        @blk.gpsimd
        def _(pool):
            for ev in (rope_summed, normed):
                pool.sem_inc(ev.sem, 2 * ev.per)

            def body(layer, it, s, prev, new):
                for t in range(TILES):
                    if not new:
                        continue
                    n = it * TILES + t
                    i = t % 2
                    for j in range(4):
                        wait(pool, rotated, n, j)
                        pool.tensor_tensor(qk[:, i, j, :], qk[:, i, j, :], other[:, j % 2, :], ALU.add).then_inc(rope_summed.sem, 1)
                    wait(pool, norm_step, n)
                    for j in range(4):
                        wait(pool, rope_summed, n, j)
                        x = qk[:, i, j, :].rearrange("p (h d) -> p h d", d=DH)
                        pool.tensor_tensor(x, x, inv[:, i, 8 * j:8 * j + 8].unsqueeze(2).to_broadcast([P, 8, DH]),
                                           ALU.mult).then_inc(normed.sem, 1)

            rounds(pool, body)

        @blk.tensor
        def _(pe):
            for ev in (qk_projected, qk_turned, scored, p_turned, v_projected, mixed, o_turned, attn_projected,
                       f_turned, f_back, f_gate, f_value, f_out):
                pe.sem_inc(ev.sem, 2 * ev.per)
            wait(pe, fixed_made, 0)

            def body(layer, it, s, prev, new):
                for t in range(TILES):
                    cur, l1, l2 = lags(t, prev, new)
                    n = it * TILES + t
                    i = t % 2
                    if cur:
                        if t == 0 and not prev:
                            pe.wait_ge(qkv_loaded.sem, layer * 16 + 16)
                        wait(pe, staged, n)
                        for j in range(4):
                            if j >= 2:
                                wait(pe, copied, n, j - 2)
                            else:
                                wait(pe, v_placed, n - 1, j + 2)
                            pe.matmul(proj[j % 2][:, :], xs[:, i, WIN:], wqkv[:, 512 * j:512 * j + 512],
                                      start=True, stop=True).then_inc(qk_projected.sem, 1)
                    if l2:
                        wait(pe, exped, n - 2)
                        for j in range(2):
                            wait(pe, o_placed, n - 3, j)
                            for c in range(4):
                                pr = prob[:, 8 * j + 2 * c:8 * j + 2 * c + 2, :].rearrange("p h k -> p (h k)")
                                mm = pe.transpose(turned[j][:, c, :], pr, ident[:, :])
                            mm.then_inc(p_turned.sem, 1)
                    if l1:
                        for j in range(4):
                            wait(pe, normed, n - 1, j)
                            if j >= 2:
                                wait(pe, qk_placed, n - 1, j - 2)
                            elif l2:
                                wait(pe, p_placed, n - 2, j)
                            for c in range(4):
                                mm = pe.transpose(turned[j % 2][:, c, :], qk[:, (t - 1) % 2, j, P * c:P * c + P], ident[:, :])
                            mm.then_inc(qk_turned.sem, 1)
                    if l2:
                        wait(pe, p_placed, n - 2)
                        wait(pe, v_placed, n - 2)
                        wait(pe, attn_added, n - 3)
                        wait(pe, normalised, n - 3)
                        if prev and t == 0:
                            wait(pe, f_added, it - 2)
                            wait(pe, hidden, it - 2)
                        if prev and t == 3:
                            wait(pe, f_normed, it - 1)
                        for j in range(2):
                            for c in range(4):
                                for w in range(TILES):
                                    q = slice(WIN * w, WIN * w + WIN)
                                    mm = pe.matmul(mix[q, j, P * c:P * c + P], probT[:, 4 * j + c, q], v[:, i, w, 4 * j + c, :],
                                                   start=True, stop=True, skip_group_check=True)
                            mm.then_inc(mixed.sem, 1)
                    if l1:
                        wait(pe, qk_placed, n - 1)
                        wait(pe, carried, n - 2)
                        wait(pe, subtracted, n - 2)
                        for j in range(2):
                            pe.matmul(scores[:, j, :], ident16[:, :], mask[:, 0 if t == 1 else 1, :],
                                      start=True, stop=False, skip_group_check=True)
                            for c in range(4):
                                for w in range(TILES):
                                    q = slice(WIN * w, WIN * w + WIN)
                                    mm = pe.matmul(scores[q, j, P * c:P * c + P].rearrange("p (n k) -> p n k", n=2), qT[:, 4 * j + c, q],
                                                   kT[:, (t - 1) % 2, 4 * j + c, :, WIN * w:WIN * w + 2 * WIN],
                                                   start=False, stop=True, skip_group_check=True)
                        mm.then_inc(scored.sem, 1)
                    if l2:
                        wait(pe, normalised, n - 2)
                        for j in range(2):
                            if l1:
                                wait(pe, qk_placed, n - 1, 2 + j)
                            for c in range(4):
                                o = mixed_n[:, 8 * j + 2 * c:8 * j + 2 * c + 2, :].rearrange("p h d -> p (h d)")
                                mm = pe.transpose(turned[j][:, c, :], o, ident[:, :])
                            mm.then_inc(o_turned.sem, 1)
                    if cur:
                        for w in range(TILES):
                            if w < 2:
                                wait(pe, copied, n, w + 2)
                            else:
                                wait(pe, v_placed, n, w - 2)
                            for h in range(2):
                                wv = wqkv[:, 2 * INNER:].rearrange("p (c h d) -> p c h d", h=2, d=DH)[:, :, h, :]
                                mm = pe.matmul(proj[w % 2][DH * h:DH * h + DH, :].rearrange("p (c d) -> p c d", d=DH),
                                               xs[:, i, WIN * w:WIN * w + 2 * WIN], wv, start=True, stop=True, skip_group_check=True)
                            mm.then_inc(v_projected.sem, 1)
                    if prev and t == 3:
                        wait(pe, f_normed, it - 1)
                        if l2:
                            wait(pe, normalised, n - 2)
                        for k in range(TILES):
                            mm = pe.transpose(mix[:, 1, P * k:P * k + P], xn[:, k, :], ident[:, :])
                        mm.then_inc(f_back.sem, 1)
                    if l2:
                        if t == 2 and not prev:
                            pe.wait_ge(wo_loaded.sem, layer * 16 + 16)
                        wait(pe, o_placed, n - 2)
                        for c in range(PAIRS):
                            mm = pe.matmul(mix[:, 0, 0:P], wo[:, c, :], mixedT[:, c, :], start=(c == 0), stop=(c == PAIRS - 1))
                        mm.then_inc(attn_projected.sem, 1)
                    if prev and t == 2:
                        wait(pe, f_staged, it - 1)
                        for k in range(TILES):
                            mm = pe.transpose(mix[:, 1, P * k:P * k + P], xf[:, P * k:P * k + P], ident[:, :])
                        mm.then_inc(f_turned.sem, 1)
                    if prev and t == 3:
                        pe.wait_ge(ffn_loaded.sem, layer * 48 + 48)
                        wait(pe, f_scaled, it - 1)
                        if l2:
                            wait(pe, attn_added, n - 2)
                        for c, (c0, rows) in enumerate(CHUNKS):
                            if c:
                                wait(pe, gated, it - 1, c - 1)
                            pe.matmul(mix[0:rows, 0, :], w1[:, HID + c0:HID + c0 + rows], xnT[:, :], start=True, stop=True).then_inc(f_gate.sem, 1)
                            if c:
                                wait(pe, hidden, it - 1, c - 1)
                            pe.matmul(mix[0:rows, 1, :], w1[:, c0:c0 + rows], xnT[:, :], start=True, stop=True).then_inc(f_value.sem, 1)
                        wait(pe, hidden, it - 1)
                        for c, (c0, rows) in enumerate(CHUNKS):
                            mm = pe.matmul(mix[:, 0, :], w2[0:rows, c, :], hid[0:rows, c, :], start=(c == 0), stop=(c == 2))
                        mm.then_inc(f_out.sem, 1)

            rounds(pe, body)


def final_norm(nc, a, XT, X1T, ident, out):
    with ExitStack() as ctx:
        def sb(name, shape, dt=F32):
            return ctx.enter_context(nc.sbuf_tensor("c_" + name, shape, dt))

        def sem(name):
            return ctx.enter_context(nc.semaphore("c_" + name))

        bank = [ctx.enter_context(nc.psum_tensor(f"c_bank{i}", [P, TILES, D], F32)) for i in range(2)]
        total, tok = sb("total", [P, 2, L]), sb("tok", [P, 2, TILES, D])
        stats, mv = sb("stats", [P, TILES, 6]), sb("mv", [P, TILES, 2])
        dev, eps, pause = sb("dev", [P, TILES]), sb("eps", [P, 1]), sb("pause", [P, 1])
        turned, deviation = sem("turned"), sem("deviation")
        stored = [sem("stored_even"), sem("stored_odd")]
        steps = Steps(sem("vector_step"), [f"{n}{q}" for q in range(2) for n in (
            ["total"] + [f"stats{t}" for t in range(TILES)] + [f"mean{t}" for t in range(TILES)] + ["inv dev"]
            + [f"norm{t}" for t in range(TILES)])])
        blk = ctx.enter_context(nc.Block())

        @blk.vector
        def _(dve):
            dve.sem_inc(steps.sem, ONE)
            dve.memset(eps[:, :], LN_EPS)
            with dve.Fori(0, B // 2) as s2:
                def step(instruction, name, wait=True):
                    steps.did(instruction, name)
                    if wait:
                        dve.wait_ge(steps.sem, steps.count(s2, name))

                for q in range(2):
                    s = s2 * 2 + q
                    step(dve.tensor_tensor(total[:, q, :], XT[:, bass.ds(s, 1), PAD:].rearrange("p o t -> p (o t)"),
                                           X1T[:, bass.ds(s, 1), :].rearrange("p o t -> p (o t)"), ALU.add), f"total{q}", False)
                    dve.wait_ge(turned, s + 1)
                    for t in range(TILES):
                        step(dve.bn_stats(stats[:, t, :], bank[q][:, t, :]), f"stats{t}{q}", t == TILES - 1)
                    dve.memset(pause[:, :], 0.0)
                    for t in range(TILES):
                        step(dve.bn_aggr(mv[:, t, :], stats[:, t, :]), f"mean{t}{q}", False)
                    dve.wait_ge(deviation, s + 1)
                    step(dve.reciprocal(dev[:, :], dev[:, :]), f"inv dev{q}")
                    dve.wait_ge(stored[q], s2 * 16 + 1)
                    for t in range(TILES):
                        step(dve.tensor_scalar(tok[:, q, t, :], bank[q][:, t, :], mv[:, t, 0:1], dev[:, t:t + 1],
                                               ALU.subtract, ALU.mult), f"norm{t}{q}", False)

        @blk.scalar
        def _(act):
            with act.Fori(0, B // 2) as s2:
                for q in range(2):
                    act.wait_ge(steps.sem, steps.count(s2, f"mean{TILES - 1}{q}"))
                    act.activation(dev[:, :], mv[:, :, 1], ACT.Sqrt, bias=eps[:, 0:1]).then_inc(deviation, 1)

        @blk.tensor
        def _(pe):
            with pe.Fori(0, B // 2) as s2:
                for q in range(2):
                    pe.wait_ge(steps.sem, steps.count(s2, f"total{q}"))
                    for t in range(TILES):
                        mm = pe.transpose(bank[q][:, t, :], total[:, q, P * t:P * t + P], ident[:, :])
                    mm.then_inc(turned, 1)

        @blk.sync
        def _(sp):
            sp.sem_inc(stored[0], ONE)
            sp.sem_inc(stored[1], ONE)
            with sp.Fori(0, B // 2) as s2:
                for q in range(2):
                    s = s2 * 2 + q
                    sp.wait_ge(steps.sem, steps.count(s2, f"norm{TILES - 1}{q}"))
                    sp.dma_start(out[bass.ds(s, 1)].rearrange("o (t p) d -> p (o t) d", p=P), tok[:, q, :, :]).then_inc(stored[q], 16)
            for q in range(2):
                sp.wait_ge(stored[q], ONE + 16 * B // 2)


def build(nc, a, out, layers=True):
    with ExitStack() as ctx:
        XT = ctx.enter_context(nc.sbuf_tensor("XT", [P, B, SPAN], F32))
        X1T = ctx.enter_context(nc.sbuf_tensor("X1T", [P, B, L], F32))
        ident = ctx.enter_context(nc.sbuf_tensor("ident", [P, P], F32))
        state_space_layer(nc, a, XT, X1T, ident)
        if layers:
            attention_layers(nc, a, XT, ident)
        final_norm(nc, a, XT, X1T, ident, out)


def lay_out(x):
    f = lambda v: np.ascontiguousarray(v)
    g = {n: np.asarray(v) for n, v in x.items()}
    rows = lambda v: f(np.broadcast_to(v.reshape(1, -1), (P, v.size)))
    qk = np.stack([g["L0_ffn_q_scale"], g["L0_ffn_k_scale"]], 1)
    back = np.concatenate([qk[..., DH // 2:], qk[..., :DH // 2]], -1)
    qk = np.stack([qk, back], 2)
    W2 = g["L0_ffn_W2"]
    d = dict(
        x=g["L0_attn_x"], xT=f(g["L0_attn_x"].transpose(2, 0, 1)), W_in=g["L0_attn_W_in"],
        W_out=g["L0_attn_W_out"], w_conv=f(g["L0_attn_w_conv"][:, 0, :].T), b_conv=g["L0_attn_b_conv"],
        theta=rows(g["L0_attn_theta"]), logits=rows(g["L0_attn_deriv_logits"]),
        slopes=np.concatenate([g["L0_attn_decay_slopes"], g["L0_attn_anchor_slopes"]]),
        score_scale=g["L0_attn_score_scale"], W_re=g["L0_attn_W_re"], W_im=g["L0_attn_W_im"],
        norm_scale=g["L0_attn_norm_scale"],
        Wqkv=g["L0_ffn_Wqkv"], qk_scale=f(np.broadcast_to(qk.reshape(DEPTH, 1, -1), (DEPTH, P, qk[0].size))),
        Wo=g["L0_ffn_Wo"], ln_g=f(g["L0_ffn_ln_g"].T), ln_b=f(g["L0_ffn_ln_b"].T),
        W1=g["L0_ffn_W1"], b1=g["L0_ffn_b1"], W2=W2, b2=f(g["L0_ffn_b2"].T))
    d.update(constants())
    return d


def kernel(**inputs):
    import concourse.bacc as _bacc
    from concourse.bass_utils import run_bass_kernel_spmd as _run

    nc = _bacc.Bacc("TRN2", target_bir_lowering=False, num_devices=1)
    arrays = {f"in_{n}_dram": v for n, v in lay_out(inputs).items()}
    a = {n[3:-5]: nc.dram_tensor(n, v.shape, mybir.dt.from_np(v.dtype), kind="ExternalInput").ap()
         for n, v in arrays.items()}
    out = nc.dram_tensor("out_dram", (B, L, D), F32, kind="ExternalOutput").ap()
    build(nc, a, out)
    r = _run(nc, [arrays], core_ids=[0])
    return r.results[0]["out_dram"]
```

```python
from contextlib import ExitStack

import numpy as np

import concourse.bass as bass
from concourse import mybir

F32 = mybir.dt.float32
BF16 = mybir.dt.bfloat16
F32R = mybir.dt.float32r
I32 = mybir.dt.int32
ALU = mybir.AluOpType
ACT = mybir.ActivationFunctionType
AX = mybir.AxisListType

P = 128
B, L, D = 8, 512, 128
TILES = L // P
K, H, M = 32, 4, 4
TAPS = 4
TOTAL = 2 * D + K
LN_EPS = 1e-5
MAGIC = 12582912.0
TWO_PI = 6.283185
TURN = 1.0 / 6.283185307179586
DEPTH, HEADS, DH, WIN = 6, 16, 64, 32
DEPTH_RUN = DEPTH
INNER = HEADS * DH
PAIRS = HEADS // 2
HID = int(D * 4 * 2 / 3)
CHUNKS = [(c, min(P, HID - c)) for c in range(0, HID, P)]
PAD = WIN + 1
SPAN = PAD + L
MASKED = -1e30
ONE = 1


def constants():
    f = np.float32
    ident = np.eye(P, dtype=f)
    i = np.arange(P)
    late = (np.arange(L)[None, :] >= i[:, None]).astype(f)
    block = (np.arange(K)[None, None, :] == 8 * np.arange(4)[None, :, None] + (i // 16)[:, None, None]).astype(f)
    spread = (np.arange(P)[None, :] // H == np.arange(K)[:, None]).astype(f)
    rep16 = (np.arange(P)[None, :] % 16 == np.arange(16)[:, None]).astype(f)
    pos = np.arange(L, dtype=f)
    dist = np.concatenate([np.tile(f(L - 1) - pos, (K - 4, 1)), np.tile(pos, (4, 1))], 0).astype(f)
    half = np.arange(0, DH, 2, dtype=f)
    inv = f(1.0) / f(10000.0) ** (half / f(DH))
    fr = (pos[:, None] * inv[None, :]).astype(f)
    fr = np.concatenate([fr, fr], -1)
    base = ((half + f(0.4 * DH)) / f(1.4 * DH)).astype(f)
    power = (pos - L // 2) / f(WIN // 2)
    sc = base[None, :] ** power[:, None]
    sc = np.concatenate([sc, sc], -1).astype(f)
    sign = np.where(np.arange(DH) < DH // 2, -1, 1).astype(f)
    cos, sin = np.cos(fr), np.sin(fr) * sign
    q = np.stack([cos * sc * 8, sin * sc * 8], 1)
    k = np.stack([cos / sc, sin / sc], 1)
    rope = np.stack([q, k], 1).reshape(TILES, P, 2, 2, DH).transpose(1, 0, 2, 3, 4)
    a, b = (i % WIN)[:, None], np.arange(2 * WIN)[None, :]
    off = (b < a) | (b > a + WIN)
    first = off | ((i < WIN)[:, None] & (b < WIN))
    mask = np.stack([np.tile(np.where(m, MASKED, 0.0), (1, 8)) for m in (first, off)], 1)
    out = dict(ident=ident, late=late, block=block.reshape(P, 4 * K), spread=spread, rep16=rep16,
               dist=dist, rope=rope.reshape(P, -1), mask=mask.reshape(P, -1))
    return {n: np.ascontiguousarray(x, f) for n, x in out.items()}


class Steps:

    def __init__(self, sem, names):
        self.sem, self.names, self.at = sem, names, 0

    def did(self, instruction, name):
        assert self.names[self.at] == name, (self.names[self.at], name)
        self.at = (self.at + 1) % len(self.names)
        instruction.then_inc(self.sem, 1)

    def count(self, rounds, name):
        return rounds * len(self.names) + self.names.index(name) + 1 + ONE


class Event:

    def __init__(self, sem, per=1):
        self.sem, self.per = sem, per

    def value(self, rounds, part=None):
        return rounds * self.per + (self.per if part is None else part + 1) + 2 * self.per


def rsqrt(dve, lanes):
    def each(op):
        for tick, x, y, h in lanes:
            tick(op(x, y, h))
        for tick, x, y, h in lanes:
            tick()

    each(lambda x, y, h: dve.tensor_scalar(y.bitcast(I32), x.bitcast(I32), 1, None, ALU.logical_shift_right))
    each(lambda x, y, h: dve.tensor_scalar(y.bitcast(I32), y.bitcast(I32), -1.0, float(0x5F3759DF), ALU.mult, ALU.add))
    for _ in range(3):
        each(lambda x, y, h: dve.scalar_tensor_tensor(out=h, in0=y, scalar=-0.5, in1=y, op0=ALU.mult, op1=ALU.mult))
        each(lambda x, y, h: dve.tensor_tensor(h, h, x, ALU.mult))
        each(lambda x, y, h: dve.scalar_tensor_tensor(out=y, in0=h, scalar=1.5, in1=y, op0=ALU.add, op1=ALU.mult))


ABS_BITS = 0x7FFFFFFF
RSQRT = 11


def state_space_layer(nc, a, XT, X1T, ident):
    with ExitStack() as ctx:
        def sb(name, shape, dt=F32):
            return ctx.enter_context(nc.sbuf_tensor("a_" + name, shape, dt))

        def sem(name):
            return ctx.enter_context(nc.semaphore("a_" + name))

        bank = [ctx.enter_context(nc.psum_tensor(f"a_bank{i}", [P, 512], F32)) for i in range(8)]
        xin, xtok = sb("xin", [P, B, L]), sb("xtok", [P, B, TILES, D])
        w_in, w_out = sb("w_in", [P, TOTAL]), sb("w_out", [P, D])
        taps, bias = sb("taps", [P, 3, TAPS]), sb("bias", [P, 3])
        theta, logit = sb("theta", [P, P, M]), sb("logit", [P, 3])
        top, weights, total = sb("top", [P, 1]), sb("weights", [P, 3]), sb("total", [P, 1])
        slope, sscale = sb("slope", [K, 1]), sb("sscale", [K, 1])
        soft = sb("soft", [K, 10])
        w16, nscale, wrep = sb("w16", [16, 8]), sb("nscale", [16, 2]), sb("wrep", [P, 8])
        late, block = sb("late", [P, L]), sb("block", [P, 4 * K])
        spread, rep16 = sb("spread", [K, P]), sb("rep16", [16, P])
        time_w = sb("time_w", [K, L])
        w_blk, sum_blk = sb("w_blk", [P, 8, P]), sb("sum_blk", [P, 4, P])
        magic, quarter, eps = sb("magic", [P, 1]), sb("quarter", [P, 1]), sb("eps", [P, 1])
        ones = sb("ones", [P, L])
        z, conv, gate = sb("z", [P, 3, TAPS - 1 + L]), sb("conv", [P, 3, L]), sb("gate", [P, L])
        pw, poly, den = sb("pw", [K, L]), sb("poly", [P, L]), sb("den", [P, L])
        g_tok = sb("g_tok", [P, TILES, P])
        whole, turn, turn_abs = (sb(n, [P, 2, 512]) for n in ("whole", "turn", "turn_abs"))
        sin, cos = sb("sin", [P, 2, 512]), sb("cos", [P, 2, 512])
        moments = sb("moments", [P, TILES, 2 * 512])
        num, sq = sb("num", [P, 2, L]), sb("sq", [P, 2, L])
        ms, yg = sb("ms", [P, L]), sb("yg", [P, L])
        res, res_n = sb("res", [P, TILES, D]), sb("res_n", [P, TILES, D])
        stats, mv, dev = sb("stats", [P, TILES, 6]), sb("mv", [P, TILES, 2]), sb("dev", [P, TILES])
        pause = sb("pause", [P, 1])

        loaded = sem("loaded")
        vector_ready, scalar_ready, spread_ready = sem("vector_ready"), sem("scalar_ready"), sem("spread_ready")
        setup_done, vector_own = sem("setup_done"), sem("vector_own")
        pe_s = Steps(sem("tensor_step"), ["z2", "z0", "z1", "spread", "g turned"]
                     + [f"phase{t}" for t in range(TILES)]
                     + ["cumulated0"] + [f"{n}" for c in range(1, 8) for n in (f"cumulated{c}", f"contracted{c - 1}")]
                     + ["contracted7", "out", "turned"])
        act_s = Steps(sem("scalar_step"), ["z2", "z0", "z1", "p", "silu", "g turned"]
                      + [f"{n}{t}" for t in range(TILES) for n in ("magic", "sin", "cos")]
                      + [f"square{c}" for c in range(8)] + ["rms", "deviation", "stored", "kept"])
        dve_s = Steps(sem("vector_step"), [f"conv2{j}" for j in range(TAPS)] + ["clip low", "clip"]
                      + [f"conv{c}{j}" for c in (0, 1) for j in range(TAPS)]
                      + ["weight", "poly1", "poly2", "g", "den"]
                      + [f"{n}{t}" for t in range(TILES) for n in ("turn", "turn_abs", "re", "im")]
                      + [f"num{c}" for c in range(8)]
                      + ["den floor", "inv den", "ms1", "ms2", "ms3", "inv rms", "factor", "y", "yg",
                         "residual"] + [f"stats{t}" for t in range(TILES)]
                      + [f"mean{t}" for t in range(TILES)] + ["inv dev"] + [f"norm{t}" for t in range(TILES)])
        col = lambda x: x.rearrange("(p o) -> p o", o=1)
        loads = [(xin[:, :, :], a["xT"]), (w_in[:, :], a["W_in"]), (w_out[:, :], a["W_out"]),
                 (taps[:, 0:2, :], a["w_conv"][0:2 * P, :].rearrange("(c p) j -> p c j", p=P)),
                 (taps[0:K, 2, :], a["w_conv"][2 * P:TOTAL, :]),
                 (bias[:, 0:1], col(a["b_conv"][0:P])), (bias[:, 1:2], col(a["b_conv"][P:2 * P])),
                 (bias[0:K, 2:3], col(a["b_conv"][2 * P:TOTAL])),
                 (theta[:, :, :], a["theta"].rearrange("p (c m) -> p c m", m=M)), (logit[:, :], a["logits"]),
                 (slope[:, :], col(a["slopes"])), (sscale[:, :], col(a["score_scale"])),
                 (w16[:, 0:4], a["W_re"]), (w16[:, 4:8], a["W_im"]),
                 (nscale[:, 0:1], col(a["norm_scale"][0:16])), (nscale[:, 1:2], col(a["norm_scale"][16:32])),
                 (late[:, :], a["late"]), (block[:, :], a["block"]), (spread[:, :], a["spread"]),
                 (rep16[:, :], a["rep16"]), (time_w[:, :], a["dist"]), (ident[:, :], a["ident"])]
        loads += [(xtok[:, s, :, :], a["x"][s].rearrange("(t p) d -> p t d", p=P)) for s in range(B)]

        blk = ctx.enter_context(nc.Block())

        @blk.sync
        def _(sp):
            for dst, src in loads:
                sp.dma_start(dst, src).then_inc(loaded, 16)

        @blk.vector
        def _(dve):
            dve.sem_inc(dve_s.sem, ONE)
            own = [0]

            def tick(instruction):
                own[0] += 1
                instruction.then_inc(vector_own, 1)
                dve.wait_ge(vector_own, own[0])

            for buf, v in ((ones, 1.0), (magic, MAGIC), (quarter, 1.5707963267948966), (eps, LN_EPS)):
                dve.memset(buf[:, :], v)
            dve.memset(z[:, :, 0:TAPS - 1], 0.0)
            tick(dve.memset(XT[:, :, 0:PAD], 0.0))
            dve.wait_ge(loaded, 16 * len(loads))
            tick(dve.tensor_reduce(top[:, :], logit[:, :], AX.X, ALU.max))
            dve.tensor_scalar(logit[:, :], logit[:, :], top[:, 0:1], None, ALU.subtract).then_inc(vector_ready, 1)
            dve.tensor_scalar(soft[:, 0:1].bitcast(I32), slope[:, :].bitcast(I32), ABS_BITS, None, ALU.bitwise_and).then_inc(vector_ready, 1)
            dve.wait_ge(scalar_ready, 2)
            tick(dve.tensor_reduce(total[:, :], logit[:, :], AX.X, ALU.add))
            tick(dve.reciprocal(total[:, :], total[:, :]))
            tick(dve.tensor_scalar(weights[:, :], logit[:, :], total[:, 0:1], None, ALU.mult))
            dve.tensor_scalar(soft[:, 2:3], soft[:, 1:2], 1.0, None, ALU.add).then_inc(vector_ready, 1)
            dve.wait_ge(vector_ready, 3)
            tick(dve.tensor_scalar(soft[:, 3:4], soft[:, 2:3], 1.0, None, ALU.subtract))
            tick(dve.tensor_tensor(soft[:, 4:5], soft[:, 1:2], soft[:, 3:4], ALU.subtract))
            tick(dve.reciprocal(soft[:, 5:6], soft[:, 2:3]))
            dve.wait_ge(scalar_ready, 3)
            tick(dve.scalar_tensor_tensor(out=soft[:, 7:8], in0=soft[:, 4:5], scalar=soft[:, 5:6],
                                          in1=soft[:, 6:7], op0=ALU.mult, op1=ALU.add))
            tick(dve.scalar_tensor_tensor(out=soft[:, 8:9], in0=slope[:, :], scalar=0.0,
                                          in1=soft[:, 7:8], op0=ALU.max, op1=ALU.add))
            dve.tensor_scalar(time_w[:, :], time_w[:, :], soft[:, 8:9], None, ALU.mult).then_inc(vector_ready, 1)
            dve.tensor_scalar(w16[:, 0:4], w16[:, 0:4], nscale[:, 0:1], None, ALU.mult)
            dve.tensor_scalar(w16[:, 4:8], w16[:, 4:8], nscale[:, 1:2], None, ALU.mult).then_inc(vector_ready, 1)
            tick(dve.scalar_tensor_tensor(out=theta[:, :, :], in0=theta[:, :, :], scalar=TURN,
                                          in1=ident[:, :].unsqueeze(2).to_broadcast([P, P, M]),
                                          op0=ALU.mult, op1=ALU.mult))
            blocks = block[:, :].unsqueeze(2).to_broadcast([P, 4 * K, H])
            tick(dve.tensor_copy(sum_blk[:, :, :].rearrange("p c (k h) -> p (c k) h", h=H), blocks))
            dve.wait_ge(spread_ready, 1)
            tick(dve.tensor_copy(wrep[:, :], bank[0][:, 0:8]))
            for i in range(2):
                tick(dve.tensor_tensor(w_blk[:, 4 * i:4 * i + 4, :].rearrange("p c (k h) -> p (c k) h", h=H), blocks,
                                       wrep[:, 4 * i:4 * i + 4].unsqueeze(1).to_broadcast([P, 4 * K, H]), ALU.mult))
            tick(dve.tensor_scalar(top[:, :], weights[:, 2:3], -1.0, None, ALU.mult))
            dve.sem_inc(setup_done, 1)

            with dve.Fori(0, B) as s:
                def after(steps, name):
                    dve.wait_ge(steps.sem, steps.count(s, name))

                def step(instruction, name, wait=True):
                    dve_s.did(instruction, name)
                    if wait:
                        after(dve_s, name)

                for c in (2, 0, 1):
                    w = K if c == 2 else P
                    after(act_s, f"z{c}")
                    step(dve.tensor_scalar(conv[0:w, c, :], z[0:w, c, 0:L], taps[0:w, c, 0:1], bias[0:w, c:c + 1],
                                           ALU.mult, ALU.add), f"conv{c}0")
                    for j in range(1, TAPS):
                        step(dve.scalar_tensor_tensor(out=conv[0:w, c, :], in0=z[0:w, c, j:j + L],
                                                      scalar=taps[0:w, c, j:j + 1], in1=conv[0:w, c, :],
                                                      op0=ALU.mult, op1=ALU.add), f"conv{c}{j}")
                    if c == 2:
                        step(dve.tensor_scalar(conv[0:K, 2, :], conv[0:K, 2, :], sscale[:, 0:1], -20.0,
                                               ALU.mult, ALU.max), "clip low")
                        step(dve.tensor_scalar(conv[0:K, 2, :], conv[0:K, 2, :], 20.0, None, ALU.min), "clip", False)
                after(act_s, "p")
                step(dve.tensor_tensor(pw[:, :], conv[0:K, 2, :], time_w[:, :], ALU.mult), "weight", False)
                step(dve.tensor_scalar(poly[:, :], conv[:, 0, :], top[:, 0:1], weights[:, 1:2], ALU.mult, ALU.add), "poly1")
                step(dve.tensor_tensor(poly[:, :], poly[:, :], conv[:, 0, :], ALU.mult), "poly2")
                after(pe_s, "spread")
                step(dve.scalar_tensor_tensor(out=poly[:, :], in0=poly[:, :], scalar=weights[:, 0:1], in1=bank[3][:, :],
                                              op0=ALU.add, op1=ALU.mult), "g", False)
                step(dve.tensor_tensor_scan(den[:, :], ones[:, :], bank[3][:, :], 0.0, ALU.mult, ALU.add), "den", False)
                for t in range(TILES):
                    i = t % 2
                    after(act_s, f"magic{t}")
                    step(dve.scalar_tensor_tensor(out=turn[:, i, :], in0=whole[:, i, :], scalar=MAGIC,
                                                  in1=bank[4 + i][:, :], op0=ALU.subtract, op1=ALU.subtract), f"turn{t}")
                    step(dve.tensor_scalar(turn_abs[:, i, :].bitcast(I32), turn[:, i, :].bitcast(I32), ABS_BITS, None,
                                           ALU.bitwise_and), f"turn_abs{t}", False)
                    amp = g_tok[:, t, :].unsqueeze(2).to_broadcast([P, P, M])
                    after(act_s, f"cos{t}")
                    for n, (part, trig) in enumerate((("re", cos), ("im", sin))):
                        step(dve.tensor_tensor(moments[:, t, 512 * n:512 * n + 512].rearrange("p (c m) -> p c m", m=M),
                                               trig[:, i, :].rearrange("p (c m) -> p c m", m=M), amp, ALU.mult),
                             f"{part}{t}", False)
                for c in range(8):
                    after(pe_s, f"cumulated{c}")
                    if c >= 2:
                        after(pe_s, f"contracted{c - 2}")
                    step(dve.tensor_copy(num[:, c % 2, :], bank[c % 2][:, :]), f"num{c}", False)
                step(dve.tensor_scalar(den[:, :], den[:, :], 1e-4, None, ALU.max), "den floor")
                step(dve.reciprocal(den[:, :], den[:, :]), "inv den")
                after(pe_s, "contracted7")
                step(dve.tensor_tensor(ms[:, :], bank[2][:, :], den[:, :], ALU.mult), "ms1")
                step(dve.tensor_tensor(ms[:, :], ms[:, :], den[:, :], ALU.mult), "ms2")
                step(dve.tensor_scalar(ms[:, :], ms[:, :], 1.0 / (2 * H * M), 1e-5, ALU.mult, ALU.add), "ms3", False)
                after(act_s, "rms")
                step(dve.reciprocal(ms[:, :], ms[:, :]), "inv rms")
                step(dve.tensor_tensor(ms[:, :], ms[:, :], den[:, :], ALU.mult), "factor")
                step(dve.tensor_tensor(yg[:, :], bank[7][:, :], ms[:, :], ALU.mult), "y")
                step(dve.tensor_tensor(yg[:, :], yg[:, :], gate[:, :], ALU.mult), "yg", False)
                after(pe_s, "out")
                step(dve.tensor_tensor(res[:, :, :].rearrange("p t d -> p (t d)"), bank[3][:, :],
                                       xtok[:, bass.ds(s, 1), :, :].rearrange("p o t d -> p (o t d)"), ALU.add), "residual")
                for t in range(TILES):
                    step(dve.bn_stats(stats[:, t, :], res[:, t, :]), f"stats{t}", t == TILES - 1)
                dve.memset(pause[:, :], 0.0)
                for t in range(TILES):
                    step(dve.bn_aggr(mv[:, t, :], stats[:, t, :]), f"mean{t}", False)
                after(act_s, "deviation")
                step(dve.reciprocal(dev[:, :], dev[:, :]), "inv dev")
                for t in range(TILES):
                    step(dve.tensor_scalar(res_n[:, t, :], res[:, t, :], mv[:, t, 0:1], dev[:, t:t + 1],
                                           ALU.subtract, ALU.mult), f"norm{t}", False)

        @blk.scalar
        def _(act):
            act.sem_inc(act_s.sem, ONE)
            act.wait_ge(vector_ready, 1)
            act.activation(logit[:, :], logit[:, :], ACT.Exp).then_inc(scalar_ready, 1)
            act.wait_ge(vector_ready, 2)
            act.activation(soft[:, 1:2], soft[:, 0:1], ACT.Exp, scale=-1.0).then_inc(scalar_ready, 1)
            act.wait_ge(vector_ready, 3)
            act.activation(soft[:, 6:7], soft[:, 2:3], ACT.Ln).then_inc(scalar_ready, 1)
            act.wait_ge(vector_ready, 4)
            act.activation(time_w[:, :], time_w[:, :], ACT.Exp, scale=-1.0).then_inc(scalar_ready, 1)
            act.wait_ge(setup_done, 1)

            with act.Fori(0, B) as s:
                def after(steps, name):
                    act.wait_ge(steps.sem, steps.count(s, name))

                for c in (2, 0, 1):
                    w = K if c == 2 else P
                    after(pe_s, f"z{c}")
                    act_s.did(act.activation(z[0:w, c, TAPS - 1:], bank[c][0:w, :], ACT.Identity), f"z{c}")
                after(dve_s, "clip")
                act_s.did(act.activation(conv[0:K, 2, :], conv[0:K, 2, :], ACT.Exp), "p")
                after(dve_s, f"conv1{TAPS - 1}")
                act_s.did(act.activation(gate[:, :], conv[:, 1, :], ACT.Silu), "silu")
                after(pe_s, "g turned")
                act_s.did(act.activation(g_tok[:, :, :].rearrange("p t c -> p (t c)"), bank[6][:, :], ACT.Identity), "g turned")
                for t in range(TILES):
                    i = t % 2
                    after(pe_s, f"phase{t}")
                    if t >= 2:
                        after(dve_s, f"turn{t - 2}")
                    act_s.did(act.activation(whole[:, i, :], bank[4 + i][:, :], ACT.Identity, bias=magic[:, 0:1]), f"magic{t}")
                    after(dve_s, f"turn_abs{t}")
                    if t >= 2:
                        after(dve_s, f"im{t - 2}")
                    act_s.did(act.activation(sin[:, i, :], turn[:, i, :], ACT.Sin, scale=-TWO_PI), f"sin{t}")
                    act_s.did(act.activation(cos[:, i, :], turn_abs[:, i, :], ACT.Sin, scale=-TWO_PI, bias=quarter[:, 0:1]), f"cos{t}")
                for c in range(8):
                    after(dve_s, f"num{c}")
                    if c >= 2:
                        after(pe_s, f"contracted{c - 2}")
                    act_s.did(act.activation(sq[:, c % 2, :], num[:, c % 2, :], ACT.Square), f"square{c}")
                after(dve_s, "ms3")
                act_s.did(act.activation(ms[:, :], ms[:, :], ACT.Sqrt), "rms")
                after(dve_s, f"mean{TILES - 1}")
                act_s.did(act.activation(dev[:, :], mv[:, :, 1], ACT.Sqrt, bias=eps[:, 0:1]), "deviation")
                after(pe_s, "turned")
                act_s.did(act.activation(XT[:, bass.ds(s, 1), PAD:].rearrange("p o t -> p (o t)"), bank[6][:, :], ACT.Identity), "stored")
                act_s.did(act.activation(X1T[:, bass.ds(s, 1), :].rearrange("p o t -> p (o t)"), bank[6][:, :], ACT.Identity), "kept")
            act.wait_ge(act_s.sem, act_s.count(B - 1, "kept"))

        @blk.tensor
        def _(pe):
            pe.sem_inc(pe_s.sem, ONE)
            pe.wait_ge(loaded, 16 * len(loads))
            pe.wait_ge(vector_ready, 5)
            pe.matmul(bank[0][:, 0:8], rep16[:, :], w16[:, :], start=True, stop=True).then_inc(spread_ready, 1)
            pe.wait_ge(setup_done, 1)
            with pe.Fori(0, B) as s:
                def after(steps, name):
                    pe.wait_ge(steps.sem, steps.count(s, name))

                pe.wait_ge(act_s.sem, act_s.count(s, "kept") - len(act_s.names))
                for c in (2, 0, 1):
                    w = K if c == 2 else P
                    pe_s.did(pe.matmul(bank[c][0:w, :], w_in[:, P * c:P * c + w],
                                       xin[:, bass.ds(s, 1), :].rearrange("p o t -> p (o t)"), start=True, stop=True), f"z{c}")
                after(dve_s, "weight")
                pe_s.did(pe.matmul(bank[3][:, :], spread[:, :], pw[:, :], start=True, stop=True), "spread")
                after(dve_s, "g")
                for t in range(TILES):
                    mm = pe.transpose(bank[6][:, P * t:P * t + P], poly[:, P * t:P * t + P], ident[:, :])
                pe_s.did(mm, "g turned")
                for t in range(TILES):
                    if t >= 2:
                        after(dve_s, f"turn{t - 2}")
                    pe_s.did(pe.matmul(bank[4 + t % 2][:, :], conv[:, 0, P * t:P * t + P],
                                       theta[:, :, :].rearrange("p c m -> p (c m)"), start=True, stop=True), f"phase{t}")
                after(dve_s, f"im{TILES - 1}")

                def contract(c):
                    after(act_s, f"square{c}")
                    pe.matmul(bank[7][:, :], w_blk[:, c, :], num[:, c % 2, :], start=(c == 0), stop=(c == 7))
                    pe_s.did(pe.matmul(bank[2][:, :], sum_blk[:, c % 4, :], sq[:, c % 2, :],
                                       start=(c == 0), stop=(c == 7)), f"contracted{c}")

                for c in range(8):
                    if c >= 2:
                        after(dve_s, f"num{c - 2}")
                    for t in range(TILES):
                        mm = pe.matmul(bank[c % 2][:, P * t:L], moments[:, t, P * c:P * c + P], late[:, 0:L - P * t],
                                       start=(t == 0), stop=(t == TILES - 1))
                    pe_s.did(mm, f"cumulated{c}")
                    if c >= 1:
                        contract(c - 1)
                contract(7)
                after(dve_s, "yg")
                for t in range(TILES):
                    mm = pe.matmul(bank[3][:, P * t:P * t + P], yg[:, P * t:P * t + P], w_out[:, :], start=True, stop=True)
                pe_s.did(mm, "out")
                after(dve_s, f"norm{TILES - 1}")
                for t in range(TILES):
                    mm = pe.transpose(bank[6][:, P * t:P * t + P], res_n[:, t, :], ident[:, :])
                pe_s.did(mm, "turned")


def attention_layers(nc, a, XT, ident):
    with ExitStack() as ctx:
        def sb(name, shape, dt=F32):
            return ctx.enter_context(nc.sbuf_tensor("b_" + name, shape, dt))

        def event(name, per=1):
            return Event(ctx.enter_context(nc.semaphore("b_" + name)), per)

        proj = [ctx.enter_context(nc.psum_tensor(f"b_proj{i}", [P, 512], F32)) for i in range(2)]
        scores = ctx.enter_context(nc.psum_tensor("b_scores", [P, 2, 512], F32))
        turned = [ctx.enter_context(nc.psum_tensor(f"b_turned{i}", [P, 4, P], F32)) for i in range(2)]
        mix = ctx.enter_context(nc.psum_tensor("b_mix", [P, 2, 512], F32))

        wqk = sb("wqk", [P, 2 * INNER])
        w_hi, w_lo = sb("w_hi", [P, 2 * INNER], F32R), sb("w_lo", [P, 2 * INNER], F32R)
        wvT, wo = sb("wvT", [DH, HEADS, D]), sb("wo", [DH, HEADS, D])
        wvo = sb("wvo", [P, HEADS, D])
        w1, w2 = sb("w1", [P, 2 * HID]), sb("w2", [P, len(CHUNKS), D])
        vectors, vec = sb("vectors", [P, DEPTH, 9]), sb("vec", [P, 9])
        B1, B1_GATE, LN_G, LN_B, B2 = 0, 3, 6, 7, 8
        rope, qk_scale = sb("rope", [P, TILES, 2, 2, DH]), sb("qk_scale", [P, 2, 2, DH])
        table = sb("table", [P, TILES, 2, 2, DH])
        mask = sb("mask", [P, 2, 512], BF16)
        ident16 = sb("ident16", [P, P], BF16)
        xs = sb("xs", [P, 2, WIN + P])
        doubled = sb("doubled", [P, 2, TILES, 2, 2 * WIN])
        x_hi, x_lo = sb("x_hi", [P, 2, P], F32R), sb("x_lo", [P, 2, P], F32R)
        keys = sb("keys", [P, TILES, TILES, D])
        raw, sq = sb("raw", [P, 4, 512]), sb("sq", [P, 4, 512])
        qk, other = sb("qk", [P, 2, 4, 512]), sb("other", [P, 4, 512])
        ss, inv, half = sb("ss", [P, 32]), sb("inv", [P, 2, 32]), sb("half", [P, 32])
        qT, kT = sb("qT", [P, PAIRS, P]), sb("kT", [P, 2, PAIRS, 2, WIN + P])
        top, total = sb("top", [P, HEADS]), sb("total", [P, HEADS])
        prob, probT = sb("prob", [P, HEADS, 2 * WIN]), sb("probT", [P, PAIRS, P])
        y = sb("y", [P, PAIRS, 2, P])
        xf, xn, xnT = sb("xf", [P, L]), sb("xn", [P, TILES, D]), sb("xnT", [P, L])
        hid = sb("hid", [P, 3, L])
        mask32 = hid[:, 0:2, :]
        stats, mv = sb("stats", [P, TILES, 6]), sb("mv", [P, TILES, 2])
        pool_pause = sb("pool_pause", [P, 1])
        var, dev, dev_half, pause = sb("var", [P, TILES]), sb("dev", [P, TILES]), sb("dev_half", [P, TILES]), sb("pause", [P, 1])

        fixed_loaded, qkv_loaded, scale_loaded = event("fixed_loaded"), event("qkv_loaded"), event("scale_loaded")
        wvo_loaded, ffn_loaded = event("wvo_loaded"), event("ffn_loaded")
        fixed_made, tables_made, vec_made = event("fixed_made", 3), event("tables_made"), event("vec_made")
        weights_split = event("weights_split", 8)
        wvo_made, wvo_placed = event("wvo_made", 4), event("wvo_placed", 4)
        staged = event("staged", 2)
        low_staged = event("low_staged")
        tokens_doubled = event("tokens_doubled")
        qk_projected = event("qk_projected", 4)
        copied, squared = event("copied", 4), event("squared", 4)
        rotated = event("rotated", 4)
        squares_summed = event("squares_summed", 4)
        norm_step = event("norm_step", RSQRT + 1)
        rope_summed, normed = event("rope_summed", 4), event("normed", 4)
        qk_turned, qk_placed = event("qk_turned", 4), event("qk_placed", 4)
        carried = event("carried")
        scored = event("scored", 2)
        top_found, subtracted = event("top_found", 2), event("subtracted", 2)
        exped = event("exped", 2)
        totalled, inverted, weighed = event("totalled", 2), event("inverted"), event("weighed", 2)
        p_turned, p_placed = event("p_turned", 2), event("p_placed", 2)
        keys_turned, keys_placed = event("keys_turned"), event("keys_placed")
        mixed, placed = event("mixed", 4), event("placed", 4)
        attn_projected, attn_added = event("attn_projected"), event("attn_added")
        f_staged, f_turned, f_copied = event("f_staged"), event("f_turned"), event("f_copied")
        f_norm_step, f_normed = event("f_norm_step", 3 + RSQRT), event("f_normed")
        f_back, f_scaled = event("f_back"), event("f_scaled")
        f_gate, f_value = event("f_gate", 3), event("f_value", 3)
        gated, hidden = event("gated", 3), event("hidden", 3)
        f_out, f_added = event("f_out"), event("f_added")

        def wait(engine, ev, rounds, part=None):
            engine.wait_ge(ev.sem, ev.value(rounds, part))

        def lags(t, prev, new):
            return new, (new or t < 1) and (prev or t >= 1), (new or t < 2) and (prev or t >= 2)

        def rounds(engine, body):
            body(0, 0, 0, None, True, True)
            if DEPTH_RUN > 1:
                with engine.Fori(0, DEPTH_RUN - 1) as layer:
                    with engine.Fori(1, B) as s:
                        body(layer, layer * B + s, s, s - 1, False, True)
                    body(layer + 1, layer * B + B, 0, B - 1, True, True)
            with engine.Fori(1, B) as s:
                body(DEPTH_RUN - 1, (DEPTH_RUN - 1) * B + s, s, s - 1, False, True)
            body(DEPTH_RUN - 1, DEPTH_RUN * B, None, B - 1, False, False)

        def at_slot(x, s):
            return XT[x, s, :] if isinstance(s, int) else XT[x, bass.ds(s, 1), :].rearrange("p o t -> p (o t)")

        b1 = a["b1"]
        fixed = [(rope[:, :, :, :, :].rearrange("p t q c d -> p (t q c d)"), a["rope"]),
                 (mask32[:, :, :].rearrange("p n c -> p (n c)"), a["mask"]),
                 (vectors[:, :, LN_G], a["ln_g"]), (vectors[:, :, LN_B], a["ln_b"]), (vectors[:, :, B2], a["b2"])]
        for c, (c0, rows) in enumerate(CHUNKS):
            for col, at in ((B1, c0), (B1_GATE, HID + c0)):
                fixed.append((vectors[0:rows, :, col + c], b1[:, at:at + rows].rearrange("l p -> p l")))

        blk = ctx.enter_context(nc.Block())

        @blk.sync
        def _(sp):
            wait(sp, fixed_made, 0, 0)
            with nc.allow_non_contiguous_dma(reason="small per-channel vectors"):
                for dst, src in fixed:
                    sp.dma_start(dst, src).then_inc(fixed_loaded.sem, 16)
            with sp.Fori(0, DEPTH_RUN) as layer:
                one = lambda x: x[bass.ds(layer, 1)]
                wait(sp, weights_split, layer - 1)
                sp.dma_start(wqk[:, :], a["Wqkv"][bass.ds(layer, 1), :, 0:2 * INNER].rearrange("o p n -> p (o n)")).then_inc(qkv_loaded.sem, 16)
                wait(sp, tables_made, layer - 1)
                sp.dma_start(qk_scale[:, :, :, :].rearrange("p q c d -> p (q c d)"),
                             one(a["qk_scale"]).rearrange("o p n -> p (o n)")).then_inc(scale_loaded.sem, 16)
                wait(sp, wvo_made, layer - 1)
                sp.dma_start(wvT[:, :, :], one(a["WvT"]).rearrange("o p h n -> p (o h) n")).then_inc(wvo_loaded.sem, 16)
                sp.dma_start(wo[:, :, :], one(a["Wo"]).rearrange("o (h p) n -> p (o h) n", p=DH)).then_inc(wvo_loaded.sem, 16)
                wait(sp, f_out, layer * B - 1)
                sp.dma_start(w1[:, :], one(a["W1"]).rearrange("o p n -> p (o n)")).then_inc(ffn_loaded.sem, 16)
                sp.dma_start(w2[:, 0:2, :], a["W2"][bass.ds(layer, 1), 0:2 * P].rearrange("o (c p) n -> p (o c) n", p=P)).then_inc(ffn_loaded.sem, 16)
                sp.dma_start(w2[0:CHUNKS[2][1], 2, :], a["W2"][bass.ds(layer, 1), 2 * P:HID].rearrange("o p n -> p (o n)")).then_inc(ffn_loaded.sem, 16)

        @blk.vector
        def _(dve):
            credit = (rotated, squares_summed, norm_step, top_found, subtracted, totalled, inverted, weighed,
                      attn_added, f_staged, f_norm_step, f_normed, hidden, f_added, tables_made, vec_made, fixed_made,
                      weights_split)
            for ev in credit:
                dve.sem_inc(ev.sem, 2 * ev.per)
            dve.memset(vectors[:, :, :], 0.0).then_inc(fixed_made.sem, 1)
            dve.memset(kT[:, 0, :, :, :].rearrange("p c n t -> p (c n t)"), 0.0)
            dve.memset(kT[:, 1, :, :, :].rearrange("p c n t -> p (c n t)"), 0.0).then_inc(fixed_made.sem, 1)
            dve.wait_ge(fixed_loaded.sem, 16 * len(fixed))
            dve.tensor_copy(ident16[:, :], ident[:, :])
            dve.tensor_copy(mask[:, :, :], mask32[:, :, :]).then_inc(fixed_made.sem, 1)

            def make_vec(layer):
                rd = layer * B - 1
                for ev in (hidden, f_scaled, gated, f_added):
                    wait(dve, ev, rd)
                src = vectors[:, layer, :] if isinstance(layer, int) else vectors[:, bass.ds(layer, 1), :].rearrange("p o c -> p (o c)")
                dve.tensor_copy(vec[:, :], src).then_inc(vec_made.sem, 1)
                wait(dve, vec_made, layer)

            def body(layer, it, s, before, first, new):
                prev = before is not None

                if first:
                    dve.wait_ge(qkv_loaded.sem, layer * 16 + 16)
                    wait(dve, qk_projected, it * TILES - 1)
                    for j in range(4):
                        cols = slice(512 * j, 512 * j + 512)
                        dve.tensor_copy(w_hi[:, cols], wqk[:, cols]).then_inc(weights_split.sem, 1)
                        wait(dve, weights_split, layer, 2 * j)
                        dve.tensor_tensor(w_lo[:, cols], wqk[:, cols], w_hi[:, cols].bitcast(F32), ALU.subtract).then_inc(weights_split.sem, 1)
                    dve.wait_ge(scale_loaded.sem, layer * 16 + 16)
                    wait(dve, rotated, it * TILES - 1)
                    for q in range(2):
                        for c in range(2):
                            tb = dve.tensor_tensor(table[:, :, q, c, :], rope[:, :, q, c, :],
                                                   qk_scale[:, q, c, :].unsqueeze(1).to_broadcast([P, TILES, DH]), ALU.mult)
                    tb.then_inc(tables_made.sem, 1)
                    wait(dve, tables_made, layer)
                    if not prev:
                        make_vec(layer)
                for t in range(TILES):
                    cur, l1, l2 = lags(t, prev, new)
                    n = it * TILES + t
                    i = t % 2
                    if (new or t < 3) and (prev or t >= 3):
                        wait(dve, attn_projected, n - 3)
                        at = PAD + P * ((t - 3) % TILES)
                        x = at_slot(slice(0, P), s if t >= 3 else before)[:, at:at + P]
                        dve.tensor_tensor(x, x, mix[:, 0, 0:P], ALU.add).then_inc(attn_added.sem, 1)
                    if prev and t == 2:
                        wait(dve, attn_added, it * TILES - 1)
                        for h in range(2):
                            ch = slice(DH * h, DH * h + DH)
                            cp = dve.tensor_copy(xf[ch, :], at_slot(ch, before)[:, PAD - h:PAD - h + L])
                        cp.then_inc(f_staged.sem, 1)
                    if cur:
                        wait(dve, qk_turned, n - 2)
                        for j in range(4):
                            kind = j // 2
                            wait(dve, copied, n, j)
                            heads = raw[:, j, :].rearrange("p (h c d) -> p h c d", c=2, d=DH // 2)
                            cos = table[:, t, kind, 0, :].rearrange("p (c d) -> p c d", c=2).unsqueeze(1).to_broadcast([P, 8, 2, DH // 2])
                            sin = table[:, t, kind, 1, :].rearrange("p (c d) -> p c d", c=2).unsqueeze(1).to_broadcast([P, 8, 2, DH // 2])
                            dve.tensor_tensor(qk[:, i, j, :].rearrange("p (h c d) -> p h c d", c=2, d=DH // 2), heads, cos, ALU.mult)
                            wait(dve, rope_summed, n - 1, j)
                            dve.tensor_tensor(other[:, j, :].rearrange("p (h c d) -> p h c d", c=2, d=DH // 2),
                                              heads[:, :, ::-1, :], sin, ALU.mult).then_inc(rotated.sem, 1)
                        for j in range(4):
                            wait(dve, squared, n, j)
                            dve.tensor_reduce(ss[:, 8 * j:8 * j + 8], sq[:, j, :].rearrange("p (h d) -> p h d", d=DH),
                                              AX.X, ALU.add).then_inc(squares_summed.sem, 1)
                        wait(dve, squares_summed, n)
                        wait(dve, normed, n - 2)

                    def ticker(ev, rounds):
                        done = [0]

                        def tick(ins=None):
                            if ins is None:
                                wait(dve, ev, rounds, done[0] - 1)
                            else:
                                ins.then_inc(ev.sem, 1)
                                done[0] += 1

                        return tick

                    tick, f_tick = ticker(norm_step, n), ticker(f_norm_step, it - 1)
                    lanes = []
                    if prev and t == 3:
                        wait(dve, f_copied, it - 1)
                        for k in range(TILES):
                            st = dve.bn_stats(stats[:, k, :], xn[:, k, :])
                        f_tick(st)
                        lanes.append((f_tick, var[:, :], dev[:, :], dev_half[:, :]))
                    if cur:
                        tick(dve.tensor_scalar(ss[:, :], ss[:, :], 1e-24, None, ALU.max))
                        lanes.append((tick, ss[:, :], inv[:, i, :], half[:, :]))
                    if prev and t == 3:
                        f_tick()
                        dve.memset(pause[:, :], 0.0)
                        for k in range(TILES):
                            st = dve.bn_aggr(mv[:, k, :], stats[:, k, :])
                        f_tick(st)
                        f_tick()
                        f_tick(dve.tensor_scalar(var[:, :], mv[:, :, 1], LN_EPS, None, ALU.add))
                    for lane in lanes:
                        lane[0]()
                    if lanes:
                        rsqrt(dve, lanes)
                    if prev and t == 3:
                        for k in range(TILES):
                            st = dve.tensor_scalar(xn[:, k, :], xn[:, k, :], mv[:, k, 0:1], dev[:, k:k + 1], ALU.subtract, ALU.mult)
                        st.then_inc(f_normed.sem, 1)

                    def hide(c):
                        rows = CHUNKS[c][1]
                        wait(dve, gated, it - 1, c)
                        wait(dve, f_value, it - 1, c)
                        dve.scalar_tensor_tensor(out=hid[0:rows, c, :], in0=proj[0][0:rows, :], scalar=vec[0:rows, B1 + c:B1 + c + 1],
                                                 in1=hid[0:rows, c, :], op0=ALU.add, op1=ALU.mult).then_inc(hidden.sem, 1)

                    if l1:
                        half_heads = lambda x, j: x[:, 8 * j:8 * j + 8]
                        wide = lambda x, j: half_heads(x, j).unsqueeze(2).to_broadcast([P, 8, 2 * WIN])
                        s3 = [scores[:, j, :].rearrange("p (h k) -> p h k", k=2 * WIN) for j in range(2)]
                        for j in range(2):
                            wait(dve, scored, n - 1, j)
                            dve.tensor_reduce(half_heads(top, j), s3[j], AX.X, ALU.max).then_inc(top_found.sem, 1)
                        for j in range(2):
                            wait(dve, top_found, n - 1, j)
                            wait(dve, p_turned, n - 2)
                            dve.tensor_tensor(half_heads(prob, j), s3[j], wide(top, j), ALU.subtract).then_inc(subtracted.sem, 1)
                    if l1:
                        for j in range(2):
                            wait(dve, exped, n - 1, j)
                            dve.tensor_reduce(half_heads(total, j), half_heads(prob, j), AX.X, ALU.add).then_inc(totalled.sem, 1)
                        wait(dve, totalled, n - 1)
                        dve.reciprocal(total[:, :], total[:, :]).then_inc(inverted.sem, 1)
                        wait(dve, inverted, n - 1)
                        for j in range(2):
                            dve.tensor_tensor(half_heads(prob, j), half_heads(prob, j), wide(total, j), ALU.mult).then_inc(weighed.sem, 1)
                    if prev and t == 3:
                        for c in range(len(CHUNKS)):
                            hide(c)
                        wait(dve, f_out, it - 1)
                        x = at_slot(slice(0, P), before)[:, PAD:]
                        dve.scalar_tensor_tensor(out=x, in0=mix[:, 1, :], scalar=vec[:, B2:B2 + 1], in1=x,
                                                 op0=ALU.add, op1=ALU.add).then_inc(f_added.sem, 1)
                        if first:
                            make_vec(layer)

            rounds(dve, body)

        @blk.scalar
        def _(act):
            for ev in (staged, copied, squared, qk_placed, carried, exped, p_placed, keys_placed, placed, wvo_placed, f_copied, f_scaled, gated):
                act.sem_inc(ev.sem, 2 * ev.per)
            wait(act, fixed_made, 0)

            def body(layer, it, s, before, first, new):
                prev = before is not None
                for t in range(TILES):
                    cur, l1, l2 = lags(t, prev, new)
                    n = it * TILES + t
                    i = t % 2
                    def stage(t):
                        n = it * TILES + t
                        wait(act, tokens_doubled, n - 2)
                        wait(act, low_staged, n - 2)
                        wait(act, qk_projected, n - 2)
                        for h in range(2):
                            ch = slice(DH * h, DH * h + DH)
                            at = PAD - WIN + P * t - h
                            cp = act.activation(xs[ch, t % 2, :], at_slot(ch, s)[:, at:at + WIN + P], ACT.Identity)
                        cp.then_inc(staged.sem, 1)
                        wait(act, staged, n, 0)
                        act.activation(x_hi[:, t % 2, :], xs[:, t % 2, WIN:], ACT.Identity).then_inc(staged.sem, 1)

                    def copy(j):
                        wait(act, qk_projected, n, j)
                        wait(act, rotated, n - 1, j)
                        act.activation(raw[:, j, :], proj[j % 2][:, :], ACT.Identity).then_inc(copied.sem, 1)

                    def place_qk(j):
                        o = (t - 1) % 2
                        wait(act, qk_turned, n - 1, j)
                        pairs = slice(4 * (j % 2), 4 * (j % 2) + 4)
                        if j < 2:
                            cp = act.activation(qT[:, pairs, :], turned[j % 2][:, :, :], ACT.Identity)
                        else:
                            for h in range(2):
                                ch = slice(DH * h, DH * h + DH)
                                cp = act.activation(kT[ch, o, pairs, h, WIN:], turned[j % 2][ch, :, :], ACT.Identity)
                        cp.then_inc(qk_placed.sem, 1)

                    def place(j):
                        wait(act, mixed, n - 2, j)
                        w0, h = 2 * (j // 2), j % 2
                        act.activation(y[:, :, h, WIN * w0:WIN * w0 + 2 * WIN].rearrange("p c (w q) -> p w c q", q=WIN),
                                       mix[:, h, :].rearrange("p (w c q) -> p w c q", w=2, q=WIN), ACT.Identity).then_inc(placed.sem, 1)

                    if cur and t == 0:
                        stage(0)
                    if cur:
                        copy(0)
                        copy(1)
                    if l2:
                        for j in range(2):
                            wait(act, p_turned, n - 2, j)
                            act.activation(probT[:, 4 * j:4 * j + 4, :], turned[j][:, :, :], ACT.Identity).then_inc(p_placed.sem, 1)
                    if cur:
                        copy(2)
                        copy(3)
                    def square(j):
                        wait(act, copied, n, j)
                        wait(act, squares_summed, n - 1, j)
                        act.activation(sq[:, j, :], raw[:, j, :], ACT.Square).then_inc(squared.sem, 1)

                    def open_gate(c):
                        rows = CHUNKS[c][1]
                        wait(act, f_gate, it - 1, c)
                        act.activation(hid[0:rows, c, :], proj[1][0:rows, :], ACT.Gelu,
                                       bias=vec[0:rows, B1_GATE + c:B1_GATE + c + 1]).then_inc(gated.sem, 1)

                    if l1:
                        place_qk(0)
                        place_qk(1)
                    if cur:
                        square(0)
                        square(1)
                    if l1:
                        place_qk(2)
                    if cur:
                        square(2)
                        square(3)
                    if l1:
                        place_qk(3)
                        o = (t - 1) % 2
                        wait(act, qk_placed, n - 1)
                        act.activation(kT[:, 1 - o, :, :, 0:WIN].rearrange("p c n t -> p (c n) t"),
                                       kT[:, o, :, :, P:].rearrange("p c n t -> p (c n) t"), ACT.Identity).then_inc(carried.sem, 1)
                    if prev and t == 2:
                        wait(act, f_turned, it - 1)
                        act.activation(xn[:, :, :].rearrange("p t d -> p (t d)"), proj[1][:, :], ACT.Identity).then_inc(f_copied.sem, 1)
                    if l2:
                        place(0)
                        place(1)
                    if cur:
                        wait(act, keys_turned, n)
                        act.activation(keys[:, t, :, :].rearrange("p w d -> p (w d)"), proj[0][:, :], ACT.Identity).then_inc(keys_placed.sem, 1)
                    if cur and t < TILES - 1:
                        stage(t + 1)
                    if l2:
                        place(2)
                        place(3)
                    if prev and t == 3:
                        wait(act, f_back, it - 1)
                        act.activation(xnT[:, :], proj[1][:, :], ACT.Identity, scale=vec[:, LN_G:LN_G + 1],
                                       bias=vec[:, LN_B:LN_B + 1]).then_inc(f_scaled.sem, 1)
                    if l1:
                        for j in range(2):
                            wait(act, subtracted, n - 1, j)
                            act.activation(prob[:, 8 * j:8 * j + 8, :], prob[:, 8 * j:8 * j + 8, :], ACT.Exp).then_inc(exped.sem, 1)
                    if prev and t == 3:
                        for c in range(len(CHUNKS)):
                            open_gate(c)
                    if first and t == 1:
                        for j in range(4):
                            wait(act, wvo_made, layer, j)
                            act.activation(wvo[:, 4 * j:4 * j + 4, :], turned[j % 2][:, :, :], ACT.Identity).then_inc(wvo_placed.sem, 1)

            rounds(act, body)

        @blk.gpsimd
        def _(pool):
            for ev in (low_staged, tokens_doubled, rope_summed, normed):
                pool.sem_inc(ev.sem, 2 * ev.per)

            def body(layer, it, s, before, first, new):
                def stage_low(t):
                    n, i = it * TILES + t, t % 2
                    wait(pool, staged, n)
                    wait(pool, qk_projected, n - 2)
                    pool.tensor_tensor(x_lo[:, i, :], xs[:, i, WIN:], x_hi[:, i, :].bitcast(F32), ALU.subtract).then_inc(low_staged.sem, 1)

                for t in range(TILES if new else 0):
                    n = it * TILES + t
                    i = t % 2
                    if t == 0:
                        stage_low(0)
                    wait(pool, keys_turned, n - 2)
                    pool.tensor_tensor(pool_pause[:, :], ident[:, 0:1], ident[:, 0:1], ALU.add)
                    for w in range(TILES):
                        tokens = xs[:, i, WIN * w:WIN * w + 2 * WIN].unsqueeze(1).to_broadcast([P, 2, 2 * WIN])
                        cp = pool.tensor_copy(doubled[:, i, w, :, :], tokens)
                    cp.then_inc(tokens_doubled.sem, 1)
                    for j in range(4):
                        wait(pool, rotated, n, j)
                        pool.tensor_tensor(qk[:, i, j, :], qk[:, i, j, :], other[:, j, :], ALU.add).then_inc(rope_summed.sem, 1)
                    if t < TILES - 1:
                        stage_low(t + 1)
                    wait(pool, norm_step, n)
                    for j in range(4):
                        wait(pool, rope_summed, n, j)
                        x = qk[:, i, j, :].rearrange("p (h d) -> p h d", d=DH)
                        pool.tensor_tensor(x, x, inv[:, i, 8 * j:8 * j + 8].unsqueeze(2).to_broadcast([P, 8, DH]),
                                           ALU.mult).then_inc(normed.sem, 1)

            rounds(pool, body)

        @blk.tensor
        def _(pe):
            for ev in (qk_projected, qk_turned, scored, p_turned, keys_turned, mixed, attn_projected, wvo_made,
                       f_turned, f_back, f_gate, f_value, f_out):
                pe.sem_inc(ev.sem, 2 * ev.per)
            wait(pe, fixed_made, 0)

            def body(layer, it, s, before, first, new):
                prev = before is not None
                for t in range(TILES):
                    cur, l1, l2 = lags(t, prev, new)
                    n = it * TILES + t
                    i = t % 2
                    def project(j):
                        cols = slice(512 * j, 512 * j + 512)
                        if first and t == 0:
                            wait(pe, weights_split, layer, 2 * j + 1)
                        if j >= 2:
                            wait(pe, copied, n, j - 2)
                        elif j == 1:
                            wait(pe, copied, n - 1, 3)
                            if prev and t == 0:
                                wait(pe, gated, it - 2)
                            if prev and t == 3:
                                wait(pe, f_copied, it - 1)
                        else:
                            wait(pe, keys_placed, n - 1)
                            if prev and t == 0:
                                wait(pe, hidden, it - 2)
                        pe.matmul(proj[j % 2][:, :], x_hi[:, i, :], w_hi[:, cols], start=True, stop=False)
                        pe.matmul(proj[j % 2][:, :], x_hi[:, i, :], w_lo[:, cols], start=False, stop=False)
                        pe.matmul(proj[j % 2][:, :], x_lo[:, i, :], w_hi[:, cols], start=False, stop=True).then_inc(qk_projected.sem, 1)

                    def turn_qk(j):
                        wait(pe, normed, n - 1, j)
                        if j >= 2:
                            wait(pe, qk_placed, n - 1, j - 2)
                        elif l2:
                            wait(pe, p_placed, n - 2, j)
                        for c in range(4):
                            mm = pe.transpose(turned[j % 2][:, c, :], qk[:, (t - 1) % 2, j, P * c:P * c + P], ident[:, :])
                        mm.then_inc(qk_turned.sem, 1)

                    def mix_windows(w0):
                        for h in range(2):
                            half = slice(DH * h, DH * h + DH)
                            if w0:
                                wait(pe, placed, n - 2, h)
                            for w in (w0, w0 + 1):
                                mm = pe.matmul(mix[:, h, 256 * (w - w0):256 * (w - w0) + 256].rearrange("p (c q) -> p c q", q=WIN),
                                               keys[half, (t - 2) % TILES, w, :], probT[half, :, WIN * w:WIN * w + WIN],
                                               start=True, stop=True)
                            mm.then_inc(mixed.sem, 1)

                    def map_heads(h):
                        if first and t == 2:
                            wait(pe, wvo_placed, layer)
                        wait(pe, placed, n - 2, 2 + h)
                        for c in range(PAIRS):
                            mm = pe.matmul(mix[:, 0, 0:P], wvo[:, 2 * c + h, :], y[:, c, h, :],
                                           start=(h == 0 and c == 0), stop=(h == 1 and c == PAIRS - 1))
                        if h:
                            mm.then_inc(attn_projected.sem, 1)

                    def feed(c):
                        c0, rows = CHUNKS[c]
                        if c == 0:
                            pe.wait_ge(ffn_loaded.sem, (layer - 1 if first else layer) * 48 + 48)
                            wait(pe, f_scaled, it - 1)
                            if new:
                                wait(pe, copied, n, 3)
                                wait(pe, keys_placed, n)
                        else:
                            wait(pe, gated, it - 1, c - 1)
                        pe.matmul(proj[1][0:rows, :], w1[:, HID + c0:HID + c0 + rows], xnT[:, :], start=True, stop=True).then_inc(f_gate.sem, 1)
                        if c:
                            wait(pe, hidden, it - 1, c - 1)
                        pe.matmul(proj[0][0:rows, :], w1[:, c0:c0 + rows], xnT[:, :], start=True, stop=True).then_inc(f_value.sem, 1)

                    if cur:
                        wait(pe, low_staged, n)
                        project(0)
                        project(1)
                    if l2:
                        for j in range(2):
                            wait(pe, weighed, n - 2, j)
                            wait(pe, qk_placed, n - 2, 2 + j)
                            if first and t == 2:
                                wait(pe, wvo_placed, layer, 2 + j)
                            for c in range(4):
                                pr = prob[:, 8 * j + 2 * c:8 * j + 2 * c + 2, :].rearrange("p h k -> p (h k)")
                                mm = pe.transpose(turned[j][:, c, :], pr, ident[:, :])
                            mm.then_inc(p_turned.sem, 1)
                    if cur:
                        project(2)
                        project(3)
                    if l1:
                        turn_qk(0)
                        turn_qk(1)
                    if prev and t == 2:
                        wait(pe, f_staged, it - 1)
                        if new:
                            wait(pe, copied, n, 3)
                        for k in range(TILES):
                            mm = pe.transpose(proj[1][:, P * k:P * k + P], xf[:, P * k:P * k + P], ident[:, :])
                        mm.then_inc(f_turned.sem, 1)
                    if l1:
                        turn_qk(2)
                        turn_qk(3)
                    if l2:
                        wait(pe, p_placed, n - 2)
                        wait(pe, keys_placed, n - 2)
                        wait(pe, attn_added, n - 3)
                        if prev and t == 0:
                            wait(pe, f_added, it - 2)
                        mix_windows(0)
                    if cur:
                        wait(pe, tokens_doubled, n)
                        wait(pe, copied, n, 2)
                        for w in range(TILES):
                            mm = pe.transpose(proj[0][:, P * w:P * w + P], doubled[:, i, w, :, :].rearrange("p r k -> p (r k)"), ident[:, :])
                        mm.then_inc(keys_turned.sem, 1)
                    if l1:
                        wait(pe, carried, n - 2)
                        for j in range(2):
                            wait(pe, qk_placed, n - 1, 2 + j)
                            wait(pe, subtracted, n - 2, j)
                            pe.matmul(scores[:, j, :], ident16[:, :], mask[:, 0 if t == 1 else 1, :],
                                      start=True, stop=False, skip_group_check=True)
                            for c in range(4):
                                for w in range(TILES):
                                    q = slice(WIN * w, WIN * w + WIN)
                                    mm = pe.matmul(scores[q, j, P * c:P * c + P].rearrange("p (n k) -> p n k", n=2), qT[:, 4 * j + c, q],
                                                   kT[:, (t - 1) % 2, 4 * j + c, :, WIN * w:WIN * w + 2 * WIN],
                                                   start=False, stop=True, skip_group_check=True)
                            mm.then_inc(scored.sem, 1)
                    if l2:
                        mix_windows(2)
                    if l2:
                        map_heads(0)
                    if prev and t == 3:
                        wait(pe, f_normed, it - 1)
                        if new:
                            wait(pe, copied, n, 3)
                        for k in range(TILES):
                            mm = pe.transpose(proj[1][:, P * k:P * k + P], xn[:, k, :], ident[:, :])
                        mm.then_inc(f_back.sem, 1)
                    if l2:
                        map_heads(1)
                    if prev and t == 3:
                        feed(0)
                        feed(1)
                        feed(2)
                        wait(pe, hidden, it - 1)
                        wait(pe, placed, n - 2 if l2 else it * TILES - 1)
                        for c, (c0, rows) in enumerate(CHUNKS):
                            mm = pe.matmul(mix[:, 1, :], w2[0:rows, c, :], hid[0:rows, c, :], start=(c == 0), stop=(c == 2))
                        mm.then_inc(f_out.sem, 1)
                    if first and t == 1:
                        pe.wait_ge(wvo_loaded.sem, layer * 32 + 32)
                        for j in range(4):
                            if j >= 2:
                                wait(pe, wvo_placed, layer, j - 2)
                            else:
                                wait(pe, qk_placed, n - 1, 2 + j)
                            for c in range(4):
                                mm = pe.matmul(turned[j % 2][:, c, :], wvT[:, 4 * j + c, :], wo[:, 4 * j + c, :], start=True, stop=True)
                            mm.then_inc(wvo_made.sem, 1)

            rounds(pe, body)


def final_norm(nc, a, XT, X1T, ident, out):
    with ExitStack() as ctx:
        def sb(name, shape, dt=F32):
            return ctx.enter_context(nc.sbuf_tensor("c_" + name, shape, dt))

        def sem(name):
            return ctx.enter_context(nc.semaphore("c_" + name))

        bank = [ctx.enter_context(nc.psum_tensor(f"c_bank{i}", [P, TILES, D], F32)) for i in range(2)]
        total, tok = sb("total", [P, 2, L]), sb("tok", [P, 2, TILES, D])
        stats, mv = sb("stats", [P, TILES, 6]), sb("mv", [P, TILES, 2])
        dev, eps, pause = sb("dev", [P, TILES]), sb("eps", [P, 1]), sb("pause", [P, 1])
        turned, deviation = sem("turned"), sem("deviation")
        stored = [sem("stored_even"), sem("stored_odd")]
        steps = Steps(sem("vector_step"), [f"{n}{q}" for q in range(2) for n in (
            ["total"] + [f"stats{t}" for t in range(TILES)] + [f"mean{t}" for t in range(TILES)] + ["inv dev"]
            + [f"norm{t}" for t in range(TILES)])])
        blk = ctx.enter_context(nc.Block())

        @blk.vector
        def _(dve):
            dve.sem_inc(steps.sem, ONE)
            dve.memset(eps[:, :], LN_EPS)
            with dve.Fori(0, B // 2) as s2:
                def step(instruction, name, wait=True):
                    steps.did(instruction, name)
                    if wait:
                        dve.wait_ge(steps.sem, steps.count(s2, name))

                for q in range(2):
                    s = s2 * 2 + q
                    step(dve.tensor_tensor(total[:, q, :], XT[:, bass.ds(s, 1), PAD:].rearrange("p o t -> p (o t)"),
                                           X1T[:, bass.ds(s, 1), :].rearrange("p o t -> p (o t)"), ALU.add), f"total{q}", False)
                    dve.wait_ge(turned, s + 1)
                    for t in range(TILES):
                        step(dve.bn_stats(stats[:, t, :], bank[q][:, t, :]), f"stats{t}{q}", t == TILES - 1)
                    dve.memset(pause[:, :], 0.0)
                    for t in range(TILES):
                        step(dve.bn_aggr(mv[:, t, :], stats[:, t, :]), f"mean{t}{q}", False)
                    dve.wait_ge(deviation, s + 1)
                    step(dve.reciprocal(dev[:, :], dev[:, :]), f"inv dev{q}")
                    dve.wait_ge(stored[q], s2 * 16 + 1)
                    for t in range(TILES):
                        step(dve.tensor_scalar(tok[:, q, t, :], bank[q][:, t, :], mv[:, t, 0:1], dev[:, t:t + 1],
                                               ALU.subtract, ALU.mult), f"norm{t}{q}", False)

        @blk.scalar
        def _(act):
            with act.Fori(0, B // 2) as s2:
                for q in range(2):
                    act.wait_ge(steps.sem, steps.count(s2, f"mean{TILES - 1}{q}"))
                    act.activation(dev[:, :], mv[:, :, 1], ACT.Sqrt, bias=eps[:, 0:1]).then_inc(deviation, 1)

        @blk.tensor
        def _(pe):
            with pe.Fori(0, B // 2) as s2:
                for q in range(2):
                    pe.wait_ge(steps.sem, steps.count(s2, f"total{q}"))
                    for t in range(TILES):
                        mm = pe.transpose(bank[q][:, t, :], total[:, q, P * t:P * t + P], ident[:, :])
                    mm.then_inc(turned, 1)

        @blk.sync
        def _(sp):
            sp.sem_inc(stored[0], ONE)
            sp.sem_inc(stored[1], ONE)
            with sp.Fori(0, B // 2) as s2:
                for q in range(2):
                    s = s2 * 2 + q
                    sp.wait_ge(steps.sem, steps.count(s2, f"norm{TILES - 1}{q}"))
                    sp.dma_start(out[bass.ds(s, 1)].rearrange("o (t p) d -> p (o t) d", p=P), tok[:, q, :, :]).then_inc(stored[q], 16)
            for q in range(2):
                sp.wait_ge(stored[q], ONE + 16 * B // 2)


def build(nc, a, out, layers=True):
    with ExitStack() as ctx:
        XT = ctx.enter_context(nc.sbuf_tensor("XT", [P, B, SPAN], F32))
        X1T = ctx.enter_context(nc.sbuf_tensor("X1T", [P, B, L], F32))
        ident = ctx.enter_context(nc.sbuf_tensor("ident", [P, P], F32))
        state_space_layer(nc, a, XT, X1T, ident)
        if layers:
            attention_layers(nc, a, XT, ident)
        final_norm(nc, a, XT, X1T, ident, out)


def lay_out(x):
    f = lambda v: np.ascontiguousarray(v)
    g = {n: np.asarray(v) for n, v in x.items()}
    rows = lambda v: f(np.broadcast_to(v.reshape(1, -1), (P, v.size)))
    qk = np.stack([g["L0_ffn_q_scale"], g["L0_ffn_k_scale"]], 1)
    back = np.concatenate([qk[..., DH // 2:], qk[..., :DH // 2]], -1)
    qk = np.stack([qk, back], 2)
    W2 = g["L0_ffn_W2"]
    d = dict(
        x=g["L0_attn_x"], xT=f(g["L0_attn_x"].transpose(2, 0, 1)), W_in=g["L0_attn_W_in"],
        W_out=g["L0_attn_W_out"], w_conv=f(g["L0_attn_w_conv"][:, 0, :].T), b_conv=g["L0_attn_b_conv"],
        theta=rows(g["L0_attn_theta"]), logits=rows(g["L0_attn_deriv_logits"]),
        slopes=np.concatenate([g["L0_attn_decay_slopes"], g["L0_attn_anchor_slopes"]]),
        score_scale=g["L0_attn_score_scale"], W_re=g["L0_attn_W_re"], W_im=g["L0_attn_W_im"],
        norm_scale=g["L0_attn_norm_scale"],
        Wqkv=g["L0_ffn_Wqkv"],
        WvT=f(g["L0_ffn_Wqkv"][:, :, 2 * INNER:].reshape(DEPTH, D, HEADS, DH).transpose(0, 3, 2, 1)), qk_scale=f(np.broadcast_to(qk.reshape(DEPTH, 1, -1), (DEPTH, P, qk[0].size))),
        Wo=g["L0_ffn_Wo"], ln_g=f(g["L0_ffn_ln_g"].T), ln_b=f(g["L0_ffn_ln_b"].T),
        W1=g["L0_ffn_W1"], b1=g["L0_ffn_b1"], W2=W2, b2=f(g["L0_ffn_b2"].T))
    d.update(constants())
    return d


def kernel(**inputs):
    import concourse.bacc as _bacc
    from concourse.bass_utils import run_bass_kernel_spmd as _run

    nc = _bacc.Bacc("TRN2", target_bir_lowering=False, num_devices=1)
    arrays = {f"in_{n}_dram": v for n, v in lay_out(inputs).items()}
    a = {n[3:-5]: nc.dram_tensor(n, v.shape, mybir.dt.from_np(v.dtype), kind="ExternalInput").ap()
         for n, v in arrays.items()}
    out = nc.dram_tensor("out_dram", (B, L, D), F32, kind="ExternalOutput").ap()
    build(nc, a, out)
    r = _run(nc, [arrays], core_ids=[0])
    return r.results[0]["out_dram"]
```

```python
from contextlib import ExitStack

import numpy as np

import concourse.bass as bass
from concourse import mybir

F32 = mybir.dt.float32
BF16 = mybir.dt.bfloat16
F32R = mybir.dt.float32r
I32 = mybir.dt.int32
ALU = mybir.AluOpType
ACT = mybir.ActivationFunctionType
AX = mybir.AxisListType

P = 128
B, L, D = 8, 512, 128
TILES = L // P
K, H, M = 32, 4, 4
TAPS = 4
TOTAL = 2 * D + K
LN_EPS = 1e-5
MAGIC = 12582912.0
TWO_PI = 6.283185
TURN = 1.0 / 6.283185307179586
DEPTH, HEADS, DH, WIN = 6, 16, 64, 32
DEPTH_RUN = DEPTH
INNER = HEADS * DH
PAIRS = HEADS // 2
HID = int(D * 4 * 2 / 3)
CHUNKS = [(c, min(P, HID - c)) for c in range(0, HID, P)]
PAD = WIN + 1
SPAN = PAD + L
MASKED = -1e30
ONE = 1


def constants():
    f = np.float32
    ident = np.eye(P, dtype=f)
    i = np.arange(P)
    late = (np.arange(L)[None, :] >= i[:, None]).astype(f)
    block = (np.arange(K)[None, None, :] == 8 * np.arange(4)[None, :, None] + (i // 16)[:, None, None]).astype(f)
    spread = (np.arange(P)[None, :] // H == np.arange(K)[:, None]).astype(f)
    rep16 = (np.arange(P)[None, :] % 16 == np.arange(16)[:, None]).astype(f)
    pos = np.arange(L, dtype=f)
    dist = np.concatenate([np.tile(f(L - 1) - pos, (K - 4, 1)), np.tile(pos, (4, 1))], 0).astype(f)
    half = np.arange(0, DH, 2, dtype=f)
    inv = f(1.0) / f(10000.0) ** (half / f(DH))
    fr = (pos[:, None] * inv[None, :]).astype(f)
    fr = np.concatenate([fr, fr], -1)
    base = ((half + f(0.4 * DH)) / f(1.4 * DH)).astype(f)
    power = (pos - L // 2) / f(WIN // 2)
    sc = base[None, :] ** power[:, None]
    sc = np.concatenate([sc, sc], -1).astype(f)
    sign = np.where(np.arange(DH) < DH // 2, -1, 1).astype(f)
    cos, sin = np.cos(fr), np.sin(fr) * sign
    q = np.stack([cos * sc * 8, sin * sc * 8], 1)
    k = np.stack([cos / sc, sin / sc], 1)
    rope = np.stack([q, k], 1).reshape(TILES, P, 2, 2, DH).transpose(1, 0, 2, 3, 4)
    a, b = (i % WIN)[:, None], np.arange(2 * WIN)[None, :]
    off = (b < a) | (b > a + WIN)
    first = off | ((i < WIN)[:, None] & (b < WIN))
    mask = np.stack([np.tile(np.where(m, MASKED, 0.0), (1, 8)) for m in (first, off)], 1)
    out = dict(ident=ident, late=late, block=block.reshape(P, 4 * K), spread=spread, rep16=rep16,
               dist=dist, rope=rope.reshape(P, -1), mask=mask.reshape(P, -1))
    return {n: np.ascontiguousarray(x, f) for n, x in out.items()}


class Steps:

    def __init__(self, sem, names):
        self.sem, self.names, self.at = sem, names, 0

    def did(self, instruction, name):
        assert self.names[self.at] == name, (self.names[self.at], name)
        self.at = (self.at + 1) % len(self.names)
        instruction.then_inc(self.sem, 1)

    def skip(self, engine, rounds, name):
        assert self.names[self.at] == name, (self.names[self.at], name)
        engine.wait_ge(self.sem, self.count(rounds, name) - 1)
        engine.sem_inc(self.sem, 1)
        self.at = (self.at + 1) % len(self.names)

    def count(self, rounds, name):
        return rounds * len(self.names) + self.names.index(name) + 1 + ONE


class Event:

    def __init__(self, sem, per=1):
        self.sem, self.per = sem, per

    def value(self, rounds, part=None):
        return rounds * self.per + (self.per if part is None else part + 1) + 2 * self.per


def rsqrt(dve, lanes):
    def each(op):
        for tick, x, y, h in lanes:
            tick(op(x, y, h))
        for tick, x, y, h in lanes:
            tick()

    each(lambda x, y, h: dve.tensor_scalar(y.bitcast(I32), x.bitcast(I32), 1, None, ALU.logical_shift_right))
    each(lambda x, y, h: dve.tensor_scalar(y.bitcast(I32), y.bitcast(I32), -1.0, float(0x5F3759DF), ALU.mult, ALU.add))
    for _ in range(3):
        each(lambda x, y, h: dve.scalar_tensor_tensor(out=h, in0=y, scalar=-0.5, in1=y, op0=ALU.mult, op1=ALU.mult))
        each(lambda x, y, h: dve.tensor_tensor(h, h, x, ALU.mult))
        each(lambda x, y, h: dve.scalar_tensor_tensor(out=y, in0=h, scalar=1.5, in1=y, op0=ALU.add, op1=ALU.mult))


ABS_BITS = 0x7FFFFFFF
RSQRT = 11


def state_space_layer(nc, a, XT, X1T, ident):
    ORDER = [c + 4 * i for c in range(4) for i in range(2)]
    with ExitStack() as ctx:
        def sb(name, shape, dt=F32):
            return ctx.enter_context(nc.sbuf_tensor("a_" + name, shape, dt))

        def sem(name):
            return ctx.enter_context(nc.semaphore("a_" + name))

        bank = [ctx.enter_context(nc.psum_tensor(f"a_bank{i}", [P, 512], F32)) for i in range(8)]
        xin, xtok = sb("xin", [P, B, L]), sb("xtok", [P, B, TILES, D])
        w_in, w_out = sb("w_in", [P, TOTAL]), sb("w_out", [P, D])
        taps, bias = sb("taps", [P, 3, TAPS]), sb("bias", [P, 3])
        theta, logit = sb("theta", [P, P, M]), sb("logit", [P, 3])
        top, weights, total = sb("top", [P, 1]), sb("weights", [P, 3]), sb("total", [P, 1])
        slope, sscale = sb("slope", [K, 1]), sb("sscale", [K, 1])
        soft = sb("soft", [K, 10])
        w16, nscale, wrep = sb("w16", [16, 8]), sb("nscale", [16, 2]), sb("wrep", [P, 8])
        late, block = sb("late", [P, L]), sb("block", [P, 4 * K])
        spread, rep16 = sb("spread", [K, P]), sb("rep16", [16, P])
        time_w = sb("time_w", [K, L])
        w_blk, sum_blk = sb("w_blk", [P, 8, P]), sb("sum_blk", [P, 4, P])
        magic, quarter, eps = sb("magic", [P, 1]), sb("quarter", [P, 1]), sb("eps", [P, 1])
        ones = sb("ones", [P, L])
        z, conv, gate = sb("z", [P, 3, TAPS - 1 + L]), sb("conv", [P, 3, L]), sb("gate", [P, L])
        pw, poly, den = sb("pw", [K, L]), sb("poly", [P, L]), sb("den", [P, L])
        g_tok = sb("g_tok", [P, TILES, P])
        values, phase = sb("values", [P, TILES, P]), sb("phase", [P, 2, 512])
        whole, turn, turn_abs = (sb(n, [P, 2, 512]) for n in ("whole", "turn", "turn_abs"))
        sin, cos = sb("sin", [P, TILES, 512]), sb("cos", [P, TILES, 512])
        moments = sb("moments", [P, TILES, 2 * 512])
        tiles_before = sb("tiles_before", [P, 2, 2 * 512])
        num, sq, sq_sum = sb("num", [P, 2, L]), sb("sq", [P, 2, L]), sb("sq_sum", [P, 2, L])
        ms, yg = sb("ms", [P, L]), sb("yg", [P, L])
        res, res_n = sb("res", [P, TILES, D]), sb("res_n", [P, TILES, D])
        stats, mv = sb("stats", [P, TILES, 6]), sb("mv", [P, TILES, 2])
        var, dev, dev_half = sb("var", [P, TILES]), sb("dev", [P, TILES]), sb("dev_half", [P, TILES])
        pause = sb("pause", [P, 1])

        small_loaded, channels_loaded, tokens_loaded = sem("small_loaded"), sem("channels_loaded"), sem("tokens_loaded")
        vector_ready, scalar_ready, spread_ready = sem("vector_ready"), sem("scalar_ready"), sem("spread_ready")
        setup_done, vector_own = sem("setup_done"), sem("vector_own")
        pe_s = Steps(sem("tensor_step"), ["feat_z0", "feat_z2", "sum_cum0", "feat_z1", "sum_cum1", "sum_map0", "feat_values",
                                          "sum_cum2", "sum_map1", "sum_cum3", "sum_map2", "norm_out", "sum_squares0",
                                          "sum_cum4", "sum_map3", "feat_spread", "sum_cum5", "sum_map4", "sum_squares1",
                                          "feat_g", "sum_cum6", "sum_map5", "norm_turned", "sum_cum7", "sum_map6", "sum_squares2",
                                          "sum_map7", "sum_squares3"])
        act_s = Steps(sem("scalar_step"), ["feat_z0", "feat_z2", "sum_num0", "sum_square0", "feat_z1", "sum_num1", "sum_square1",
                                           "feat_values", "sum_num2", "sum_square2", "feat_p", "sum_num3", "sum_square3",
                                           "feat_whole0", "feat_sin0", "feat_cos0", "feat_whole1", "sum_num4", "sum_square4",
                                           "feat_sin1", "feat_cos1", "feat_whole2", "sum_num5", "sum_square5",
                                           "feat_sin2", "feat_cos2", "feat_g", "feat_whole3", "sum_num6", "sum_square6",
                                           "feat_sin3", "feat_cos3", "sum_num7", "sum_square7", "norm_stored", "norm_kept",
                                           "feat_silu", "sum_rms"])
        conv_steps = lambda c: [f"feat_conv{c}{j}" for j in range(TAPS)]
        dve_s = Steps(sem("vector_step"), conv_steps(0) + conv_steps(2) + ["feat_clip_low", "feat_clip", "norm_inv_rms", "norm_yg",
                                          "feat_poly1", "feat_poly2", "feat_turn0", "feat_turn_abs0", "feat_weight",
                                          "norm_residual"]
                      + [f"norm_stats{t}" for t in range(TILES)] + [f"norm_mean{t}" for t in range(TILES)]
                      + ["feat_turn1", "feat_turn_abs1", "feat_g", "norm_var"] + [f"norm_inv_dev{i}" for i in range(RSQRT)]
                      + [f"norm_norm{t}" for t in range(TILES)]
                      + ["feat_turn2", "feat_turn_abs2"] + conv_steps(1) + ["feat_turn3", "feat_turn_abs3"]
                      + [f"feat_{n}{t}" for t in range(TILES) for n in ("re", "im")]
                      + ["sum_yg", "sum_ms", "feat_den", "feat_den_floor", "feat_den_square"])
        pool_s = Steps(sem("pool_step"), ["sum_added0", "feat_phase0", "feat_phase1", "sum_added1", "feat_phase2",
                                          "sum_added2", "feat_phase3", "sum_added3", "feat_before0", "feat_before1"])
        PROJ, VALUES, SPREAD, OUT = {2: 0, 0: 1, 1: 0}, 1, 2, 3
        CUM, MAPPED, SQUARES = [4, 5], 6, 7

        def slot(x, r, back):
            part = x[:, r - back] if isinstance(r, int) else x[:, bass.ds(r - back if back else r, 1)]
            if not isinstance(r, int):
                part = part.rearrange("p o t -> p (o t)") if len(x.shape) == 3 else part.rearrange("p o t d -> p (o t) d")
            return part

        def rounds(engine, body):
            body(0, True, False, False)
            body(1, True, True, False)
            with engine.Fori(2, B) as r:
                body(r, True, True, True)
            body(B, False, True, True)
            body(B + 1, False, False, True)

        def ways(engine, own, r, feat, sums, norm):
            runs = dict(feat=feat, sums=sums, norm=norm)
            active = lambda name: runs[{"feat": "feat", "sum_": "sums", "norm": "norm"}[name[:4]]]

            def after(steps, name, need=True):
                if need and active(name):
                    engine.wait_ge(steps.sem, steps.count(r, name))

            def before(steps, name, need=True):
                if need and not (isinstance(r, int) and r == 0):
                    engine.wait_ge(steps.sem, steps.count(r - 1, name))

            def do(name, make, wait=False):
                if active(name):
                    own.did(make(), name)
                    if wait:
                        engine.wait_ge(own.sem, own.count(r, name))
                else:
                    own.skip(engine, r, name)

            return after, before, do

        col = lambda x: x.rearrange("(p o) -> p o", o=1)
        loads = [(w_in[:, :], a["W_in"]), (w_out[:, :], a["W_out"]),
                 (taps[:, 0:2, :], a["w_conv"][0:2 * P, :].rearrange("(c p) j -> p c j", p=P)),
                 (taps[0:K, 2, :], a["w_conv"][2 * P:TOTAL, :]),
                 (bias[:, 0:1], col(a["b_conv"][0:P])), (bias[:, 1:2], col(a["b_conv"][P:2 * P])),
                 (bias[0:K, 2:3], col(a["b_conv"][2 * P:TOTAL])),
                 (theta[:, :, :], a["theta"].rearrange("p (c m) -> p c m", m=M)), (logit[:, :], a["logits"]),
                 (slope[:, :], col(a["slopes"])), (sscale[:, :], col(a["score_scale"])),
                 (w16[:, 0:4], a["W_re"]), (w16[:, 4:8], a["W_im"]),
                 (nscale[:, 0:1], col(a["norm_scale"][0:16])), (nscale[:, 1:2], col(a["norm_scale"][16:32])),
                 (late[:, :], a["late"]), (block[:, :], a["block"]), (spread[:, :], a["spread"]),
                 (rep16[:, :], a["rep16"]), (time_w[:, :], a["dist"]), (ident[:, :], a["ident"])]

        blk = ctx.enter_context(nc.Block())

        @blk.sync
        def _(sp):
            for dst, src in loads:
                sp.dma_start(dst, src).then_inc(small_loaded, 16)
            sp.dma_start(xin[:, :, :], a["xT"]).then_inc(channels_loaded, 16)
            for s in range(B):
                sp.dma_start(xtok[:, s, :, :], a["x"][s].rearrange("(t p) d -> p t d", p=P)).then_inc(tokens_loaded, 16)

        @blk.vector
        def _(dve):
            dve.sem_inc(dve_s.sem, ONE)
            own = [0]

            def tick(instruction):
                own[0] += 1
                instruction.then_inc(vector_own, 1)
                dve.wait_ge(vector_own, own[0])

            for buf, v in ((ones, 1.0), (magic, MAGIC), (quarter, 1.5707963267948966), (eps, LN_EPS)):
                dve.memset(buf[:, :], v)
            dve.memset(z[:, :, 0:TAPS - 1], 0.0)
            tick(dve.memset(XT[:, :, 0:PAD], 0.0))
            dve.wait_ge(small_loaded, 16 * len(loads))
            tick(dve.tensor_reduce(top[:, :], logit[:, :], AX.X, ALU.max))
            dve.tensor_scalar(logit[:, :], logit[:, :], top[:, 0:1], None, ALU.subtract).then_inc(vector_ready, 1)
            dve.tensor_scalar(soft[:, 0:1].bitcast(I32), slope[:, :].bitcast(I32), ABS_BITS, None, ALU.bitwise_and).then_inc(vector_ready, 1)
            dve.wait_ge(scalar_ready, 2)
            tick(dve.tensor_reduce(total[:, :], logit[:, :], AX.X, ALU.add))
            tick(dve.reciprocal(total[:, :], total[:, :]))
            tick(dve.tensor_scalar(weights[:, :], logit[:, :], total[:, 0:1], None, ALU.mult))
            dve.tensor_scalar(soft[:, 2:3], soft[:, 1:2], 1.0, None, ALU.add).then_inc(vector_ready, 1)
            dve.wait_ge(vector_ready, 3)
            tick(dve.tensor_scalar(soft[:, 3:4], soft[:, 2:3], 1.0, None, ALU.subtract))
            tick(dve.tensor_tensor(soft[:, 4:5], soft[:, 1:2], soft[:, 3:4], ALU.subtract))
            tick(dve.reciprocal(soft[:, 5:6], soft[:, 2:3]))
            dve.wait_ge(scalar_ready, 3)
            tick(dve.scalar_tensor_tensor(out=soft[:, 7:8], in0=soft[:, 4:5], scalar=soft[:, 5:6],
                                          in1=soft[:, 6:7], op0=ALU.mult, op1=ALU.add))
            tick(dve.scalar_tensor_tensor(out=soft[:, 8:9], in0=slope[:, :], scalar=0.0,
                                          in1=soft[:, 7:8], op0=ALU.max, op1=ALU.add))
            dve.tensor_scalar(time_w[:, :], time_w[:, :], soft[:, 8:9], None, ALU.mult).then_inc(vector_ready, 1)
            dve.tensor_scalar(w16[:, 0:4], w16[:, 0:4], nscale[:, 0:1], None, ALU.mult)
            dve.tensor_scalar(w16[:, 4:8], w16[:, 4:8], nscale[:, 1:2], None, ALU.mult).then_inc(vector_ready, 1)
            tick(dve.tensor_scalar(theta[:, :, :], theta[:, :, :], TURN, None, ALU.mult))
            blocks = block[:, :].unsqueeze(2).to_broadcast([P, 4 * K, H])
            tick(dve.tensor_copy(sum_blk[:, :, :].rearrange("p c (k h) -> p (c k) h", h=H), blocks))
            dve.wait_ge(spread_ready, 1)
            tick(dve.tensor_copy(wrep[:, :], bank[0][:, 0:8]))
            for i in range(2):
                tick(dve.tensor_tensor(w_blk[:, 4 * i:4 * i + 4, :].rearrange("p c (k h) -> p (c k) h", h=H), blocks,
                                       wrep[:, 4 * i:4 * i + 4].unsqueeze(1).to_broadcast([P, 4 * K, H]), ALU.mult))
            tick(dve.tensor_scalar(top[:, :], weights[:, 2:3], -1.0, None, ALU.mult))
            dve.sem_inc(setup_done, 1)

            def body(r, feat, sums, norm):
                after, before, do = ways(dve, dve_s, r, feat, sums, norm)
                x = conv[:, 0, :]

                def convolve(c):
                    w = K if c == 2 else P
                    after(act_s, f"feat_z{c}")
                    if c == 1:
                        before(act_s, "feat_silu")
                    do(f"feat_conv{c}0", lambda: dve.tensor_scalar(conv[0:w, c, :], z[0:w, c, 0:L], taps[0:w, c, 0:1],
                                                                   bias[0:w, c:c + 1], ALU.mult, ALU.add), True)
                    for j in range(1, TAPS):
                        do(f"feat_conv{c}{j}", lambda: dve.scalar_tensor_tensor(out=conv[0:w, c, :], in0=z[0:w, c, j:j + L],
                                                                                scalar=taps[0:w, c, j:j + 1], in1=conv[0:w, c, :],
                                                                                op0=ALU.mult, op1=ALU.add), True)


                def remainder(t):
                    i = t % 2
                    after(act_s, f"feat_whole{t}")
                    if t >= 2:
                        after(act_s, f"feat_cos{t - 2}")
                    do(f"feat_turn{t}", lambda: dve.scalar_tensor_tensor(out=turn[:, i, :], in0=whole[:, i, :], scalar=MAGIC,
                                                                         in1=phase[:, i, :], op0=ALU.subtract, op1=ALU.subtract), True)
                    do(f"feat_turn_abs{t}", lambda: dve.tensor_scalar(turn_abs[:, i, :].bitcast(I32), turn[:, i, :].bitcast(I32),
                                                                      ABS_BITS, None, ALU.bitwise_and))

                convolve(0)
                convolve(2)
                do("feat_clip_low", lambda: dve.tensor_scalar(conv[0:K, 2, :], conv[0:K, 2, :], sscale[:, 0:1], -20.0,
                                                              ALU.mult, ALU.max), True)
                do("feat_clip", lambda: dve.tensor_scalar(conv[0:K, 2, :], conv[0:K, 2, :], 20.0, None, ALU.min))
                before(act_s, "sum_rms", norm)
                do("norm_inv_rms", lambda: dve.reciprocal(ms[:, :], ms[:, :]), True)
                do("norm_yg", lambda: dve.tensor_tensor(yg[:, :], yg[:, :], ms[:, :], ALU.mult))
                do("feat_poly1", lambda: dve.tensor_scalar(poly[:, :], x, top[:, 0:1], weights[:, 1:2], ALU.mult, ALU.add), True)
                do("feat_poly2", lambda: dve.tensor_tensor(poly[:, :], poly[:, :], x, ALU.mult), True)
                remainder(0)
                after(act_s, "feat_p")
                do("feat_weight", lambda: dve.tensor_tensor(pw[:, :], conv[0:K, 2, :], time_w[:, :], ALU.mult))
                after(pe_s, "norm_out")
                if norm:
                    dve.wait_ge(tokens_loaded, 16 * B)
                do("norm_residual", lambda: dve.tensor_tensor(res[:, :, :].rearrange("p t d -> p (t d)"), bank[OUT][:, :],
                                                              slot(xtok, r, 2).rearrange("p t d -> p (t d)"), ALU.add), True)
                for t in range(TILES):
                    do(f"norm_stats{t}", lambda: dve.bn_stats(stats[:, t, :], res[:, t, :]), t == TILES - 1)
                dve.memset(pause[:, :], 0.0)
                for t in range(TILES):
                    do(f"norm_mean{t}", lambda: dve.bn_aggr(mv[:, t, :], stats[:, t, :]))
                remainder(1)
                after(pe_s, "feat_spread")
                do("feat_g", lambda: dve.scalar_tensor_tensor(out=poly[:, :], in0=poly[:, :], scalar=weights[:, 0:1],
                                                              in1=bank[SPREAD][:, :], op0=ALU.add, op1=ALU.mult))
                do("norm_var", lambda: dve.tensor_scalar(var[:, :], mv[:, :, 1], LN_EPS, None, ALU.add), True)
                newton = iter(range(RSQRT))

                def tick(instruction=None):
                    if instruction is not None:
                        dve_s.did(instruction, f"norm_inv_dev{next(newton)}")
                    else:
                        dve.wait_ge(dve_s.sem, dve_s.count(r, dve_s.names[dve_s.at - 1]))

                if norm:
                    rsqrt(dve, [(tick, var[:, :], dev[:, :], dev_half[:, :])])
                else:
                    for i in range(RSQRT):
                        dve_s.skip(dve, r, f"norm_inv_dev{i}")
                for t in range(TILES):
                    do(f"norm_norm{t}", lambda: dve.tensor_scalar(res_n[:, t, :], res[:, t, :], mv[:, t, 0:1], dev[:, t:t + 1],
                                                                  ALU.subtract, ALU.mult))
                remainder(2)
                convolve(1)
                remainder(3)
                if feat:
                    after(pe_s, "sum_cum7", sums)
                    after(act_s, "feat_g")
                for t in range(TILES):
                    amp = g_tok[:, t, :].unsqueeze(2).to_broadcast([P, P, M])
                    after(act_s, f"feat_cos{t}")
                    for n, (part, trig) in enumerate((("re", cos), ("im", sin))):
                        do(f"feat_{part}{t}", lambda: dve.tensor_tensor(
                            moments[:, t, 512 * n:512 * n + 512].rearrange("p (c m) -> p c m", m=M),
                            trig[:, t, :].rearrange("p (c m) -> p c m", m=M), amp, ALU.mult))
                after(pe_s, "sum_map7")
                do("sum_yg", lambda: dve.tensor_tensor(yg[:, :], bank[MAPPED][:, :], gate[:, :], ALU.mult))
                after(pe_s, "sum_squares3")
                do("sum_ms", lambda: dve.scalar_tensor_tensor(out=ms[:, :], in0=bank[SQUARES][:, :], scalar=1.0 / (2 * H * M),
                                                              in1=den[:, :], op0=ALU.mult, op1=ALU.add), True)
                do("feat_den", lambda: dve.tensor_tensor_scan(den[:, :], ones[:, :], bank[SPREAD][:, :], 0.0, ALU.mult, ALU.add), True)
                do("feat_den_floor", lambda: dve.tensor_scalar(den[:, :], den[:, :], 1e-4, None, ALU.max), True)
                do("feat_den_square", lambda: dve.scalar_tensor_tensor(out=den[:, :], in0=den[:, :], scalar=1e-5, in1=den[:, :],
                                                                       op0=ALU.mult, op1=ALU.mult), True)

            rounds(dve, body)

        @blk.scalar
        def _(act):
            act.sem_inc(act_s.sem, ONE)
            act.wait_ge(vector_ready, 1)
            act.activation(logit[:, :], logit[:, :], ACT.Exp).then_inc(scalar_ready, 1)
            act.wait_ge(vector_ready, 2)
            act.activation(soft[:, 1:2], soft[:, 0:1], ACT.Exp, scale=-1.0).then_inc(scalar_ready, 1)
            act.wait_ge(vector_ready, 3)
            act.activation(soft[:, 6:7], soft[:, 2:3], ACT.Ln).then_inc(scalar_ready, 1)
            act.wait_ge(vector_ready, 4)
            act.activation(time_w[:, :], time_w[:, :], ACT.Exp, scale=-1.0).then_inc(scalar_ready, 1)
            act.wait_ge(setup_done, 1)

            def body(r, feat, sums, norm):
                after, before, do = ways(act, act_s, r, feat, sums, norm)

                def take(c):
                    w = K if c == 2 else P
                    after(pe_s, f"feat_z{c}")
                    do(f"feat_z{c}", lambda: act.activation(z[0:w, c, TAPS - 1:], bank[PROJ[c]][0:w, :], ACT.Identity))

                def sums_of(k):
                    after(pe_s, f"sum_cum{k}")
                    if k >= 2:
                        after(pe_s, f"sum_map{k - 2}")
                    do(f"sum_num{k}", lambda: act.activation(num[:, k % 2, :], bank[CUM[k % 2]][:, :], ACT.Identity), True)
                    if k >= 2:
                        after(pool_s, f"sum_added{k // 2 - 1}")
                    do(f"sum_square{k}", lambda: act.activation(sq[:, k % 2, :], num[:, k % 2, :], ACT.Square))

                def whole_turns(t):
                    after(pool_s, f"feat_phase{t}")
                    if t >= 2:
                        after(dve_s, f"feat_turn{t - 2}")
                    do(f"feat_whole{t}", lambda: act.activation(whole[:, t % 2, :], phase[:, t % 2, :], ACT.Identity, bias=magic[:, 0:1]))

                def sin_cos(t):
                    after(dve_s, f"feat_turn_abs{t}")
                    do(f"feat_sin{t}", lambda: act.activation(sin[:, t, :], turn[:, t % 2, :], ACT.Sin, scale=-TWO_PI))
                    do(f"feat_cos{t}", lambda: act.activation(cos[:, t, :], turn_abs[:, t % 2, :], ACT.Sin, scale=-TWO_PI, bias=quarter[:, 0:1]))

                take(0)
                take(2)
                sums_of(0)
                take(1)
                sums_of(1)
                after(pe_s, "feat_values")
                do("feat_values", lambda: act.activation(values[:, :, :].rearrange("p t c -> p (t c)"), bank[VALUES][:, :], ACT.Identity))
                sums_of(2)
                after(dve_s, "feat_clip")
                do("feat_p", lambda: act.activation(conv[0:K, 2, :], conv[0:K, 2, :], ACT.Exp))
                sums_of(3)
                whole_turns(0)
                sin_cos(0)
                whole_turns(1)
                sums_of(4)
                sin_cos(1)
                whole_turns(2)
                sums_of(5)
                sin_cos(2)
                after(pe_s, "feat_g")
                before(dve_s, f"feat_im{TILES - 1}", feat)
                do("feat_g", lambda: act.activation(g_tok[:, :, :].rearrange("p t c -> p (t c)"), bank[VALUES][:, :], ACT.Identity))
                whole_turns(3)
                sums_of(6)
                sin_cos(3)
                sums_of(7)
                after(pe_s, "norm_turned")
                do("norm_stored", lambda: act.activation(slot(XT, r, 2)[:, PAD:], bank[OUT][:, :], ACT.Identity))
                do("norm_kept", lambda: act.activation(slot(X1T, r, 2), bank[OUT][:, :], ACT.Identity))
                after(dve_s, f"feat_conv1{TAPS - 1}")
                if feat:
                    after(dve_s, "sum_yg", sums)
                do("feat_silu", lambda: act.activation(gate[:, :], conv[:, 1, :], ACT.Silu))
                after(dve_s, "sum_ms")
                do("sum_rms", lambda: act.activation(ms[:, :], ms[:, :], ACT.Sqrt))

            rounds(act, body)
            act.wait_ge(act_s.sem, act_s.count(B + 1, "sum_rms"))

        @blk.tensor
        def _(pe):
            pe.sem_inc(pe_s.sem, ONE)
            pe.wait_ge(small_loaded, 16 * len(loads))
            pe.wait_ge(vector_ready, 5)
            pe.matmul(bank[0][:, 0:8], rep16[:, :], w16[:, :], start=True, stop=True).then_inc(spread_ready, 1)
            pe.wait_ge(setup_done, 1)
            pe.wait_ge(channels_loaded, 16)
            def body(r, feat, sums, norm):
                after, before, do = ways(pe, pe_s, r, feat, sums, norm)

                def project(c):
                    w = K if c == 2 else P
                    do(f"feat_z{c}", lambda: pe.matmul(bank[PROJ[c]][0:w, :], w_in[:, P * c:P * c + w], slot(xin, r, 0), start=True, stop=True))

                def cumulate(k):
                    c = ORDER[k]
                    if k >= 2:
                        after(act_s, f"sum_num{k - 2}")

                    def products():
                        for t in range(TILES):
                            cols, rows = slice(P * t, P * t + P), slice(P * c, P * c + P)
                            mm = pe.matmul(bank[CUM[k % 2]][:, cols], moments[:, t, rows], late[:, 0:P], start=True, stop=(t == 0))
                            if t:
                                earlier = tiles_before[:, t - 2, rows] if t >= 2 else moments[:, 0, rows]
                                mm = pe.matmul(bank[CUM[k % 2]][:, cols], earlier, late[:, P:2 * P], start=False, stop=True)
                        return mm

                    do(f"sum_cum{k}", products)

                def to_channels(k):
                    after(act_s, f"sum_num{k}")
                    do(f"sum_map{k}", lambda: pe.matmul(bank[MAPPED][:, :], w_blk[:, ORDER[k], :], num[:, k % 2, :],
                                                        start=(k == 0), stop=(k == 7)))

                def add_squares(i):
                    after(pool_s, f"sum_added{i}")
                    do(f"sum_squares{i}", lambda: pe.matmul(bank[SQUARES][:, :], sum_blk[:, i, :], sq_sum[:, i % 2, :],
                                                            start=(i == 0), stop=(i == 3)))

                def turn_tiles(name, to, source):
                    def products():
                        for t in range(TILES):
                            mm = pe.transpose(bank[to][:, P * t:P * t + P], source(t), ident[:, :])
                        return mm

                    do(name, products)

                def out_products():
                    for t in range(TILES):
                        mm = pe.matmul(bank[OUT][:, P * t:P * t + P], yg[:, P * t:P * t + P], w_out[:, :], start=True, stop=True)
                    return mm

                before(act_s, "feat_g", feat)
                before(act_s, "feat_z1", feat)
                project(0)
                project(2)
                before(act_s, "sum_num6", sums)
                before(dve_s, f"feat_im{TILES - 1}", sums)
                before(pool_s, "feat_before1", sums)
                cumulate(0)
                after(act_s, "feat_z2")
                project(1)
                before(act_s, "sum_num7", sums)
                cumulate(1)
                before(dve_s, "sum_yg", sums)
                to_channels(0)
                after(dve_s, f"feat_conv0{TAPS - 1}")
                turn_tiles("feat_values", VALUES, lambda t: conv[:, 0, P * t:P * t + P])
                cumulate(2)
                to_channels(1)
                cumulate(3)
                to_channels(2)
                after(dve_s, "norm_yg")
                before(act_s, "norm_kept", norm)
                do("norm_out", out_products)
                before(dve_s, "sum_ms", sums)
                add_squares(0)
                cumulate(4)
                to_channels(3)
                after(dve_s, "feat_weight")
                before(dve_s, "feat_den", feat)
                do("feat_spread", lambda: pe.matmul(bank[SPREAD][:, :], spread[:, :], pw[:, :], start=True, stop=True))
                cumulate(5)
                to_channels(4)
                add_squares(1)
                after(dve_s, "feat_g")
                after(act_s, "feat_values")
                turn_tiles("feat_g", VALUES, lambda t: poly[:, P * t:P * t + P])
                cumulate(6)
                to_channels(5)
                after(dve_s, f"norm_norm{TILES - 1}")
                turn_tiles("norm_turned", OUT, lambda t: res_n[:, t, :])
                cumulate(7)
                to_channels(6)
                add_squares(2)
                to_channels(7)
                add_squares(3)

            rounds(pe, body)

        @blk.gpsimd
        def _(pool):
            pool.sem_inc(pool_s.sem, ONE)

            def body(r, feat, sums, norm):
                after, before, do = ways(pool, pool_s, r, feat, sums, norm)

                def add_squares(i):
                    after(act_s, f"sum_square{2 * i + 1}")
                    if i >= 2:
                        after(pe_s, f"sum_squares{i - 2}")
                    do(f"sum_added{i}", lambda: pool.tensor_tensor(sq_sum[:, i % 2, :], sq[:, 0, :], sq[:, 1, :], ALU.add))

                def phases(t):
                    after(act_s, "feat_values")
                    if t >= 2:
                        after(dve_s, f"feat_turn{t - 2}")
                    else:
                        before(dve_s, f"feat_turn{t + 2}", feat)
                    do(f"feat_phase{t}", lambda: pool.tensor_tensor(
                        phase[:, t % 2, :].rearrange("p (c m) -> p c m", m=M), theta[:, :, :],
                        values[:, t, :].unsqueeze(2).to_broadcast([P, P, M]), ALU.mult))

                add_squares(0)
                phases(0)
                phases(1)
                add_squares(1)
                phases(2)
                add_squares(2)
                phases(3)
                add_squares(3)
                for i in range(2):
                    after(dve_s, f"feat_im{i + 1}")
                    first = tiles_before[:, 0, :] if i else moments[:, 0, :]
                    do(f"feat_before{i}", lambda: pool.tensor_tensor(tiles_before[:, i, :], first, moments[:, i + 1, :], ALU.add), True)

            rounds(pool, body)


def attention_layers(nc, a, XT, ident):
    with ExitStack() as ctx:
        def sb(name, shape, dt=F32):
            return ctx.enter_context(nc.sbuf_tensor("b_" + name, shape, dt))

        def event(name, per=1):
            return Event(ctx.enter_context(nc.semaphore("b_" + name)), per)

        proj = [ctx.enter_context(nc.psum_tensor(f"b_proj{i}", [P, 512], F32)) for i in range(2)]
        scores = ctx.enter_context(nc.psum_tensor("b_scores", [P, 2, 512], F32))
        turned = [ctx.enter_context(nc.psum_tensor(f"b_turned{i}", [P, 4, P], F32)) for i in range(2)]
        mix = ctx.enter_context(nc.psum_tensor("b_mix", [P, 2, 512], F32))

        wqk = sb("wqk", [P, 2 * INNER])
        w_hi, w_lo = sb("w_hi", [P, 2 * INNER], F32R), sb("w_lo", [P, 2 * INNER], F32R)
        wvT, wo = sb("wvT", [DH, HEADS, D]), sb("wo", [DH, HEADS, D])
        wvo = sb("wvo", [P, HEADS, D])
        w1_wide = 2 * HID + P - CHUNKS[-1][1]
        w1_hi, w1_lo = sb("w1_hi", [P, w1_wide], F32R), sb("w1_lo", [P, w1_wide], F32R)
        w2 = sb("w2", [P, len(CHUNKS), D])
        vectors, vec = sb("vectors", [P, DEPTH, 9]), sb("vec", [P, 9])
        B1, B1_GATE, LN_G, LN_B, B2 = 0, 3, 6, 7, 8
        rope, qk_scale = sb("rope", [P, TILES, 2, 2, DH]), sb("qk_scale", [P, 2, 2, DH])
        table = sb("table", [P, TILES, 2, 2, DH])
        mask = sb("mask", [P, 2, 512], BF16)
        ident16 = sb("ident16", [P, P], BF16)
        xs = sb("xs", [P, 2, WIN + P])
        doubled = sb("doubled", [P, 2, TILES, 2, 2 * WIN])
        x_hi, x_lo = sb("x_hi", [P, 2, P], F32R), sb("x_lo", [P, 2, P], F32R)
        keys = sb("keys", [P, TILES, TILES, D])
        raw, sq = sb("raw", [P, 4, 512]), sb("sq", [P, 4, 512])
        qk, other = sb("qk", [P, 2, 4, 512]), sb("other", [P, 4, 512])
        ss, inv, half = sb("ss", [P, 32]), sb("inv", [P, 2, 32]), sb("half", [P, 32])
        qT, kT = sb("qT", [P, PAIRS, P]), sb("kT", [P, 2, PAIRS, 2, WIN + P])
        top, total = sb("top", [P, HEADS]), sb("total", [P, HEADS])
        prob, probT = sb("prob", [P, HEADS, 2 * WIN]), sb("probT", [P, PAIRS, P])
        y = sb("y", [P, PAIRS, 2, P])
        xn_hi, xn_lo = sb("xn_hi", [P, L], F32R), sb("xn_lo", [P, L], F32R)
        hid = sb("hid", [P, 3, L])
        mask32 = hid[:, 0:2, :]
        xf, xn, xnT = hid[:, 0, :], hid[:, 1, :].rearrange("p (t d) -> p t d", d=D), hid[:, 2, :]
        stats, mv = sb("stats", [P, TILES, 6]), sb("mv", [P, TILES, 2])
        pool_pause = sb("pool_pause", [P, 1])
        var, dev, dev_half, pause = sb("var", [P, TILES]), sb("dev", [P, TILES]), sb("dev_half", [P, TILES]), sb("pause", [P, 1])

        fixed_loaded, qkv_loaded, scale_loaded = event("fixed_loaded"), event("qkv_loaded"), event("scale_loaded")
        wvo_loaded, w1_loaded, w2_loaded = event("wvo_loaded"), event("w1_loaded"), event("w2_loaded")
        fixed_made, tables_made, vec_made = event("fixed_made", 3), event("tables_made"), event("vec_made")
        weights_split = event("weights_split", 8)
        wvo_made, wvo_placed = event("wvo_made", 4), event("wvo_placed", 4)
        staged = event("staged", 2)
        low_staged = event("low_staged")
        tokens_doubled = event("tokens_doubled")
        qk_projected = event("qk_projected", 4)
        copied, squared = event("copied", 4), event("squared", 4)
        rotated = event("rotated", 4)
        squares_summed = event("squares_summed", 4)
        norm_step = event("norm_step", RSQRT + 1)
        rope_summed, normed = event("rope_summed", 4), event("normed", 4)
        qk_turned, qk_placed = event("qk_turned", 4), event("qk_placed", 4)
        carried = event("carried")
        scored = event("scored", 2)
        top_found, subtracted = event("top_found", 2), event("subtracted", 2)
        exped = event("exped", 2)
        totalled, inverted, weighed = event("totalled", 2), event("inverted"), event("weighed", 2)
        p_turned, p_placed = event("p_turned", 2), event("p_placed", 2)
        keys_turned, keys_placed = event("keys_turned"), event("keys_placed")
        mixed, placed = event("mixed", 4), event("placed", 4)
        attn_projected, attn_added = event("attn_projected"), event("attn_added")
        f_staged, f_turned, f_copied = event("f_staged"), event("f_turned"), event("f_copied")
        f_norm_step, f_normed = event("f_norm_step", 3 + RSQRT), event("f_normed")
        f_back, f_scaled = event("f_back"), event("f_scaled", 2)
        f_low = event("f_low")
        w1_split = event("w1_split", 2)
        f_gate, f_value = event("f_gate", 3), event("f_value", 3)
        gated, hidden = event("gated", 3), event("hidden", 3)
        f_out, f_added = event("f_out"), event("f_added")

        flat = lambda x: x[:, :, :].rearrange("p c t -> p (c t)")
        gate_in = [flat(turned[0]), proj[1][:, :], scores[:, 0, :]]
        value_in = [flat(turned[1]), proj[0][:, :], scores[:, 1, :]]

        def wait(engine, ev, rounds, part=None):
            engine.wait_ge(ev.sem, ev.value(rounds, part))

        def lags(t, prev, new):
            return new, (new or t < 1) and (prev or t >= 1), (new or t < 2) and (prev or t >= 2)

        def rounds(engine, body):
            body(0, 0, 0, None, True, True)
            if DEPTH_RUN > 1:
                with engine.Fori(0, DEPTH_RUN - 1) as layer:
                    with engine.Fori(1, B) as s:
                        body(layer, layer * B + s, s, s - 1, False, True)
                    body(layer + 1, layer * B + B, 0, B - 1, True, True)
            with engine.Fori(1, B) as s:
                body(DEPTH_RUN - 1, (DEPTH_RUN - 1) * B + s, s, s - 1, False, True)
            body(DEPTH_RUN - 1, DEPTH_RUN * B, None, B - 1, False, False)

        def at_slot(x, s):
            return XT[x, s, :] if isinstance(s, int) else XT[x, bass.ds(s, 1), :].rearrange("p o t -> p (o t)")

        b1 = a["b1"]
        fixed = [(rope[:, :, :, :, :].rearrange("p t q c d -> p (t q c d)"), a["rope"]),
                 (mask32[:, :, :].rearrange("p n c -> p (n c)"), a["mask"]),
                 (vectors[:, :, LN_G], a["ln_g"]), (vectors[:, :, LN_B], a["ln_b"]), (vectors[:, :, B2], a["b2"])]
        for c, (c0, rows) in enumerate(CHUNKS):
            for col, at in ((B1, c0), (B1_GATE, HID + c0)):
                fixed.append((vectors[0:rows, :, col + c], b1[:, at:at + rows].rearrange("l p -> p l")))

        blk = ctx.enter_context(nc.Block())

        @blk.sync
        def _(sp):
            wait(sp, fixed_made, 0, 0)
            with nc.allow_non_contiguous_dma(reason="small per-channel vectors"):
                for dst, src in fixed:
                    sp.dma_start(dst, src).then_inc(fixed_loaded.sem, 16)
            with sp.Fori(0, DEPTH_RUN) as layer:
                one = lambda x: x[bass.ds(layer, 1)]
                wait(sp, w1_split, layer - 1)
                sp.dma_start(wqk[:, :], a["Wqkv"][bass.ds(layer, 1), :, 0:2 * INNER].rearrange("o p n -> p (o n)")).then_inc(qkv_loaded.sem, 16)
                wait(sp, tables_made, layer - 1)
                sp.dma_start(qk_scale[:, :, :, :].rearrange("p q c d -> p (q c d)"),
                             one(a["qk_scale"]).rearrange("o p n -> p (o n)")).then_inc(scale_loaded.sem, 16)
                wait(sp, wvo_made, layer - 1)
                sp.dma_start(wvT[:, :, :], one(a["WvT"]).rearrange("o p h n -> p (o h) n")).then_inc(wvo_loaded.sem, 16)
                sp.dma_start(wo[:, :, :], one(a["Wo"]).rearrange("o (h p) n -> p (o h) n", p=DH)).then_inc(wvo_loaded.sem, 16)
                wait(sp, weights_split, layer)
                sp.dma_start(wqk[:, 0:2 * HID], one(a["W1"]).rearrange("o p n -> p (o n)")).then_inc(w1_loaded.sem, 16)
                wait(sp, f_out, layer * B - 1)
                sp.dma_start(w2[:, 0:2, :], a["W2"][bass.ds(layer, 1), 0:2 * P].rearrange("o (c p) n -> p (o c) n", p=P)).then_inc(w2_loaded.sem, 16)
                sp.dma_start(w2[0:CHUNKS[2][1], 2, :], a["W2"][bass.ds(layer, 1), 2 * P:HID].rearrange("o p n -> p (o n)")).then_inc(w2_loaded.sem, 16)

        @blk.vector
        def _(dve):
            credit = (rotated, squares_summed, norm_step, top_found, subtracted, totalled, inverted, weighed,
                      attn_added, f_staged, f_norm_step, f_normed, hidden, f_added, tables_made, vec_made, fixed_made,
                      weights_split, w1_split, f_low)
            for ev in credit:
                dve.sem_inc(ev.sem, 2 * ev.per)
            for x in (w1_hi, w1_lo):
                dve.memset(x[:, 2 * HID:].bitcast(F32), 0.0)
            dve.memset(vectors[:, :, :], 0.0).then_inc(fixed_made.sem, 1)
            dve.memset(kT[:, 0, :, :, :].rearrange("p c n t -> p (c n t)"), 0.0)
            dve.memset(kT[:, 1, :, :, :].rearrange("p c n t -> p (c n t)"), 0.0).then_inc(fixed_made.sem, 1)
            dve.wait_ge(fixed_loaded.sem, 16 * len(fixed))
            dve.tensor_copy(ident16[:, :], ident[:, :])
            dve.tensor_copy(mask[:, :, :], mask32[:, :, :]).then_inc(fixed_made.sem, 1)

            def make_vec(layer):
                rd = layer * B - 1
                for ev in (hidden, f_scaled, gated, f_added):
                    wait(dve, ev, rd)
                src = vectors[:, layer, :] if isinstance(layer, int) else vectors[:, bass.ds(layer, 1), :].rearrange("p o c -> p (o c)")
                dve.tensor_copy(vec[:, :], src).then_inc(vec_made.sem, 1)
                wait(dve, vec_made, layer)

            def body(layer, it, s, before, first, new):
                prev = before is not None

                if first:
                    dve.wait_ge(qkv_loaded.sem, layer * 16 + 16)
                    wait(dve, qk_projected, it * TILES - 1)
                    for j in range(4):
                        cols = slice(512 * j, 512 * j + 512)
                        dve.tensor_copy(w_hi[:, cols], wqk[:, cols]).then_inc(weights_split.sem, 1)
                        wait(dve, weights_split, layer, 2 * j)
                        dve.tensor_tensor(w_lo[:, cols], wqk[:, cols], w_hi[:, cols].bitcast(F32), ALU.subtract).then_inc(weights_split.sem, 1)
                    dve.wait_ge(scale_loaded.sem, layer * 16 + 16)
                    wait(dve, rotated, it * TILES - 1)
                    for q in range(2):
                        for c in range(2):
                            tb = dve.tensor_tensor(table[:, :, q, c, :], rope[:, :, q, c, :],
                                                   qk_scale[:, q, c, :].unsqueeze(1).to_broadcast([P, TILES, DH]), ALU.mult)
                    tb.then_inc(tables_made.sem, 1)
                    wait(dve, tables_made, layer)
                    if not prev:
                        make_vec(layer)
                for t in range(TILES):
                    cur, l1, l2 = lags(t, prev, new)
                    n = it * TILES + t
                    i = t % 2
                    if (new or t < 3) and (prev or t >= 3):
                        wait(dve, attn_projected, n - 3)
                        at = PAD + P * ((t - 3) % TILES)
                        x = at_slot(slice(0, P), s if t >= 3 else before)[:, at:at + P]
                        dve.tensor_tensor(x, x, mix[:, 0, 0:P], ALU.add).then_inc(attn_added.sem, 1)
                    if prev and t == 2:
                        wait(dve, attn_added, it * TILES - 1)
                        for h in range(2):
                            ch = slice(DH * h, DH * h + DH)
                            cp = dve.tensor_copy(xf[ch, :], at_slot(ch, before)[:, PAD - h:PAD - h + L])
                        cp.then_inc(f_staged.sem, 1)
                    if cur:
                        wait(dve, qk_turned, n - 2)
                        for j in range(4):
                            kind = j // 2
                            wait(dve, copied, n, j)
                            heads = raw[:, j, :].rearrange("p (h c d) -> p h c d", c=2, d=DH // 2)
                            cos = table[:, t, kind, 0, :].rearrange("p (c d) -> p c d", c=2).unsqueeze(1).to_broadcast([P, 8, 2, DH // 2])
                            sin = table[:, t, kind, 1, :].rearrange("p (c d) -> p c d", c=2).unsqueeze(1).to_broadcast([P, 8, 2, DH // 2])
                            dve.tensor_tensor(qk[:, i, j, :].rearrange("p (h c d) -> p h c d", c=2, d=DH // 2), heads, cos, ALU.mult)
                            wait(dve, rope_summed, n - 1, j)
                            dve.tensor_tensor(other[:, j, :].rearrange("p (h c d) -> p h c d", c=2, d=DH // 2),
                                              heads[:, :, ::-1, :], sin, ALU.mult).then_inc(rotated.sem, 1)
                        for j in range(4):
                            wait(dve, squared, n, j)
                            dve.tensor_reduce(ss[:, 8 * j:8 * j + 8], sq[:, j, :].rearrange("p (h d) -> p h d", d=DH),
                                              AX.X, ALU.add).then_inc(squares_summed.sem, 1)
                        wait(dve, squares_summed, n)
                        wait(dve, normed, n - 2)

                    def ticker(ev, rounds):
                        done = [0]

                        def tick(ins=None):
                            if ins is None:
                                wait(dve, ev, rounds, done[0] - 1)
                            else:
                                ins.then_inc(ev.sem, 1)
                                done[0] += 1

                        return tick

                    tick, f_tick = ticker(norm_step, n), ticker(f_norm_step, it - 1)
                    lanes = []
                    if prev and t == 3:
                        wait(dve, f_copied, it - 1)
                        for k in range(TILES):
                            st = dve.bn_stats(stats[:, k, :], xn[:, k, :])
                        f_tick(st)
                        lanes.append((f_tick, var[:, :], dev[:, :], dev_half[:, :]))
                    if cur:
                        tick(dve.tensor_scalar(ss[:, :], ss[:, :], 1e-24, None, ALU.max))
                        lanes.append((tick, ss[:, :], inv[:, i, :], half[:, :]))
                    if prev and t == 3:
                        f_tick()
                        dve.memset(pause[:, :], 0.0)
                        for k in range(TILES):
                            st = dve.bn_aggr(mv[:, k, :], stats[:, k, :])
                        f_tick(st)
                        f_tick()
                        f_tick(dve.tensor_scalar(var[:, :], mv[:, :, 1], LN_EPS, None, ALU.add))
                    for lane in lanes:
                        lane[0]()
                    if lanes:
                        rsqrt(dve, lanes)
                    if prev and t == 3:
                        for k in range(TILES):
                            st = dve.tensor_scalar(xn[:, k, :], xn[:, k, :], mv[:, k, 0:1], dev[:, k:k + 1], ALU.subtract, ALU.mult)
                        st.then_inc(f_normed.sem, 1)

                    def hide(c):
                        rows = CHUNKS[c][1]
                        wait(dve, gated, it - 1, c)
                        wait(dve, f_value, it - 1, c)
                        dve.scalar_tensor_tensor(out=hid[0:rows, c, :], in0=value_in[c][0:rows], scalar=vec[0:rows, B1 + c:B1 + c + 1],
                                                 in1=hid[0:rows, c, :], op0=ALU.add, op1=ALU.mult).then_inc(hidden.sem, 1)

                    if l1:
                        half_heads = lambda x, j: x[:, 8 * j:8 * j + 8]
                        wide = lambda x, j: half_heads(x, j).unsqueeze(2).to_broadcast([P, 8, 2 * WIN])
                        s3 = [scores[:, j, :].rearrange("p (h k) -> p h k", k=2 * WIN) for j in range(2)]
                        for j in range(2):
                            wait(dve, scored, n - 1, j)
                            dve.tensor_reduce(half_heads(top, j), s3[j], AX.X, ALU.max).then_inc(top_found.sem, 1)
                        for j in range(2):
                            wait(dve, top_found, n - 1, j)
                            wait(dve, p_turned, n - 2)
                            dve.tensor_tensor(half_heads(prob, j), s3[j], wide(top, j), ALU.subtract).then_inc(subtracted.sem, 1)
                    if prev and t == 3:
                        wait(dve, f_scaled, it - 1)
                        dve.tensor_tensor(xn_lo[:, :], xnT, xn_hi[:, :].bitcast(F32), ALU.subtract).then_inc(f_low.sem, 1)
                    if l1:
                        for j in range(2):
                            wait(dve, exped, n - 1, j)
                            dve.tensor_reduce(half_heads(total, j), half_heads(prob, j), AX.X, ALU.add).then_inc(totalled.sem, 1)
                        wait(dve, totalled, n - 1)
                        dve.reciprocal(total[:, :], total[:, :]).then_inc(inverted.sem, 1)
                        wait(dve, inverted, n - 1)
                        for j in range(2):
                            dve.tensor_tensor(half_heads(prob, j), half_heads(prob, j), wide(total, j), ALU.mult).then_inc(weighed.sem, 1)
                    if prev and t == 3:
                        for c in range(len(CHUNKS)):
                            hide(c)
                        wait(dve, f_out, it - 1)
                        x = at_slot(slice(0, P), before)[:, PAD:]
                        dve.scalar_tensor_tensor(out=x, in0=mix[:, 1, :], scalar=vec[:, B2:B2 + 1], in1=x,
                                                 op0=ALU.add, op1=ALU.add).then_inc(f_added.sem, 1)
                        if first:
                            make_vec(layer)
                    if first and t == 3:
                        dve.wait_ge(w1_loaded.sem, layer * 16 + 16)
                        dve.tensor_copy(w1_hi[:, 0:2 * HID], wqk[:, 0:2 * HID]).then_inc(w1_split.sem, 1)
                        wait(dve, w1_split, layer, 0)
                        dve.tensor_tensor(w1_lo[:, 0:2 * HID], wqk[:, 0:2 * HID], w1_hi[:, 0:2 * HID].bitcast(F32), ALU.subtract).then_inc(w1_split.sem, 1)

            rounds(dve, body)

        @blk.scalar
        def _(act):
            for ev in (staged, copied, squared, qk_placed, carried, exped, p_placed, keys_placed, placed, wvo_placed, f_copied, f_scaled, gated):
                act.sem_inc(ev.sem, 2 * ev.per)
            wait(act, fixed_made, 0)

            def body(layer, it, s, before, first, new):
                prev = before is not None
                for t in range(TILES):
                    cur, l1, l2 = lags(t, prev, new)
                    n = it * TILES + t
                    i = t % 2
                    def stage(t):
                        n = it * TILES + t
                        wait(act, tokens_doubled, n - 2)
                        wait(act, low_staged, n - 2)
                        wait(act, qk_projected, n - 2)
                        for h in range(2):
                            ch = slice(DH * h, DH * h + DH)
                            at = PAD - WIN + P * t - h
                            cp = act.activation(xs[ch, t % 2, :], at_slot(ch, s)[:, at:at + WIN + P], ACT.Identity)
                        cp.then_inc(staged.sem, 1)
                        wait(act, staged, n, 0)
                        act.activation(x_hi[:, t % 2, :], xs[:, t % 2, WIN:], ACT.Identity).then_inc(staged.sem, 1)

                    def copy(j):
                        wait(act, qk_projected, n, j)
                        wait(act, rotated, n - 1, j)
                        act.activation(raw[:, j, :], proj[j % 2][:, :], ACT.Identity).then_inc(copied.sem, 1)

                    def place_qk(j):
                        o = (t - 1) % 2
                        wait(act, qk_turned, n - 1, j)
                        pairs = slice(4 * (j % 2), 4 * (j % 2) + 4)
                        if j < 2:
                            cp = act.activation(qT[:, pairs, :], turned[j % 2][:, :, :], ACT.Identity)
                        else:
                            for h in range(2):
                                ch = slice(DH * h, DH * h + DH)
                                cp = act.activation(kT[ch, o, pairs, h, WIN:], turned[j % 2][ch, :, :], ACT.Identity)
                        cp.then_inc(qk_placed.sem, 1)

                    def place(j):
                        wait(act, mixed, n - 2, j)
                        w0, h = 2 * (j // 2), j % 2
                        act.activation(y[:, :, h, WIN * w0:WIN * w0 + 2 * WIN].rearrange("p c (w q) -> p w c q", q=WIN),
                                       mix[:, h, :].rearrange("p (w c q) -> p w c q", w=2, q=WIN), ACT.Identity).then_inc(placed.sem, 1)

                    if cur and t == 0:
                        stage(0)
                    if cur:
                        copy(0)
                        copy(1)
                    if l2:
                        for j in range(2):
                            wait(act, p_turned, n - 2, j)
                            act.activation(probT[:, 4 * j:4 * j + 4, :], turned[j][:, :, :], ACT.Identity).then_inc(p_placed.sem, 1)
                    if cur:
                        copy(2)
                        copy(3)
                    def square(j):
                        wait(act, copied, n, j)
                        wait(act, squares_summed, n - 1, j)
                        act.activation(sq[:, j, :], raw[:, j, :], ACT.Square).then_inc(squared.sem, 1)

                    def open_gate(c):
                        rows = CHUNKS[c][1]
                        wait(act, f_gate, it - 1, c)
                        act.activation(hid[0:rows, c, :], gate_in[c][0:rows], ACT.Gelu,
                                       bias=vec[0:rows, B1_GATE + c:B1_GATE + c + 1]).then_inc(gated.sem, 1)

                    if l1:
                        place_qk(0)
                        place_qk(1)
                    if cur:
                        square(0)
                        square(1)
                    if l1:
                        place_qk(2)
                    if cur:
                        square(2)
                        square(3)
                    if l2:
                        place(0)
                        place(1)
                    if l1:
                        place_qk(3)
                        o = (t - 1) % 2
                        wait(act, qk_placed, n - 1)
                        act.activation(kT[:, 1 - o, :, :, 0:WIN].rearrange("p c n t -> p (c n) t"),
                                       kT[:, o, :, :, P:].rearrange("p c n t -> p (c n) t"), ACT.Identity).then_inc(carried.sem, 1)
                    if prev and t == 2:
                        wait(act, f_turned, it - 1)
                        act.activation(xn[:, :, :].rearrange("p t d -> p (t d)"), proj[1][:, :], ACT.Identity).then_inc(f_copied.sem, 1)
                    if cur:
                        wait(act, keys_turned, n)
                        act.activation(keys[:, t, :, :].rearrange("p w d -> p (w d)"), proj[0][:, :], ACT.Identity).then_inc(keys_placed.sem, 1)
                    if l2:
                        place(2)
                        place(3)
                    if cur and t < TILES - 1:
                        stage(t + 1)
                    if prev and t == 3:
                        wait(act, f_back, it - 1)
                        for x in (xn_hi[:, :], xnT):
                            act.activation(x, proj[1][:, :], ACT.Identity, scale=vec[:, LN_G:LN_G + 1],
                                           bias=vec[:, LN_B:LN_B + 1]).then_inc(f_scaled.sem, 1)
                    if l1:
                        for j in range(2):
                            wait(act, subtracted, n - 1, j)
                            act.activation(prob[:, 8 * j:8 * j + 8, :], prob[:, 8 * j:8 * j + 8, :], ACT.Exp).then_inc(exped.sem, 1)
                    if prev and t == 3:
                        for c in range(len(CHUNKS)):
                            open_gate(c)
                    if first and t == 1:
                        for j in range(4):
                            wait(act, wvo_made, layer, j)
                            act.activation(wvo[:, 4 * j:4 * j + 4, :], turned[j % 2][:, :, :], ACT.Identity).then_inc(wvo_placed.sem, 1)

            rounds(act, body)

        @blk.gpsimd
        def _(pool):
            for ev in (low_staged, tokens_doubled, rope_summed, normed):
                pool.sem_inc(ev.sem, 2 * ev.per)

            def body(layer, it, s, before, first, new):
                def stage_low(t):
                    n, i = it * TILES + t, t % 2
                    wait(pool, staged, n)
                    wait(pool, qk_projected, n - 2)
                    pool.tensor_tensor(x_lo[:, i, :], xs[:, i, WIN:], x_hi[:, i, :].bitcast(F32), ALU.subtract).then_inc(low_staged.sem, 1)

                for t in range(TILES if new else 0):
                    n = it * TILES + t
                    i = t % 2
                    if t == 0:
                        stage_low(0)
                    wait(pool, keys_turned, n - 2)
                    pool.tensor_tensor(pool_pause[:, :], ident[:, 0:1], ident[:, 0:1], ALU.add)
                    for w in range(TILES):
                        tokens = xs[:, i, WIN * w:WIN * w + 2 * WIN].unsqueeze(1).to_broadcast([P, 2, 2 * WIN])
                        cp = pool.tensor_copy(doubled[:, i, w, :, :], tokens)
                    cp.then_inc(tokens_doubled.sem, 1)
                    for j in range(4):
                        wait(pool, rotated, n, j)
                        pool.tensor_tensor(qk[:, i, j, :], qk[:, i, j, :], other[:, j, :], ALU.add).then_inc(rope_summed.sem, 1)
                    if t < TILES - 1:
                        stage_low(t + 1)
                    wait(pool, norm_step, n)
                    for j in range(4):
                        wait(pool, rope_summed, n, j)
                        x = qk[:, i, j, :].rearrange("p (h d) -> p h d", d=DH)
                        pool.tensor_tensor(x, x, inv[:, i, 8 * j:8 * j + 8].unsqueeze(2).to_broadcast([P, 8, DH]),
                                           ALU.mult).then_inc(normed.sem, 1)

            rounds(pool, body)

        @blk.tensor
        def _(pe):
            for ev in (qk_projected, qk_turned, scored, p_turned, keys_turned, mixed, attn_projected, wvo_made,
                       f_turned, f_back, f_gate, f_value, f_out):
                pe.sem_inc(ev.sem, 2 * ev.per)
            wait(pe, fixed_made, 0)

            def body(layer, it, s, before, first, new):
                prev = before is not None
                for t in range(TILES):
                    cur, l1, l2 = lags(t, prev, new)
                    n = it * TILES + t
                    i = t % 2
                    def project(j):
                        cols = slice(512 * j, 512 * j + 512)
                        if first and t == 0:
                            wait(pe, weights_split, layer, 2 * j + 1)
                        if j >= 2:
                            wait(pe, copied, n, j - 2)
                        elif j == 1:
                            wait(pe, copied, n - 1, 3)
                            if prev and t == 0:
                                wait(pe, gated, it - 2, 1)
                            if prev and t == 3:
                                wait(pe, f_copied, it - 1)
                        else:
                            wait(pe, keys_placed, n - 1)
                            if prev and t == 0:
                                wait(pe, hidden, it - 2, 1)
                        pe.matmul(proj[j % 2][:, :], x_hi[:, i, :], w_hi[:, cols], start=True, stop=False)
                        pe.matmul(proj[j % 2][:, :], x_hi[:, i, :], w_lo[:, cols], start=False, stop=False)
                        pe.matmul(proj[j % 2][:, :], x_lo[:, i, :], w_hi[:, cols], start=False, stop=True).then_inc(qk_projected.sem, 1)

                    def turn_qk(j):
                        wait(pe, normed, n - 1, j)
                        if j >= 2:
                            wait(pe, qk_placed, n - 1, j - 2)
                        elif l2:
                            wait(pe, p_placed, n - 2, j)
                        for c in range(4):
                            mm = pe.transpose(turned[j % 2][:, c, :], qk[:, (t - 1) % 2, j, P * c:P * c + P], ident[:, :])
                        mm.then_inc(qk_turned.sem, 1)

                    def mix_windows(w0):
                        for w in (w0, w0 + 1):
                            for h in range(2):
                                half = slice(DH * h, DH * h + DH)
                                if w0 and w == w0:
                                    wait(pe, placed, n - 2, h)
                                mm = pe.matmul(mix[:, h, 256 * (w - w0):256 * (w - w0) + 256].rearrange("p (c q) -> p c q", q=WIN),
                                               keys[half, (t - 2) % TILES, w, :], probT[half, :, WIN * w:WIN * w + WIN],
                                               start=True, stop=True)
                                if w > w0:
                                    mm.then_inc(mixed.sem, 1)

                    def score(j):
                        if j == 0:
                            wait(pe, carried, n - 2)
                        wait(pe, qk_placed, n - 1, 2 + j)
                        wait(pe, subtracted, n - 2, j)
                        if prev and t == 0:
                            wait(pe, (gated, hidden)[j], it - 2, 2)
                        pe.matmul(scores[:, j, :], ident16[:, :], mask[:, 0 if t == 1 else 1, :],
                                  start=True, stop=False, skip_group_check=True)
                        for c in range(4):
                            for w in range(TILES):
                                q = slice(WIN * w, WIN * w + WIN)
                                mm = pe.matmul(scores[q, j, P * c:P * c + P].rearrange("p (n k) -> p n k", n=2), qT[:, 4 * j + c, q],
                                               kT[:, (t - 1) % 2, 4 * j + c, :, WIN * w:WIN * w + 2 * WIN],
                                               start=False, stop=True, skip_group_check=True)
                        mm.then_inc(scored.sem, 1)

                    def map_heads(h, pairs=range(PAIRS)):
                        if first and t == 2:
                            wait(pe, wvo_placed, layer)
                        wait(pe, placed, n - 2, 2 + h)
                        for c in pairs:
                            mm = pe.matmul(mix[:, 0, 0:P], wvo[:, 2 * c + h, :], y[:, c, h, :],
                                           start=(h == 0 and c == 0), stop=(h == 1 and c == PAIRS - 1))
                        if h and c == PAIRS - 1:
                            mm.then_inc(attn_projected.sem, 1)

                    def feed():
                        wait(pe, w1_split, layer - 1 if first else layer)
                        wait(pe, f_scaled, it - 1, 0)
                        wait(pe, qk_placed, n - 1 if l1 else it * TILES - 1)
                        for c, (c0, _) in enumerate(CHUNKS):
                            if c == 1:
                                wait(pe, f_scaled, it - 1)
                                if new:
                                    wait(pe, keys_placed, n)
                            if c == 2:
                                wait(pe, subtracted, n - 1 if l1 else it * TILES - 1)
                            for out, at in ((gate_in[c], HID + c0), (value_in[c], c0)):
                                pe.matmul(out, w1_hi[:, at:at + P], xn_hi[:, :], start=True, stop=False)
                                pe.matmul(out, w1_lo[:, at:at + P], xn_hi[:, :], start=False, stop=False)
                            if c == 1:
                                wait(pe, f_low, it - 1)
                            for low in ((), (0, 1), (2,))[c]:
                                b0 = CHUNKS[low][0]
                                pe.matmul(gate_in[low], w1_hi[:, HID + b0:HID + b0 + P], xn_lo[:, :], start=False, stop=True).then_inc(f_gate.sem, 1)
                                pe.matmul(value_in[low], w1_hi[:, b0:b0 + P], xn_lo[:, :], start=False, stop=True).then_inc(f_value.sem, 1)

                    if cur:
                        wait(pe, low_staged, n)
                        project(0)
                        project(1)
                    if l2:
                        for j in range(2):
                            wait(pe, weighed, n - 2, j)
                            wait(pe, qk_placed, n - 2, 2 + j)
                            if prev and t == 0:
                                wait(pe, (gated, hidden)[j], it - 2, 0)
                            if first and t == 2:
                                wait(pe, wvo_placed, layer, 2 + j)
                            for c in range(4):
                                pr = prob[:, 8 * j + 2 * c:8 * j + 2 * c + 2, :].rearrange("p h k -> p (h k)")
                                mm = pe.transpose(turned[j][:, c, :], pr, ident[:, :])
                            mm.then_inc(p_turned.sem, 1)
                    if cur:
                        project(2)
                        project(3)
                    if l1:
                        turn_qk(0)
                        turn_qk(1)
                    if prev and t == 2:
                        wait(pe, f_staged, it - 1)
                        if new:
                            wait(pe, copied, n, 3)
                        for k in range(TILES):
                            mm = pe.transpose(proj[1][:, P * k:P * k + P], xf[:, P * k:P * k + P], ident[:, :])
                        mm.then_inc(f_turned.sem, 1)
                    if cur:
                        wait(pe, tokens_doubled, n)
                        wait(pe, copied, n, 2)
                        for w in range(TILES):
                            mm = pe.transpose(proj[0][:, P * w:P * w + P], doubled[:, i, w, :, :].rearrange("p r k -> p (r k)"), ident[:, :])
                        mm.then_inc(keys_turned.sem, 1)
                    if l1:
                        turn_qk(2)
                        turn_qk(3)
                    if l2:
                        wait(pe, p_placed, n - 2)
                        wait(pe, keys_placed, n - 2)
                        wait(pe, attn_added, n - 3)
                        if prev and t == 0:
                            wait(pe, f_added, it - 2)
                        mix_windows(0)
                    if l1:
                        score(0)
                    if l2:
                        mix_windows(2)
                    if l1:
                        score(1)
                    if l2:
                        map_heads(0)
                        map_heads(1, range(PAIRS // 2))
                    if prev and t == 3:
                        wait(pe, f_normed, it - 1)
                        if new:
                            wait(pe, copied, n, 3)
                        for k in range(TILES):
                            mm = pe.transpose(proj[1][:, P * k:P * k + P], xn[:, k, :], ident[:, :])
                        mm.then_inc(f_back.sem, 1)
                    if l2:
                        map_heads(1, range(PAIRS // 2, PAIRS))
                    if prev and t == 3:
                        feed()
                        wait(pe, placed, n - 2 if l2 else it * TILES - 1)
                        pe.wait_ge(w2_loaded.sem, (layer - 1 if first else layer) * 32 + 32)
                        for c, (c0, rows) in enumerate(CHUNKS):
                            wait(pe, hidden, it - 1, c)
                            mm = pe.matmul(mix[:, 1, :], w2[0:rows, c, :], hid[0:rows, c, :], start=(c == 0), stop=(c == 2))
                        mm.then_inc(f_out.sem, 1)
                    if first and t == 1:
                        pe.wait_ge(wvo_loaded.sem, layer * 32 + 32)
                        for j in range(4):
                            if j >= 2:
                                wait(pe, wvo_placed, layer, j - 2)
                            else:
                                wait(pe, qk_placed, n - 1, 2 + j)
                            for c in range(4):
                                mm = pe.matmul(turned[j % 2][:, c, :], wvT[:, 4 * j + c, :], wo[:, 4 * j + c, :], start=True, stop=True)
                            mm.then_inc(wvo_made.sem, 1)

            rounds(pe, body)


def final_norm(nc, a, XT, X1T, ident, out):
    with ExitStack() as ctx:
        def sb(name, shape, dt=F32):
            return ctx.enter_context(nc.sbuf_tensor("c_" + name, shape, dt))

        def sem(name):
            return ctx.enter_context(nc.semaphore("c_" + name))

        bank = [ctx.enter_context(nc.psum_tensor(f"c_bank{i}", [P, TILES, D], F32)) for i in range(2)]
        total, tok = sb("total", [P, 2, L]), sb("tok", [P, 2, TILES, D])
        stats, mv = sb("stats", [P, TILES, 6]), sb("mv", [P, TILES, 2])
        dev, eps, pause = sb("dev", [P, TILES]), sb("eps", [P, 1]), sb("pause", [P, 1])
        added, turned, deviation = sem("added"), sem("turned"), sem("deviation")
        stored = [sem("stored_even"), sem("stored_odd")]
        steps = Steps(sem("vector_step"), [f"{n}{q}" for q in range(2) for n in (
            [f"stats{t}" for t in range(TILES)] + [f"mean{t}" for t in range(TILES)] + ["inv dev"]
            + [f"norm{t}" for t in range(TILES)])])
        blk = ctx.enter_context(nc.Block())

        @blk.vector
        def _(dve):
            dve.sem_inc(steps.sem, ONE + len(steps.names))
            dve.memset(eps[:, :], LN_EPS)
            with dve.Fori(0, B // 2) as s2:
                def step(instruction, name, wait=True):
                    steps.did(instruction, name)
                    if wait:
                        dve.wait_ge(steps.sem, steps.count(s2 + 1, name))

                for q in range(2):
                    s = s2 * 2 + q
                    dve.wait_ge(turned, s + 3)
                    for t in range(TILES):
                        step(dve.bn_stats(stats[:, t, :], bank[q][:, t, :]), f"stats{t}{q}", t == TILES - 1)
                    dve.memset(pause[:, :], 0.0)
                    for t in range(TILES):
                        step(dve.bn_aggr(mv[:, t, :], stats[:, t, :]), f"mean{t}{q}", False)
                    dve.wait_ge(deviation, s + 1)
                    step(dve.reciprocal(dev[:, :], dev[:, :]), f"inv dev{q}")
                    dve.wait_ge(stored[q], s2 * 16 + 1)
                    for t in range(TILES):
                        step(dve.tensor_scalar(tok[:, q, t, :], bank[q][:, t, :], mv[:, t, 0:1], dev[:, t:t + 1],
                                               ALU.subtract, ALU.mult), f"norm{t}{q}", False)

        @blk.gpsimd
        def _(pool):
            pool.sem_inc(turned, 2)
            with pool.Fori(0, B // 2) as s2:
                for q in range(2):
                    s = s2 * 2 + q
                    pool.wait_ge(turned, s + 1)
                    pool.tensor_tensor(total[:, q, :], XT[:, bass.ds(s, 1), PAD:].rearrange("p o t -> p (o t)"),
                                       X1T[:, bass.ds(s, 1), :].rearrange("p o t -> p (o t)"), ALU.add).then_inc(added, 1)

        @blk.scalar
        def _(act):
            with act.Fori(0, B // 2) as s2:
                for q in range(2):
                    act.wait_ge(steps.sem, steps.count(s2 + 1, f"mean{TILES - 1}{q}"))
                    act.activation(dev[:, :], mv[:, :, 1], ACT.Sqrt, bias=eps[:, 0:1]).then_inc(deviation, 1)

        @blk.tensor
        def _(pe):
            with pe.Fori(0, B // 2) as s2:
                for q in range(2):
                    s = s2 * 2 + q
                    pe.wait_ge(added, s + 1)
                    pe.wait_ge(steps.sem, steps.count(s2, f"norm{TILES - 1}{q}"))
                    for t in range(TILES):
                        mm = pe.transpose(bank[q][:, t, :], total[:, q, P * t:P * t + P], ident[:, :])
                    mm.then_inc(turned, 1)

        @blk.sync
        def _(sp):
            sp.sem_inc(stored[0], ONE)
            sp.sem_inc(stored[1], ONE)
            with sp.Fori(0, B // 2) as s2:
                for q in range(2):
                    s = s2 * 2 + q
                    sp.wait_ge(steps.sem, steps.count(s2 + 1, f"norm{TILES - 1}{q}"))
                    sp.dma_start(out[bass.ds(s, 1)].rearrange("o (t p) d -> p (o t) d", p=P), tok[:, q, :, :]).then_inc(stored[q], 16)
            for q in range(2):
                sp.wait_ge(stored[q], ONE + 16 * B // 2)


def build(nc, a, out, layers=True):
    with ExitStack() as ctx:
        XT = ctx.enter_context(nc.sbuf_tensor("XT", [P, B, SPAN], F32))
        X1T = ctx.enter_context(nc.sbuf_tensor("X1T", [P, B, L], F32))
        ident = ctx.enter_context(nc.sbuf_tensor("ident", [P, P], F32))
        state_space_layer(nc, a, XT, X1T, ident)
        if layers:
            attention_layers(nc, a, XT, ident)
        final_norm(nc, a, XT, X1T, ident, out)


def lay_out(x):
    f = lambda v: np.ascontiguousarray(v)
    g = {n: np.asarray(v) for n, v in x.items()}
    rows = lambda v: f(np.broadcast_to(v.reshape(1, -1), (P, v.size)))
    qk = np.stack([g["L0_ffn_q_scale"], g["L0_ffn_k_scale"]], 1)
    back = np.concatenate([qk[..., DH // 2:], qk[..., :DH // 2]], -1)
    qk = np.stack([qk, back], 2)
    W2 = g["L0_ffn_W2"]
    d = dict(
        x=g["L0_attn_x"], xT=f(g["L0_attn_x"].transpose(2, 0, 1)), W_in=g["L0_attn_W_in"],
        W_out=g["L0_attn_W_out"], w_conv=f(g["L0_attn_w_conv"][:, 0, :].T), b_conv=g["L0_attn_b_conv"],
        theta=rows(g["L0_attn_theta"]), logits=rows(g["L0_attn_deriv_logits"]),
        slopes=np.concatenate([g["L0_attn_decay_slopes"], g["L0_attn_anchor_slopes"]]),
        score_scale=g["L0_attn_score_scale"], W_re=g["L0_attn_W_re"], W_im=g["L0_attn_W_im"],
        norm_scale=g["L0_attn_norm_scale"],
        Wqkv=g["L0_ffn_Wqkv"],
        WvT=f(g["L0_ffn_Wqkv"][:, :, 2 * INNER:].reshape(DEPTH, D, HEADS, DH).transpose(0, 3, 2, 1)), qk_scale=f(np.broadcast_to(qk.reshape(DEPTH, 1, -1), (DEPTH, P, qk[0].size))),
        Wo=g["L0_ffn_Wo"], ln_g=f(g["L0_ffn_ln_g"].T), ln_b=f(g["L0_ffn_ln_b"].T),
        W1=g["L0_ffn_W1"], b1=g["L0_ffn_b1"], W2=W2, b2=f(g["L0_ffn_b2"].T))
    d.update(constants())
    return d


def kernel(**inputs):
    import concourse.bacc as _bacc
    from concourse.bass_utils import run_bass_kernel_spmd as _run

    nc = _bacc.Bacc("TRN2", target_bir_lowering=False, num_devices=1)
    arrays = {f"in_{n}_dram": v for n, v in lay_out(inputs).items()}
    a = {n[3:-5]: nc.dram_tensor(n, v.shape, mybir.dt.from_np(v.dtype), kind="ExternalInput").ap()
         for n, v in arrays.items()}
    out = nc.dram_tensor("out_dram", (B, L, D), F32, kind="ExternalOutput").ap()
    build(nc, a, out)
    r = _run(nc, [arrays], core_ids=[0])
    return r.results[0]["out_dram"]
```
